# Optimizing a Trainium2 kernel written in Bass

```python
import numpy as np
import jax
import jax.numpy as jnp

def _softmax(x, axis=-1):
    return jax.nn.softmax(x, axis=axis)

def _gelu(x):
    return jax.nn.gelu(x, approximate=True)

def _silu(x):
    return jax.nn.silu(x)

def _sigmoid(x):
    return jax.nn.sigmoid(x)

def _layernorm(x, axis=-1, eps=1e-05):
    m = jnp.mean(x, axis=axis, keepdims=True)
    v = jnp.var(x, axis=axis, keepdims=True)
    return (x - m) / jnp.sqrt(v + eps)

def _scatter_add(tgt, idx, src, axis=0):
    return tgt.at[idx].add(src)

def _segment_sum(src, seg, n):
    return jax.ops.segment_sum(src, seg, n)
kernel_name = 'mk_vit_tower_cls_d2_tok_img1024_r4_a6e81d'

def setup_inputs(seed: int=0):
    np.random.seed(seed)
    _w = jnp.asarray

    def _rec_inputs():
        import jax
        import jax.numpy as jnp
        _rk = jax.random.key(seed)
        x = -0.000169711 + 1.00022 * jax.random.normal(jax.random.fold_in(_rk, 1), (64, 3, 84, 84), jnp.float32)
        cls_tok = 0.02 * jax.random.normal(jax.random.fold_in(_rk, 5), (1, 1, 256), jnp.float32)
        return (x, cls_tok)
    x, cls_tok = _rec_inputs()

    def _L0_tok_setup():
        import jax, jax.numpy as jnp
        import numpy as np
        C = 256
        H8 = 8
        DH = C // H8
        PS = 14
        CS = 3
        IMG = 168
        B = 4

        def _ln(x, g, b):
            mu = jnp.mean(x, axis=-1, keepdims=True)
            xc = x - mu
            var = jnp.mean(xc * xc, axis=-1, keepdims=True)
            return xc * jax.lax.rsqrt(var + 1e-05) * g + b

        def _forward(pixel_values, conv_w, class_emb, la_ln_q_g, la_ln_q_b, la_wq, la_ln_kv_g, la_ln_kv_b, la_wkv, la_proj_w, la_proj_b, ga_ln_q_g, ga_ln_q_b, ga_wq, ga_ln_kv_g, ga_ln_kv_b, ga_wkv, ga_proj_w, ga_proj_b, mod_w, mod_b):
            b = pixel_values.shape[0]
            pe = jax.lax.conv_general_dilated(pixel_values, conv_w, (PS, PS), 'VALID', dimension_numbers=('NCHW', 'OIHW', 'NCHW'))
            HP = pe.shape[2]
            h = HP // CS
            hw, N = (h * h, CS * CS)
            scale = C ** (-0.5)
            grid = pe.reshape(b, C, h, CS, h, CS)
            red = grid.mean(axis=(3, 5)).reshape(b, C, hw).transpose(0, 2, 1)
            win = grid.transpose(0, 2, 4, 3, 5, 1).reshape(b, hw, N, C)
            q = _ln(red, la_ln_q_g, la_ln_q_b) @ la_wq
            q = q.reshape(b, hw, H8, DH).transpose(0, 2, 1, 3)
            kv = _ln(win, la_ln_kv_g, la_ln_kv_b) @ la_wkv
            kv = kv.reshape(b, hw, N, 2, H8, DH).transpose(3, 0, 4, 1, 2, 5)
            k_, v_ = (kv[0], kv[1])
            attn = jax.nn.softmax(jnp.einsum('bhnd,bhnkd->bhnk', q * scale, k_), axis=-1)
            agg = jnp.einsum('bhnk,bhnkd->bhnd', attn, v_)
            agg = agg.transpose(0, 2, 1, 3).reshape(b, hw, C)
            local_out = red + agg @ la_proj_w + la_proj_b
            cls = jnp.broadcast_to(class_emb, (b, 1, C))
            gq = (_ln(cls, ga_ln_q_g, ga_ln_q_b) @ ga_wq).reshape(b, H8, DH)
            gkv = _ln(local_out, ga_ln_kv_g, ga_ln_kv_b) @ ga_wkv
            gkv = gkv.reshape(b, hw, 2, H8, DH).transpose(2, 0, 3, 1, 4)
            gk, gv = (gkv[0], gkv[1])
            gattn = jax.nn.softmax(jnp.einsum('bhd,bhnd->bhn', gq * scale, gk), axis=-1)
            gagg = jnp.einsum('bhn,bhnd->bhd', gattn, gv).reshape(b, 1, C)
            cls_out = cls + gagg @ ga_proj_w + ga_proj_b
            patch_out = local_out @ mod_w + mod_b
            return jnp.concatenate([patch_out, cls_out], axis=1)
        key = jax.random.key(seed)
        ks = jax.random.split(key, 16)
        nrm = lambda k, shape: jax.random.normal(k, shape, jnp.float32) * 0.02
        return {'pixel_values': jax.random.normal(ks[0], (B, 3, IMG, IMG), jnp.float32), 'pixel_masks': jnp.ones((B, 1, IMG, IMG), jnp.float32), 'conv_w': nrm(ks[1], (C, 3, PS, PS)), 'class_emb': nrm(ks[2], (C,)), 'la_ln_q_g': jnp.ones((C,)), 'la_ln_q_b': jnp.zeros((C,)), 'la_wq': nrm(ks[3], (C, C)), 'la_ln_kv_g': jnp.ones((C,)), 'la_ln_kv_b': jnp.zeros((C,)), 'la_wkv': nrm(ks[4], (C, 2 * C)), 'la_proj_w': nrm(ks[5], (C, C)), 'la_proj_b': jnp.zeros((C,)), 'ga_ln_q_g': jnp.ones((C,)), 'ga_ln_q_b': jnp.zeros((C,)), 'ga_wq': nrm(ks[6], (C, C)), 'ga_ln_kv_g': jnp.ones((C,)), 'ga_ln_kv_b': jnp.zeros((C,)), 'ga_wkv': nrm(ks[7], (C, 2 * C)), 'ga_proj_w': nrm(ks[8], (C, C)), 'ga_proj_b': jnp.zeros((C,)), 'mod_w': nrm(ks[9], (C, C)), 'mod_b': jnp.zeros((C,))}
    _L0_tok_all = _L0_tok_setup()
    _L0_tok_in = {k: v for k, v in _L0_tok_all.items() if k in ('pixel_masks', 'conv_w', 'class_emb', 'la_ln_q_g', 'la_ln_q_b', 'la_wq', 'la_ln_kv_g', 'la_ln_kv_b', 'la_wkv', 'la_proj_w', 'la_proj_b', 'ga_ln_q_g', 'ga_ln_q_b', 'ga_wq', 'ga_ln_kv_g', 'ga_ln_kv_b', 'ga_wkv', 'ga_proj_w', 'ga_proj_b', 'mod_w', 'mod_b')}
    del _L0_tok_all

    def _L0_attn_setup():
        import jax, jax.numpy as jnp
        import numpy as np
        D = 256
        B, T = (4, 512)

        def _scan_combine(c1, c2):
            a1, b1 = c1
            a2, b2 = c2
            return (a2 * a1, a2 * b1 + b2)
        key = jax.random.key(seed)
        ks = jax.random.split(key, 7)
        s = 0.02
        return {'x': jax.random.normal(ks[0], (B, T, D), dtype=jnp.float32), 'W_in': s * jax.random.normal(ks[1], (2 * D, D), dtype=jnp.float32), 'b_in': jnp.zeros((2 * D,), dtype=jnp.float32), 'W_s': s * jax.random.normal(ks[2], (D, D), dtype=jnp.float32), 'b_s': jnp.zeros((D,), dtype=jnp.float32), 'W_o': s * jax.random.normal(ks[3], (D, D), dtype=jnp.float32), 'b_o': jnp.zeros((D,), dtype=jnp.float32)}
    _L0_attn_all = _L0_attn_setup()
    _L0_attn_in = {k: v for k, v in _L0_attn_all.items() if k in ('W_in', 'b_in', 'W_s', 'b_s', 'W_o', 'b_o')}
    del _L0_attn_all

    def _L0_ffn_setup():
        import jax, jax.numpy as jnp
        import numpy as np
        EPS = 1e-05

        @jax.custom_vjp
        def ste_quantize(w):
            scale = jnp.maximum(jnp.mean(jnp.abs(w)), EPS)
            return jnp.clip(jnp.round(w / scale), -1.0, 1.0)

        def _ste_fwd(w):
            return (ste_quantize(w), None)

        def _ste_bwd(_, g):
            return (g,)
        ste_quantize.defvjp(_ste_fwd, _ste_bwd)
        key = jax.random.key(seed)
        k1, k2 = jax.random.split(key)
        x = jax.random.normal(k1, (8, 2048, 256), dtype=jnp.float32)
        weight = jax.random.normal(k2, (256, 256), dtype=jnp.float32) * 0.02
        return {'x': x, 'weight': weight}
    _L0_ffn_all = _L0_ffn_setup()
    _L0_ffn_in = {k: v for k, v in _L0_ffn_all.items() if k in ('weight',)}
    del _L0_ffn_all

    def _L1_attn_setup():
        import jax, jax.numpy as jnp
        import numpy as np
        import math
        N_HEAD = 16
        LATENT_RANK = 64
        key = jax.random.key(seed)
        ks = jax.random.split(key, 8)
        B, T, C, H, R = (4, 512, 256, N_HEAD, LATENT_RANK)
        std = 0.02
        return {'hidden_states': jax.random.normal(ks[0], (B, T, C), jnp.float32), 'basis_w': jax.random.normal(ks[1], (R, C), jnp.float32) * std, 'core': jax.random.normal(ks[2], (R, R), jnp.float32) * std, 'head_residual': jax.random.normal(ks[3], (H, R, R), jnp.float32) * (std / 10.0), 'v_w': jax.random.normal(ks[4], (C, C), jnp.float32) * std, 'v_b': jnp.zeros((C,), jnp.float32), 'o_w': jax.random.normal(ks[5], (C, C), jnp.float32) * std, 'o_b': jnp.zeros((C,), jnp.float32)}
    _L1_attn_all = _L1_attn_setup()
    _L1_attn_in = {k: v for k, v in _L1_attn_all.items() if k in ('basis_w', 'core', 'head_residual', 'v_w', 'v_b', 'o_w', 'o_b')}
    del _L1_attn_all

    def _L1_ffn_setup():
        import jax, jax.numpy as jnp
        import numpy as np
        EMBED_DIM = 256
        MLP_RATIO = 4
        NUM_EXPERTS = 8
        CAPACITY = 1.0
        LN_EPS = 1e-05

        def _layernorm(y, gamma, beta):
            mu = jnp.mean(y, axis=-1, keepdims=True)
            var = jnp.mean(jnp.square(y - mu), axis=-1, keepdims=True)
            return (y - mu) * jax.lax.rsqrt(var + LN_EPS) * gamma + beta
        key = jax.random.key(seed)
        k0, k1, k2, k3, k4, k5 = jax.random.split(key, 6)
        d = EMBED_DIM
        dd = EMBED_DIM * MLP_RATIO
        n = NUM_EXPERTS
        x = jax.random.normal(k0, (4, 512, d), dtype=jnp.float32)
        gate_w = jax.random.normal(k1, (n, d), dtype=jnp.float32) * 0.02
        ln_gamma = jnp.ones((d,), dtype=jnp.float32)
        ln_beta = jnp.zeros((d,), dtype=jnp.float32)
        fc1s = jax.random.normal(k2, (n, dd, d), dtype=jnp.float32) * (1.0 / np.sqrt(d))
        b1s = jax.random.normal(k3, (n, dd), dtype=jnp.float32) * 0.02
        fc2s = jax.random.normal(k4, (n, d, dd), dtype=jnp.float32) * (1.0 / np.sqrt(dd))
        b2s = jax.random.normal(k5, (n, d), dtype=jnp.float32) * 0.02
        return {'x': x, 'gate_w': gate_w, 'ln_gamma': ln_gamma, 'ln_beta': ln_beta, 'fc1s': fc1s, 'b1s': b1s, 'fc2s': fc2s, 'b2s': b2s}
    _L1_ffn_all = _L1_ffn_setup()
    _L1_ffn_in = {k: v for k, v in _L1_ffn_all.items() if k in ('gate_w', 'ln_gamma', 'ln_beta', 'fc1s', 'b1s', 'fc2s', 'b2s')}
    del _L1_ffn_all
    return {'x': x, 'cls_tok': cls_tok, 'L0_tok_pixel_masks': _L0_tok_in['pixel_masks'], 'L0_tok_conv_w': _L0_tok_in['conv_w'], 'L0_tok_class_emb': _L0_tok_in['class_emb'], 'L0_tok_la_ln_q_g': _L0_tok_in['la_ln_q_g'], 'L0_tok_la_ln_q_b': _L0_tok_in['la_ln_q_b'], 'L0_tok_la_wq': _L0_tok_in['la_wq'], 'L0_tok_la_ln_kv_g': _L0_tok_in['la_ln_kv_g'], 'L0_tok_la_ln_kv_b': _L0_tok_in['la_ln_kv_b'], 'L0_tok_la_wkv': _L0_tok_in['la_wkv'], 'L0_tok_la_proj_w': _L0_tok_in['la_proj_w'], 'L0_tok_la_proj_b': _L0_tok_in['la_proj_b'], 'L0_tok_ga_ln_q_g': _L0_tok_in['ga_ln_q_g'], 'L0_tok_ga_ln_q_b': _L0_tok_in['ga_ln_q_b'], 'L0_tok_ga_wq': _L0_tok_in['ga_wq'], 'L0_tok_ga_ln_kv_g': _L0_tok_in['ga_ln_kv_g'], 'L0_tok_ga_ln_kv_b': _L0_tok_in['ga_ln_kv_b'], 'L0_tok_ga_wkv': _L0_tok_in['ga_wkv'], 'L0_tok_ga_proj_w': _L0_tok_in['ga_proj_w'], 'L0_tok_ga_proj_b': _L0_tok_in['ga_proj_b'], 'L0_tok_mod_w': _L0_tok_in['mod_w'], 'L0_tok_mod_b': _L0_tok_in['mod_b'], 'L0_attn_W_in': _L0_attn_in['W_in'], 'L0_attn_b_in': _L0_attn_in['b_in'], 'L0_attn_W_s': _L0_attn_in['W_s'], 'L0_attn_b_s': _L0_attn_in['b_s'], 'L0_attn_W_o': _L0_attn_in['W_o'], 'L0_attn_b_o': _L0_attn_in['b_o'], 'L0_ffn_weight': _L0_ffn_in['weight'], 'L1_attn_basis_w': _L1_attn_in['basis_w'], 'L1_attn_core': _L1_attn_in['core'], 'L1_attn_head_residual': _L1_attn_in['head_residual'], 'L1_attn_v_w': _L1_attn_in['v_w'], 'L1_attn_v_b': _L1_attn_in['v_b'], 'L1_attn_o_w': _L1_attn_in['o_w'], 'L1_attn_o_b': _L1_attn_in['o_b'], 'L1_ffn_gate_w': _L1_ffn_in['gate_w'], 'L1_ffn_ln_gamma': _L1_ffn_in['ln_gamma'], 'L1_ffn_ln_beta': _L1_ffn_in['ln_beta'], 'L1_ffn_fc1s': _L1_ffn_in['fc1s'], 'L1_ffn_b1s': _L1_ffn_in['b1s'], 'L1_ffn_fc2s': _L1_ffn_in['fc2s'], 'L1_ffn_b2s': _L1_ffn_in['b2s']}

def reference(x, cls_tok, L0_tok_pixel_masks, L0_tok_conv_w, L0_tok_class_emb, L0_tok_la_ln_q_g, L0_tok_la_ln_q_b, L0_tok_la_wq, L0_tok_la_ln_kv_g, L0_tok_la_ln_kv_b, L0_tok_la_wkv, L0_tok_la_proj_w, L0_tok_la_proj_b, L0_tok_ga_ln_q_g, L0_tok_ga_ln_q_b, L0_tok_ga_wq, L0_tok_ga_ln_kv_g, L0_tok_ga_ln_kv_b, L0_tok_ga_wkv, L0_tok_ga_proj_w, L0_tok_ga_proj_b, L0_tok_mod_w, L0_tok_mod_b, L0_attn_W_in, L0_attn_b_in, L0_attn_W_s, L0_attn_b_s, L0_attn_W_o, L0_attn_b_o, L0_ffn_weight, L1_attn_basis_w, L1_attn_core, L1_attn_head_residual, L1_attn_v_w, L1_attn_v_b, L1_attn_o_w, L1_attn_o_b, L1_ffn_gate_w, L1_ffn_ln_gamma, L1_ffn_ln_beta, L1_ffn_fc1s, L1_ffn_b1s, L1_ffn_fc2s, L1_ffn_b2s):
    import jax
    import jax.numpy as jnp

    def _L0_tok_ref(pixel_values, pixel_masks, conv_w, class_emb, la_ln_q_g, la_ln_q_b, la_wq, la_ln_kv_g, la_ln_kv_b, la_wkv, la_proj_w, la_proj_b, ga_ln_q_g, ga_ln_q_b, ga_wq, ga_ln_kv_g, ga_ln_kv_b, ga_wkv, ga_proj_w, ga_proj_b, mod_w, mod_b):
        import jax, jax.numpy as jnp
        import numpy as np
        C = 256
        H8 = 8
        DH = C // H8
        PS = 14
        CS = 3
        IMG = 168
        B = 4

        def _ln(x, g, b):
            mu = jnp.mean(x, axis=-1, keepdims=True)
            xc = x - mu
            var = jnp.mean(xc * xc, axis=-1, keepdims=True)
            return xc * jax.lax.rsqrt(var + 1e-05) * g + b

        def _forward(pixel_values, conv_w, class_emb, la_ln_q_g, la_ln_q_b, la_wq, la_ln_kv_g, la_ln_kv_b, la_wkv, la_proj_w, la_proj_b, ga_ln_q_g, ga_ln_q_b, ga_wq, ga_ln_kv_g, ga_ln_kv_b, ga_wkv, ga_proj_w, ga_proj_b, mod_w, mod_b):
            b = pixel_values.shape[0]
            pe = jax.lax.conv_general_dilated(pixel_values, conv_w, (PS, PS), 'VALID', dimension_numbers=('NCHW', 'OIHW', 'NCHW'))
            HP = pe.shape[2]
            h = HP // CS
            hw, N = (h * h, CS * CS)
            scale = C ** (-0.5)
            grid = pe.reshape(b, C, h, CS, h, CS)
            red = grid.mean(axis=(3, 5)).reshape(b, C, hw).transpose(0, 2, 1)
            win = grid.transpose(0, 2, 4, 3, 5, 1).reshape(b, hw, N, C)
            q = _ln(red, la_ln_q_g, la_ln_q_b) @ la_wq
            q = q.reshape(b, hw, H8, DH).transpose(0, 2, 1, 3)
            kv = _ln(win, la_ln_kv_g, la_ln_kv_b) @ la_wkv
            kv = kv.reshape(b, hw, N, 2, H8, DH).transpose(3, 0, 4, 1, 2, 5)
            k_, v_ = (kv[0], kv[1])
            attn = jax.nn.softmax(jnp.einsum('bhnd,bhnkd->bhnk', q * scale, k_), axis=-1)
            agg = jnp.einsum('bhnk,bhnkd->bhnd', attn, v_)
            agg = agg.transpose(0, 2, 1, 3).reshape(b, hw, C)
            local_out = red + agg @ la_proj_w + la_proj_b
            cls = jnp.broadcast_to(class_emb, (b, 1, C))
            gq = (_ln(cls, ga_ln_q_g, ga_ln_q_b) @ ga_wq).reshape(b, H8, DH)
            gkv = _ln(local_out, ga_ln_kv_g, ga_ln_kv_b) @ ga_wkv
            gkv = gkv.reshape(b, hw, 2, H8, DH).transpose(2, 0, 3, 1, 4)
            gk, gv = (gkv[0], gkv[1])
            gattn = jax.nn.softmax(jnp.einsum('bhd,bhnd->bhn', gq * scale, gk), axis=-1)
            gagg = jnp.einsum('bhn,bhnd->bhd', gattn, gv).reshape(b, 1, C)
            cls_out = cls + gagg @ ga_proj_w + ga_proj_b
            patch_out = local_out @ mod_w + mod_b
            return jnp.concatenate([patch_out, cls_out], axis=1)
        del pixel_masks
        return _forward(pixel_values, conv_w, class_emb, la_ln_q_g, la_ln_q_b, la_wq, la_ln_kv_g, la_ln_kv_b, la_wkv, la_proj_w, la_proj_b, ga_ln_q_g, ga_ln_q_b, ga_wq, ga_ln_kv_g, ga_ln_kv_b, ga_wkv, ga_proj_w, ga_proj_b, mod_w, mod_b)

    def _L0_attn_ref(x, W_in, b_in, W_s, b_s, W_o, b_o):
        import jax, jax.numpy as jnp
        import numpy as np
        D = 256
        B, T = (4, 512)

        def _scan_combine(c1, c2):
            a1, b1 = c1
            a2, b2 = c2
            return (a2 * a1, a2 * b1 + b2)
        gv = jnp.einsum('btd,ed->bte', x, W_in) + b_in
        gate = jax.nn.sigmoid(gv[..., :D])
        val = gv[..., D:]
        sv = jnp.tanh(jnp.einsum('btd,ed->bte', val, W_s) + b_s)
        a = 1.0 - gate
        b = gate * sv
        _, h = jax.lax.associative_scan(_scan_combine, (a, b), axis=1)
        out = jnp.einsum('btd,ed->bte', h, W_o) + b_o
        return x + out

    def _L0_ffn_ref(x, weight):
        import jax, jax.numpy as jnp
        import numpy as np
        EPS = 1e-05

        @jax.custom_vjp
        def ste_quantize(w):
            scale = jnp.maximum(jnp.mean(jnp.abs(w)), EPS)
            return jnp.clip(jnp.round(w / scale), -1.0, 1.0)

        def _ste_fwd(w):
            return (ste_quantize(w), None)

        def _ste_bwd(_, g):
            return (g,)
        ste_quantize.defvjp(_ste_fwd, _ste_bwd)
        w_ternary = ste_quantize(weight)
        scale = jnp.maximum(jnp.mean(jnp.abs(weight)), EPS)
        return jnp.einsum('bsi,oi->bso', x, w_ternary * scale)

    def _L1_attn_ref(hidden_states, basis_w, core, head_residual, v_w, v_b, o_w, o_b):
        import jax, jax.numpy as jnp
        import numpy as np
        import math
        N_HEAD = 16
        LATENT_RANK = 64
        B, T, C = hidden_states.shape
        H = N_HEAD
        R = LATENT_RANK
        head_dim = C // H
        latent = jnp.einsum('btc,rc->btr', hidden_states, basis_w)
        core_sym = 0.5 * (core + core.T)
        centered = head_residual - head_residual.mean(axis=0, keepdims=True)
        head_mats = core_sym[None] / float(H) + centered
        lt = jnp.einsum('btr,hrs->bhts', latent, head_mats)
        att = jnp.einsum('bhts,bus->bhtu', lt, latent) * (1.0 / math.sqrt(R))
        causal = jnp.tril(jnp.ones((T, T), jnp.bool_))
        att = jnp.where(causal[None, None], att, jnp.float32(-jnp.inf))
        att = jax.nn.softmax(att, axis=-1)
        v = (hidden_states @ v_w.T + v_b).reshape(B, T, H, head_dim).transpose(0, 2, 1, 3)
        y = att @ v
        y = y.transpose(0, 2, 1, 3).reshape(B, T, C)
        y = y @ o_w.T + o_b
        return y

    def _L1_ffn_ref(x, gate_w, ln_gamma, ln_beta, fc1s, b1s, fc2s, b2s):
        import jax, jax.numpy as jnp
        import numpy as np
        EMBED_DIM = 256
        MLP_RATIO = 4
        NUM_EXPERTS = 8
        CAPACITY = 1.0
        LN_EPS = 1e-05

        def _layernorm(y, gamma, beta):
            mu = jnp.mean(y, axis=-1, keepdims=True)
            var = jnp.mean(jnp.square(y - mu), axis=-1, keepdims=True)
            return (y - mu) * jax.lax.rsqrt(var + LN_EPS) * gamma + beta
        og_shape = x.shape
        d = og_shape[-1]
        xf = x.reshape(-1, d)
        bs = xf.shape[0]
        n = gate_w.shape[0]
        k = int(bs * CAPACITY) // n
        scores = xf @ gate_w.T
        scores = (jnp.tanh(scores) + 1.0) * 0.5
        vals, idx = jax.lax.top_k(scores.T, k)
        kept_w = vals.T
        flat_idx = idx.T.reshape(-1)
        y = xf[flat_idx].reshape(k, n, d)
        y = _layernorm(y, ln_gamma, ln_beta)
        h = jnp.einsum('knd,nfd->knf', y, fc1s) + b1s
        h = jax.nn.gelu(h, approximate=True)
        o = jnp.einsum('knf,ndf->knd', h, fc2s) + b2s
        o = o * kept_w[:, :, None]
        out = xf.at[flat_idx].add(o.reshape(k * n, d))
        return out.reshape(og_shape)
    h = _L0_tok_ref(x, L0_tok_pixel_masks, L0_tok_conv_w, L0_tok_class_emb, L0_tok_la_ln_q_g, L0_tok_la_ln_q_b, L0_tok_la_wq, L0_tok_la_ln_kv_g, L0_tok_la_ln_kv_b, L0_tok_la_wkv, L0_tok_la_proj_w, L0_tok_la_proj_b, L0_tok_ga_ln_q_g, L0_tok_ga_ln_q_b, L0_tok_ga_wq, L0_tok_ga_ln_kv_g, L0_tok_ga_ln_kv_b, L0_tok_ga_wkv, L0_tok_ga_proj_w, L0_tok_ga_proj_b, L0_tok_mod_w, L0_tok_mod_b)
    h = jnp.concatenate([jnp.broadcast_to(cls_tok, (h.shape[0], 1, h.shape[2])), h], axis=1)
    h = h + _L0_attn_ref(_layernorm(h, axis=-1), L0_attn_W_in, L0_attn_b_in, L0_attn_W_s, L0_attn_b_s, L0_attn_W_o, L0_attn_b_o)
    h = h + _L0_ffn_ref(_layernorm(h, axis=-1), L0_ffn_weight)
    h = h + _L1_attn_ref(_layernorm(h, axis=-1), L1_attn_basis_w, L1_attn_core, L1_attn_head_residual, L1_attn_v_w, L1_attn_v_b, L1_attn_o_w, L1_attn_o_b)
    h = h + _L1_ffn_ref(_layernorm(h, axis=-1), L1_ffn_gate_w, L1_ffn_ln_gamma, L1_ffn_ln_beta, L1_ffn_fc1s, L1_ffn_b1s, L1_ffn_fc2s, L1_ffn_b2s)
    return h

_drawn_inputs = setup_inputs


def setup_inputs(seed=0):
    import zlib

    import numpy as np

    out = dict(_drawn_inputs(seed))
    spreads = {'L0_tok_pixel_masks': (1.0, 0.2),
     'L0_tok_la_ln_q_g': (1.0, 0.6),
     'L0_tok_la_ln_q_b': (0.0, 0.8),
     'L0_tok_la_ln_kv_g': (1.0, 0.2),
     'L0_tok_la_ln_kv_b': (0.0, 0.1),
     'L0_tok_la_proj_b': (0.0, 0.1),
     'L0_tok_ga_ln_q_g': (1.0, 0.6),
     'L0_tok_ga_ln_q_b': (0.0, 2.0),
     'L0_tok_ga_ln_kv_g': (1.0, 0.2),
     'L0_tok_ga_ln_kv_b': (0.0, 0.1),
     'L0_tok_ga_proj_b': (0.0, 0.1),
     'L0_tok_mod_b': (0.0, 0.1),
     'L0_attn_b_in': (0.0, 0.8),
     'L0_attn_b_s': (0.0, 0.396),
     'L0_attn_b_o': (0.0, 0.1),
     'L1_attn_v_b': (0.0, 0.3),
     'L1_attn_o_b': (0.0, 0.1),
     'L1_ffn_ln_gamma': (1.0, 0.2),
     'L1_ffn_ln_beta': (0.0, 0.383)}
    factors = {'L0_tok_la_wq': 8.0,
     'L0_tok_ga_wq': 4.884,
     'L1_attn_basis_w': 8.0,
     'L1_attn_core': 8.0,
     'L1_attn_head_residual': 8.0,
     'L1_ffn_b1s': 8.0,
     'L1_ffn_b2s': 8.0}
    for name, (base, spread) in spreads.items():
        noise = np.random.default_rng([zlib.crc32(name.encode()), seed]).standard_normal(out[name].shape)
        drawn = base * np.exp(spread * noise) if base else spread * noise
        out[name] = jnp.asarray(drawn.astype(out[name].dtype))
    for name, factor in factors.items():
        out[name] = (out[name] * factor).astype(out[name].dtype)
    return out
```

```python
from contextlib import ExitStack

import numpy as np

import concourse.bass as bass
from concourse import mybir

F32 = mybir.dt.float32
ALU = mybir.AluOpType
ACT = mybir.ActivationFunctionType
AX = mybir.AxisListType

P = 128
C = 256
KC = C // P
IMAGES, PATCH, SIDE, CS = 64, 14, 6, 3
HW = (SIDE // CS) ** 2
NWIN = CS * CS
WINDOWS = IMAGES * HW
PIX = 3 * PATCH * PATCH
KX, KP = 5, 118
WT = 14
TP = WT * NWIN
TILES = -(-WINDOWS // WT)
LASTW = WINDOWS - WT * (TILES - 1)
RING = 3
HEAD, TAIL = 2 * RING, TILES // RING * RING
H8, DH = 8, 32
T = HW + 2
TOK = IMAGES * T
TT = TOK // P
NH, HD, R = 16, 16, 64
NP2 = NH // 2
E8, FF, FC = 8, 1024, 8
CAP = TOK // E8
EPS = 1e-5
GELU_C, GELU_A = 0.7978845608028654, 0.044715
NEG = -1.0e30


def offsets(sizes):
    at, out = 0, {}
    for name, n in sizes:
        out[name] = (at, n)
        at += n
    return out, at


TOKW, TOKW_N = offsets([(n, KC * C) for n in (
    "wq", "wkT", "wv", "proj", "mod", "gwq", "gwkT", "gwv", "gproj")])
LAYW, LAYW_N = offsets([("w_in", KC * 2 * C), ("w_s", KC * C), ("w_o", KC * C), ("tern", KC * C),
                        ("basis", KC * 2 * R), ("v_w", KC * C), ("o_w", KC * C), ("gate", KC * E8),
                        ("heads", NH * R), ("core", R), ("coreT", R), ("bo_row", C), ("ob_row", C)])
COLS, COLS_N = offsets([(n, KC) for n in (
    "q_g", "q_b", "kv_g", "kv_b", "proj_b", "mod_b", "gq_g", "gq_b", "gkv_g", "gkv_b", "gproj_b",
    "class_emb", "cls_tok", "b_s", "v_b", "ln_g", "ln_b")] + [("b_in", 2 * KC), ("b1", E8 * FC),
                                                          ("b2", E8 * KC), ("class_row", C)])
CONS, CONS_N = offsets([("ident", P), ("pool", WT), ("mask", TP), ("mask_last", LASTW * NWIN),
                        ("causal", T), ("slots", CAP), ("spread", T * P), ("heads8", KC * P),
                        ("headcol", KC * H8), ("mean", P)])


def build(nc, x_d, convw_d, cols_d, cons_d, tokw_d, layw_d, exp_d, out):
    ctx = ExitStack()
    with ctx:
        def sb(name, shape):
            return ctx.enter_context(nc.sbuf_tensor(name, shape, F32))

        def sem(name):
            return ctx.enter_context(nc.semaphore(name))

        bank = [ctx.enter_context(nc.psum_tensor(f"bank{i}", [P, 512], F32)) for i in range(8)]

        cols = sb("cols", [P, COLS_N])
        cons = sb("cons", [P, CONS_N])
        layw = sb("layw", [P, LAYW_N])
        NRES, NATT = 3, 3
        resident = [sb(f"expert{e}", [P, 2 * KC * FF]) for e in range(NRES)]
        attic = sb("attic", [P, TILES * C + KC * TILES * TP + KC * H8 * WINDOWS + RING * KX * TP])
        desk = sb("desk", [P, 10800])

        def carve(tensor, at, *shape, parts=P):
            n = int(np.prod(shape))
            v = tensor[0:parts, at:at + n]
            names = "abcd"[:len(shape)]
            if len(shape) > 1:
                v = v.rearrange(f"p ({' '.join(names)}) -> p {' '.join(names)}",
                                **{k: s for k, s in zip(names, shape)})
            return v

        o = 0
        xhat_all = carve(attic, o, TILES, C); o += TILES * C
        winT = carve(attic, o, KC, TILES * TP); o += KC * TILES * TP
        qkT = carve(attic, o, KC, WINDOWS, H8)
        ctxT = qkT; o += KC * H8 * WINDOWS
        xt = [carve(attic, o + j * KX * TP, KX, TP) for j in range(RING)]; o += RING * KX * TP
        assert o <= attic.shape[1]

        o = 0
        tokw = desk[:, 0:TOKW_N]; o += TOKW_N
        convw = carve(desk, o, KX, C); o += KX * C
        pe_sb = [carve(desk, o + j * C, C) for j in range(RING)]; o += RING * C
        xhat = [carve(desk, o + j * C, C) for j in range(RING)]; o += RING * C
        redT = carve(desk, o, KC, WINDOWS); o += KC * WINDOWS
        redx = carve(desk, o, KC, C); o += KC * C
        lnrT = carve(desk, o, KC, WINDOWS); o += KC * WINDOWS
        qT = carve(desk, o, KC, WINDOWS); o += KC * WINDOWS
        s_msk = [carve(desk, o + j * TP, TP) for j in range(2)]; o += 2 * TP
        s_exp = [carve(desk, o + j * TP, TP) for j in range(2)]; o += 2 * TP
        s_att = [carve(desk, o + j * TP, TP) for j in range(2)]; o += 2 * TP
        s_attT = [carve(desk, o + j * P, P) for j in range(2)]; o += 2 * P
        assert o <= desk.shape[1], o
        o = TOKW_N
        aggT = carve(desk, o, KC, WINDOWS); o += KC * WINDOWS
        localT = carve(desk, o, KC, WINDOWS); o += KC * WINDOWS
        lox = carve(desk, o, KC, C); o += KC * C
        lnlT = carve(desk, o, KC, WINDOWS); o += KC * WINDOWS
        assert o <= TOKW_N + KX * C + 2 * RING * C
        gvT = redx
        gprod = lnrT
        h0T = sb("h0T", [P, KC, IMAGES, T])
        gattn = sb("gattn", [H8, 3, WINDOWS])
        small = sb("small", [P, 900])
        small_row = sb("class_row_ln", [1, C])
        so = [0]

        def tiny(*shape, parts=P):
            v = carve(small, so[0], *shape, parts=parts)
            so[0] += int(np.prod(shape))
            return v

        a_st, a_mv, a_ve, a_rs = ([tiny(n) for _ in range(RING)] for n in (6, 2, 1, 1))
        half, eps = tiny(4), tiny(1)
        w_st, w_mv, w_ve, w_rs = tiny(2, 6), tiny(2, 2), tiny(2), tiny(2)
        l_st, l_mv, l_ve, l_rs = tiny(2, 6), tiny(2, 2), tiny(2), tiny(2)
        c_st, c_mv, c_ve, c_rs = tiny(6), tiny(2), tiny(1), tiny(1)
        c_lnT, c_q, c_qbd, c_qk = tiny(KC), tiny(KC), tiny(KC, H8), tiny(KC, H8)
        s_mx, s_nmx, s_sum, s_rec = ([tiny(1) for _ in range(2)] for _ in range(4))
        g_mx, g_sum, g_rec = (tiny(IMAGES, parts=H8) for _ in range(3))
        gaggT = tiny(KC, IMAGES)
        t_st, t_mv, t_ve, t_rs = tiny(TT, 6), tiny(TT, 2), tiny(TT), tiny(TT)
        w_abs, w_scale = tiny(1), tiny(3)
        m8 = tiny(6, 8, parts=E8)
        slotT, valT = tiny(TT, E8), tiny(TT, E8)
        b_in_half, cls_fix = tiny(KC), tiny(KC)

        o = 0
        h = carve(desk, o, TT, C); o += TT * C
        xn = carve(desk, o, TT, C); o += TT * C
        xT = carve(desk, o, KC, TOK); o += KC * TOK
        base = carve(desk, o, TT, C); o += TT * C
        U = o
        gate_t, keep, val, sv, drive, scanT = (carve(desk, U + i * KC * TOK, KC, TOK) for i in range(6))
        latD = carve(desk, U, IMAGES, 2, T); o = U + 2 * TOK
        latT = latD[0:R, :, 0, :]
        ltT = carve(desk, o, TOK, NP2); o += NP2 * TOK
        att = [carve(desk, o + i * 2 * TOK, IMAGES, 2, T, parts=NP2 * T) for i in range(2)]; o += 4 * TOK
        vT = carve(desk, o, KC, TOK); o += KC * TOK
        yT = carve(desk, U + 2 * TOK, KC, TOK)
        prod = carve(desk, U + 5 * TOK, TOK)
        a_stat = carve(desk, o, 3, IMAGES * 2, parts=NP2 * T); o += 6 * IMAGES
        assert o <= desk.shape[1], o
        o = U
        val8 = carve(desk, o, TOK, parts=E8); o += TOK
        work8 = [carve(desk, o + i * TOK, TOK, parts=E8) for i in range(2)]; o += 2 * TOK
        sel8 = work8[1]
        pick = carve(desk, o, TT, E8, CAP); o += TT * E8 * CAP
        wpick = carve(desk, o, TT, E8, CAP); o += TT * E8 * CAP
        wpickT = carve(desk, o, E8 // 2, TOK, parts=2 * CAP); o += E8 // 2 * TOK
        xh2 = carve(desk, o, TT, C); o += TT * C
        assert o <= desk.shape[1], o
        ysT = xT
        o2 = U
        hb = [carve(desk, o2 + i * FC * CAP, FC, CAP) for i in range(2)]; o2 += 2 * FC * CAP
        assert o2 <= U + 3 * TOK
        ha = [sb(f"hidden{i}", [P, FC, CAP]) for i in range(2)]
        oT = [sb(f"outT{i}", [P, KC, 2, CAP]) for i in range(2)]
        opair = [sb(f"outpair{i}", [2 * CAP, C]) for i in range(2)]

        def expert(e):
            if e < NRES:
                return resident[e][:, :]
            if e >= NRES + NATT:
                return resident[e - NRES - NATT][:, :]
            n = 2 * KC * FF
            return attic[:, (e - NRES) * n:(e - NRES + 1) * n]

        def w_of(pack, table, name, *shape, parts=P):
            a, n = table[name]
            v = pack[0:parts, a:a + n]
            if shape:
                names = "abcd"[:len(shape)]
                v = v.rearrange(f"p ({' '.join(names)}) -> p {' '.join(names)}",
                                **{k: s for k, s in zip(names, shape)})
            return v

        def col(name, k=0, n=1, parts=P):
            a = COLS[name][0]
            return cols[0:parts, a + k:a + k + n]

        tw = {n: w_of(tokw, TOKW, n, KC, C) for n in TOKW}
        lw = {n: w_of(layw, LAYW, n, KC, s) for n, s in (
            ("w_in", 2 * C), ("w_s", C), ("w_o", C), ("tern", C), ("basis", 2 * R), ("v_w", C),
            ("o_w", C), ("gate", E8))}
        heads = w_of(layw, LAYW, "heads", NH, R, parts=R)
        ident = w_of(cons, CONS, "ident")
        pool_m = w_of(cons, CONS, "pool", parts=TP)
        mask = w_of(cons, CONS, "mask", parts=H8 * WT)
        mask_last = w_of(cons, CONS, "mask_last", parts=H8 * LASTW)
        causal = w_of(cons, CONS, "causal", parts=NP2 * T)
        slots = w_of(cons, CONS, "slots")
        spread = w_of(cons, CONS, "spread", T, P, parts=NP2 * T)
        heads8 = w_of(cons, CONS, "heads8", KC, P, parts=H8)
        headcol = w_of(cons, CONS, "headcol", KC, H8)
        mean_m = w_of(cons, CONS, "mean")

        S = {}

        def s(name):
            if name not in S:
                S[name] = sem(name)
            return S[name]

        conv_bank = bank[0:3]
        red_bank = bank[3:5]
        tr_bank = bank[5:8]

        block = ctx.enter_context(nc.Block())

        @block.sync
        def _(sp):
            sp.dma_start(convw, convw_d).then_inc(s("convw_in"), 16)
            for j in range(RING):
                sp.dma_start(xt[j][0:KP], x_d[j]).then_inc(s(f"x_in{j}"), 16)
                if j == 0:
                    sp.dma_start(cons[:, :], cons_d).then_inc(s("cons_in"), 16)
                    sp.dma_start(cols[:, :], cols_d).then_inc(s("cols_in"), 16)
            sp.dma_start(tokw, tokw_d).then_inc(s("tokw_in"), 16)
            with sp.Fori(1, TILES // RING) as r:
                for j in range(RING):
                    sp.wait_ge(s("conv_done"), RING * r + (j - RING + 1))
                    sp.dma_start(xt[j][0:KP], x_d[RING * r + j]).then_inc(s(f"x_in{j}"), 16)
            for t in range(TILES // RING * RING, TILES):
                sp.wait_ge(s("conv_done"), t - RING + 1)
                sp.dma_start(xt[t % RING][0:KP], x_d[t]).then_inc(s(f"x_in{t % RING}"), 16)
            sp.wait_ge(s("agg_done"), 1)
            for e in range(NRES, E8):
                if e >= NRES + NATT:
                    sp.wait_ge(s("eo_done"), e - NRES - NATT + 1)
                sp.dma_start(expert(e), exp_d[e]).then_inc(s(f"expert_in{e}"), 16)
            for t in range(TT):
                sp.wait_ge(s("out_ready"), t + 1)
                sp.dma_start(out[t * P:(t + 1) * P, :], base[:, t, :]).then_inc(s("out_sent"), 16)
            sp.wait_ge(s("out_sent"), 16 * TT)

        @block.tensor
        def _(pe):
            mm = pe.matmul

            def conv(r, j):
                t = RING * r + j
                pe.wait_ge(s(f"x_in{j}"), 16 * r + 16)
                if not (isinstance(t, int) and t < RING):
                    pe.wait_ge(s("pe_copied"), t - (RING - 1))
                for k in range(KX):
                    i = mm(conv_bank[j][0:TP, 0:C], xt[j][0:KP, k, :], convw[0:KP, k, :],
                           start=(k == 0), stop=(k == KX - 1))
                i.then_inc(s("conv_done"), 1)

            def window_mean(t, j):
                pe.wait_ge(s("pe_copied"), t + 1)
                for k in range(KC):
                    i = mm(red_bank[k][:, bass.ds(t * WT, WT)], pe_sb[j][0:TP, k * P:(k + 1) * P], pool_m,
                           start=True, stop=True)
                i.then_inc(s("pool_done"), 1)

            def turn(t, j):
                pe.wait_ge(s("xhat_ready"), t + 1)
                if not (isinstance(t, int) and t < RING):
                    pe.wait_ge(s("winT_ready"), t - (RING - 1))
                for k in range(KC):
                    i = pe.transpose(tr_bank[j][:, k * P:k * P + TP], xhat[j][0:TP, k * P:(k + 1) * P],
                                     ident[0:TP, 0:TP])
                i.then_inc(s("turned"), 1)

            pe.wait_ge(s("convw_in"), 16)
            def around(t, j, before):
                if before >= 1:
                    window_mean(t - 1, (j - 1) % RING)
                if before >= 2:
                    turn(t - 2, (j - 2) % RING)

            for t in range(HEAD):
                conv(t // RING, t % RING)
                if t == 0:
                    pe.wait_ge(s("cons_in"), 16)
                around(t, t % RING, t)
            with pe.Fori(HEAD // RING, TILES // RING) as r:
                for j in range(RING):
                    conv(r, j)
                    around(RING * r + j, j, 2)
            for t in range(TAIL, TILES):
                conv(t // RING, t % RING)
                around(t, t % RING, 2)
            window_mean(TILES - 1, (TILES - 1) % RING)
            turn(TILES - 2, (TILES - 2) % RING)
            turn(TILES - 1, (TILES - 1) % RING)

            pe.wait_ge(s("redT_ready"), 2)
            for w in range(2):
                for k in range(KC):
                    i = pe.transpose(bank[0][:, w * C + k * P:w * C + (k + 1) * P],
                                     redT[:, k, w * P:(w + 1) * P], ident)
            i.then_inc(s("red_major"), 1)
            pe.wait_ge(s("redx_ready"), 2)
            for k in range(KC):
                for w in range(2):
                    i = pe.transpose(bank[1 + k][:, w * P:(w + 1) * P],
                                     redx[:, w, k * P:(k + 1) * P], ident)
            i.then_inc(s("redx_turned"), 1)
            pe.wait_ge(s("tokw_in"), 16)
            pe.wait_ge(s("lnrT_ready"), 2)
            for m in range(KC):
                for k in range(KC):
                    i = mm(bank[3][:, m * C:(m + 1) * C], tw["wq"][:, k, m * P:(m + 1) * P], lnrT[:, k, :],
                           start=(k == 0), stop=(k == KC - 1))
            i.then_inc(s("q_done"), 1)
            pe.wait_ge(s("qT_ready"), 1)
            pe.wait_ge(s("winT_ready"), TILES)
            for hh in range(H8):
                m, g = divmod(hh, 4)
                if m:
                    pe.wait_ge(s("qk_dve" if g % 2 == 0 else "qk_act"), g // 2 + 1)
                for k in range(KC):
                    i = mm(bank[4 + g][:, k * C:(k + 1) * C], tw["wkT"][g * DH:(g + 1) * DH, m, k * P:(k + 1) * P],
                           qT[g * DH:(g + 1) * DH, m, :], start=True, stop=True)
                i.then_inc(s("qk_done"), 1)

            def n_win(t):
                return WT if t < TILES - 1 else LASTW

            def scores(t):
                n = n_win(t)
                if t == 0:
                    pe.wait_ge(s("qk_dve"), 4)
                    pe.wait_ge(s("qk_act"), 4)
                if t >= 2:
                    pe.wait_ge(s("masked"), t - 1)
                for k in range(KC):
                    i = mm(bank[t % 2][0:H8 * n, 0:n * NWIN], qkT[:, k, t * WT:t * WT + n, :],
                           winT[:, k, t * TP:t * TP + n * NWIN], start=(k == 0), stop=(k == KC - 1))
                i.then_inc(s("scored"), 1)

            def turn_att(t):
                n = n_win(t)
                pe.wait_ge(s("att_ready"), t + 1)
                if t >= 2:
                    pe.wait_ge(s("attT_ready"), t - 1)
                pe.transpose(bank[2 + t % 2][0:n * NWIN, 0:H8 * n], s_att[t % 2][0:H8 * n, 0:n * NWIN],
                             ident[0:H8 * n, 0:H8 * n]).then_inc(s("att_turned"), 1)

            def attend(t):
                n = n_win(t)
                pe.wait_ge(s("attT_ready"), t + 1)
                if t == 0:
                    pe.wait_ge(s("xall_done"), TILES)
                if t >= 2:
                    pe.wait_ge(s("ctx_act"), t - 1)
                    pe.wait_ge(s("ctx_dve"), t - 1)
                for k in range(KC):
                    i = mm(bank[4 + 2 * k + t % 2][:, 0:H8 * n], xhat_all[0:n * NWIN, t, k * P:(k + 1) * P],
                           s_attT[t % 2][0:n * NWIN, 0:H8 * n], start=True, stop=True)
                i.then_inc(s("attended"), 1)

            for t in range(TILES + 2):
                if t < TILES:
                    scores(t)
                if 1 <= t <= TILES:
                    turn_att(t - 1)
                if t >= 2:
                    attend(t - 2)

            pe.wait_ge(s("ctx_act"), TILES)
            pe.wait_ge(s("ctx_dve"), TILES)
            pe.wait_ge(s("c_row"), 1)
            for k in range(KC):
                i = mm(bank[7][:, k:k + 1], small_row[0:1, k * P:(k + 1) * P], ident[0:1, 0:1], start=True, stop=True)
            i.then_inc(s("c_turned"), 1)
            pe.wait_ge(s("c_ln"), 2)
            for m in range(KC):
                for k in range(KC):
                    i = mm(bank[7][:, 8 + m:9 + m], tw["gwq"][:, k, m * P:(m + 1) * P], c_lnT[:, k:k + 1],
                           start=(k == 0), stop=(k == KC - 1))
            i.then_inc(s("c_q_done"), 1)
            pe.wait_ge(s("c_qbd"), 2)
            for k in range(KC):
                for m in range(KC):
                    i = mm(bank[7][:, 16 + k * H8:16 + (k + 1) * H8], tw["gwkT"][:, m, k * P:(k + 1) * P],
                           c_qbd[:, m, :], start=(m == 0), stop=(m == KC - 1))
            i.then_inc(s("c_qk_done"), 1)

            for m in range(KC):
                for k in range(KC):
                    for g in range(4):
                        hh = 4 * m + g
                        i = mm(bank[6][g * DH:(g + 1) * DH, m * C:(m + 1) * C],
                               tw["wv"][:, k, hh * DH:(hh + 1) * DH], ctxT[:, k, :, hh],
                               start=(k == 0), stop=(k == KC - 1))
            i.then_inc(s("agg_done"), 1)
            pe.wait_ge(s("aggT_ready"), 1)
            for m in range(KC):
                for k in range(KC):
                    i = mm(bank[m][:, 0:C], tw["proj"][:, k, m * P:(m + 1) * P], aggT[:, k, :],
                           start=(k == 0), stop=(k == KC - 1))
                i.then_inc(s("proj_done"), 1)
            pe.wait_ge(s("local_ready"), 2)
            for w in range(2):
                for k in range(KC):
                    i = pe.transpose(bank[2][:, w * C + k * P:w * C + (k + 1) * P],
                                     localT[:, k, w * P:(w + 1) * P], ident)
            i.then_inc(s("lo_major"), 1)
            for m in range(KC):
                for k in range(KC):
                    i = mm(bank[3][:, m * C:(m + 1) * C], tw["mod"][:, k, m * P:(m + 1) * P], localT[:, k, :],
                           start=(k == 0), stop=(k == KC - 1))
            i.then_inc(s("mod_done"), 1)
            pe.wait_ge(s("lox_ready"), 2)
            for k in range(KC):
                for w in range(2):
                    i = pe.transpose(bank[4 + k][:, w * P:(w + 1) * P],
                                     lox[:, w, k * P:(k + 1) * P], ident)
            i.then_inc(s("lox_turned"), 1)
            pe.wait_ge(s("lnlT_ready"), 2)
            pe.wait_ge(s("c_qk_ready"), 1)
            for k in range(KC):
                i = mm(bank[7][0:H8, 0:WINDOWS], c_qk[:, k, :], lnlT[:, k, :], start=(k == 0), stop=(k == KC - 1))
            i.then_inc(s("gscored"), 1)
            for m in range(KC):
                for k in range(KC):
                    i = mm(bank[6][:, m * C:(m + 1) * C], tw["gwv"][:, k, m * P:(m + 1) * P], lnlT[:, k, :],
                           start=(k == 0), stop=(k == KC - 1))
            i.then_inc(s("gv_done"), 1)
            pe.wait_ge(s("gattn_ready"), 1)
            for m in range(KC):
                i = mm(bank[0][:, m * C:(m + 1) * C], heads8[:, m, :], gattn[:, 2, :], start=True, stop=True)
            i.then_inc(s("gspread"), 1)
            pe.wait_ge(s("gagg_ready"), 1)
            for m in range(KC):
                for k in range(KC):
                    i = mm(bank[1][:, m * IMAGES:(m + 1) * IMAGES], tw["gproj"][:, k, m * P:(m + 1) * P],
                           gaggT[:, k, :], start=(k == 0), stop=(k == KC - 1))
            i.then_inc(s("gproj_done"), 1)

            pe.wait_ge(s("h0T_ready"), 6)
            h0T_v = h0T[:, :, :, :].rearrange("p k i t -> p k (i t)")
            for t in range(TT):
                for k in range(KC):
                    i = pe.transpose(bank[2 + t][:, k * P:(k + 1) * P], h0T_v[:, k, t * P:(t + 1) * P], ident)
                i.then_inc(s("h0_major"), 1)

            def turn_x(n):
                for t in range(TT):
                    pe.wait_ge(s("xn_ready"), TT * n + t + 1)
                    if t == 0 and n:
                        pe.wait_ge(s("xT_ready"), 2 * n)
                    for k in range(KC):
                        i = pe.transpose(bank[6 + k][:, t * P:(t + 1) * P], xn[:, t, k * P:(k + 1) * P], ident)
                i.then_inc(s("x_turned"), 1)
                pe.wait_ge(s("xT_ready"), 2 * (n + 1))

            def to_tokens(banks, srcT, w, done):
                for t in range(TT):
                    for k in range(KC):
                        i = mm(bank[banks + t][:, 0:C], srcT[:, k, t * P:(t + 1) * P], w[:, k, :],
                               start=(k == 0), stop=(k == KC - 1))
                    i.then_inc(s(done), 1)

            turn_x(0)
            for m in range(2 * KC):
                for k in range(KC):
                    i = mm(bank[m][:, 0:TOK], lw["w_in"][:, k, m * P:(m + 1) * P], xT[:, k, :],
                           start=(k == 0), stop=(k == KC - 1))
                i.then_inc(s("gv_in_done"), 1)
            pe.wait_ge(s("val_ready"), 2)
            for m in range(KC):
                for k in range(KC):
                    i = mm(bank[4 + m][:, 0:TOK], lw["w_s"][:, k, m * P:(m + 1) * P], val[:, k, :],
                           start=(k == 0), stop=(k == KC - 1))
                i.then_inc(s("sv_done"), 1)
            pe.wait_ge(s("scan_ready"), 2)
            to_tokens(0, scanT, lw["w_o"], "mix_done")
            pe.wait_ge(s("w_abs_ready"), 1)
            mm(bank[3][:, 0:1], mean_m, w_abs, start=True, stop=True).then_inc(s("w_mean_done"), 1)
            turn_x(1)
            pe.wait_ge(s("tern_ready"), 1)
            pe.wait_ge(s("h_ready"), TT)
            to_tokens(0, xT, lw["tern"], "tern_done")
            turn_x(2)
            for k in range(KC):
                i = mm(bank[3][:, 0:TOK], lw["basis"][:, k, :], xT[:, k, :], start=(k == 0), stop=(k == KC - 1))
            i.then_inc(s("lat_done"), 1)
            for m in range(KC):
                for k in range(KC):
                    i = mm(bank[4 + m][:, 0:TOK], lw["v_w"][:, k, m * P:(m + 1) * P], xT[:, k, :],
                           start=(k == 0), stop=(k == KC - 1))
                i.then_inc(s("v_done"), 1)
            pe.wait_ge(s("lat_ready"), 2)
            pe.wait_ge(s("heads_ready"), 1)
            pe.wait_ge(s("h_ready"), 2 * TT)
            for j in range(NP2):
                if j >= 3:
                    pe.wait_ge(s("lt_act" if (j - 3) % 2 else "lt_dve"), (j - 3) // 2 + 1)
                mm(bank[j % 3][:, 0:TOK], heads[:, 2 * j:2 * j + 2, :], latT, start=True, stop=True)\
                    .then_inc(s("lt_done"), 1)
            pe.wait_ge(s("lt_act"), 4)
            pe.wait_ge(s("lt_dve"), 4)
            for i_ in range(IMAGES):
                i = mm(bank[6 + i_ // 32][0:NP2 * T, (i_ % 32) * 2 * T:(i_ % 32 + 1) * 2 * T],
                       ltT[:, i_ * T:(i_ + 1) * T, :], latD[:, i_, :, :], start=True, stop=True)
                if i_ % 32 == 31:
                    i.then_inc(s("att_scored"), 1)
            pe.wait_ge(s("att_probs"), 1)
            pe.wait_ge(s("vT_ready"), 2)
            for t in range(T):
                for p in range(2):
                    n = t * 2 + p
                    if n >= 4:
                        pe.wait_ge(s("y_mul"), n - 3)
                    b = (0, 1, 2, 3)[n % 4]
                    mm(bank[b][:, 0:IMAGES * (t + 1)], spread[:, t, :], att[0][:, :, p, 0:t + 1],
                       start=True, stop=True).then_inc(s("spread_done"), 1)
            pe.wait_ge(s("y_ready"), 12)
            to_tokens(0, yT, lw["o_w"], "lat_out_done")
            turn_x(3)
            for k in range(KC):
                i = mm(bank[3][0:E8, 0:TOK], lw["gate"][:, k, :], xT[:, k, :], start=(k == 0), stop=(k == KC - 1))
            i.then_inc(s("gate_done"), 1)
            pe.wait_ge(s("slots_ready"), 1)
            for t in range(TT):
                pe.transpose(bank[4][:, t * 16:t * 16 + E8], sel8[:, t * P:(t + 1) * P], ident[0:E8, 0:E8])
                i = pe.transpose(bank[4][:, t * 16 + E8:t * 16 + 2 * E8], val8[:, t * P:(t + 1) * P],
                                 ident[0:E8, 0:E8])
            i.then_inc(s("slots_turned"), 1)
            pe.wait_ge(s("pick_ready"), 1)
            pe.wait_ge(s("xn_ready"), 5 * TT)
            for k in range(KC):
                for t in range(TT):
                    i = mm(bank[6 + k][:, 0:TOK], xh2[:, t, k * P:(k + 1) * P],
                           pick[:, t, :, :], start=(t == 0), stop=(t == TT - 1))
            i.then_inc(s("gathered"), 1)
            pe.wait_ge(s("wpick_ready"), 1)
            for q in range(E8 // 2):
                if q >= 1:
                    pe.wait_ge(s("wpickT_ready"), q)
                for t in range(TT):
                    i = pe.transpose(bank[5][0:2 * CAP, t * P:(t + 1) * P], wpick[:, t, 2 * q:2 * q + 2, :],
                                     ident)
                i.then_inc(s("wpick_turned"), 1)
            pe.wait_ge(s("wpickT_ready"), E8 // 2)
            pe.wait_ge(s("ysT_ready"), 2)

            def expert_in(e):
                pe.wait_ge(s(f"expert_in{e}"), 16)
                if e >= 2:
                    pe.wait_ge(s("hb_ready"), e - 1)
                w1 = expert(e)[:, 0:KC * FF].rearrange("p (k f) -> p k f", k=KC)
                for f in range(FC):
                    for k in range(KC):
                        i = mm(bank[e % 2][:, f * CAP:(f + 1) * CAP], w1[:, k, f * P:(f + 1) * P],
                               ysT[:, k, e * CAP:(e + 1) * CAP], start=(k == 0), stop=(k == KC - 1))
                i.then_inc(s("hid_done"), 1)

            def expert_out(e):
                pe.wait_ge(s("ha_ready"), e + 1)
                if e >= 2:
                    pe.wait_ge(s("oT_ready"), e - 1)
                w2 = expert(e)[:, KC * FF:2 * KC * FF].rearrange("p (f c) -> p f c", f=FC)
                for m in range(KC):
                    for f in range(FC):
                        i = mm(bank[2 + e % 2][:, m * CAP:(m + 1) * CAP], w2[:, f, m * P:(m + 1) * P],
                               ha[e % 2][:, f, :], start=(f == 0), stop=(f == FC - 1))
                i.then_inc(s("eo_done"), 1)

            def pair_turn(q):
                pe.wait_ge(s("oT_ready"), 2 * q + 2)
                if q >= 1:
                    pe.wait_ge(s("opair_ready"), q)
                for m in range(KC):
                    i = pe.transpose(bank[4][0:2 * CAP, m * P:(m + 1) * P], oT[q % 2][:, m, :, :], ident)
                i.then_inc(s("opair_turned"), 1)

            def pair_add(q):
                pe.wait_ge(s("opair_ready"), q + 1)
                for t in range(TT):
                    i = mm(bank[5 + t][:, 0:C], wpickT[:, q, t * P:(t + 1) * P], opair[q % 2][:, :],
                           start=(q == 0), stop=(q == E8 // 2 - 1))
                    if q == E8 // 2 - 1 or t == TT - 1:
                        i.then_inc(s("combined"), 1)

            for e in range(E8 + 1):
                if e < E8:
                    expert_in(e)
                if e >= 1:
                    expert_out(e - 1)
                if e >= 2 and e % 2 == 1:
                    pair_turn((e - 3) // 2)
                if e >= 4 and e % 2 == 0:
                    pair_add((e - 4) // 2)
            pair_turn(E8 // 2 - 1)
            pair_add(E8 // 2 - 1)

        @block.vector
        def _(dve):
            ts, tt, stt = dve.tensor_scalar, dve.tensor_tensor, dve.scalar_tensor_tensor

            def stats(t, j):
                dve.wait_ge(s("pe_copied"), t + 1)
                dve.bn_stats(a_st[j][0:TP], pe_sb[j][0:TP]).then_inc(s("bn_done"), 1)

            def norm(t, j):
                dve.wait_ge(s("rs_ready"), t + 1)
                if not (isinstance(t, int) and t < RING):
                    dve.wait_ge(s("turned"), t - (RING - 1))
                    dve.wait_ge(s("xall_done"), t - (RING - 1))
                ts(xhat[j][0:TP], pe_sb[j][0:TP], a_mv[j][0:TP, 0:1], a_rs[j][0:TP], ALU.subtract, ALU.mult)\
                    .then_inc(s("xhat_ready"), 1)

            def patch_step(t, j, first=False):
                stats(t, j)
                dve.wait_ge(s("bn_done"), t + 1)
                if not first:
                    norm(t - 1, (j - 1) % RING)
                dve.bn_aggr(a_mv[j][0:TP], a_st[j][0:TP]).then_inc(s("mv_ready"), 1)

            for t in range(HEAD):
                patch_step(t, t % RING, t == 0)
            with dve.Fori(HEAD // RING, TILES // RING) as r:
                for j in range(RING):
                    patch_step(RING * r + j, j)
            for t in range(TAIL, TILES):
                patch_step(t, t % RING)
            norm(TILES - 1, (TILES - 1) % RING)
            dve.wait_ge(s("pool_done"), TILES)
            dve.tensor_copy(redT[:, 0, :], red_bank[0][:, 0:WINDOWS]).then_inc(s("redT_ready"), 1)

            def norm_two(src_bank, st, mv, rs, dst, major, mv_name, rs_name, out_name, n_bn):
                dve.wait_ge(s(major), 1)
                for w in range(2):
                    dve.bn_stats(st[:, w, :], src_bank[:, w * C:(w + 1) * C]).then_inc(s("bn2_done"), 1)
                for w in range(2):
                    dve.wait_ge(s("bn2_done"), n_bn + w + 1)
                    dve.bn_aggr(mv[:, w, :], st[:, w, :]).then_inc(s(mv_name), 1)
                dve.wait_ge(s(rs_name), 1)
                for w in range(2):
                    ts(dst[:, w, :], src_bank[:, w * C:(w + 1) * C], mv[:, w, 0:1], rs[:, w:w + 1],
                       ALU.subtract, ALU.mult).then_inc(s(out_name), 1)

            norm_two(bank[0], w_st, w_mv, w_rs, redx, "red_major", "w_mv_ready", "w_rs_ready", "redx_ready", 0)
            dve.wait_ge(s("redx_turned"), 1)
            ts(lnrT[:, 0, :], bank[1][:, 0:C], col("q_g", 0), col("q_b", 0), ALU.mult, ALU.add)\
                .then_inc(s("lnrT_ready"), 1)
            dve.wait_ge(s("q_done"), 1)
            dve.tensor_copy(qT.rearrange("p k w -> p (k w)"), bank[3][:, :]).then_inc(s("qT_ready"), 1)
            for n in range(4):
                m, g = divmod(2 * n, 4)
                dve.wait_ge(s("qk_done"), 2 * n + 1)
                dve.tensor_copy(qkT[:, :, :, 4 * m + g], bank[4 + g][:, :].rearrange("p (k w) -> p k w", k=KC))\
                    .then_inc(s("qk_dve"), 1)

            def n_win(t):
                return WT if t < TILES - 1 else LASTW

            def masked(t):
                n, j = n_win(t), t % 2
                rows, wide = H8 * n, n * NWIN
                mk = mask if n == WT else mask_last
                dve.wait_ge(s("scored"), t + 1)
                if t >= 2:
                    dve.wait_ge(s("s_exp_ready"), t - 1)
                dve.tensor_tensor_reduce(s_msk[j][0:rows, 0:wide], bank[j][0:rows, 0:wide], mk[0:rows, 0:wide],
                                         1.0, NEG, ALU.add, ALU.max, s_mx[j][0:rows]).then_inc(s("masked"), 1)
                dve.wait_ge(s("masked"), t + 1)
                ts(s_nmx[j][0:rows], s_mx[j][0:rows], -C ** -0.5, None, ALU.mult).then_inc(s("nmx_ready"), 1)

            def soft(t):
                n, j = n_win(t), t % 2
                rows, wide = H8 * n, n * NWIN
                dve.wait_ge(s("s_exp_ready"), t + 1)
                dve.reciprocal(s_rec[j][0:rows], s_sum[j][0:rows]).then_inc(s("rec_ready"), 1)
                dve.wait_ge(s("rec_ready"), t + 1)
                if t >= 2:
                    dve.wait_ge(s("att_turned"), t - 1)
                ts(s_att[j][0:rows, 0:wide], s_exp[j][0:rows, 0:wide], s_rec[j][0:rows], None, ALU.mult)\
                    .then_inc(s("att_ready"), 1)

            def attT(t):
                n, j = n_win(t), t % 2
                dve.wait_ge(s("att_turned"), t + 1)
                if t >= 2:
                    dve.wait_ge(s("attended"), t - 1)
                dve.tensor_copy(s_attT[j][0:n * NWIN, 0:H8 * n], bank[2 + j][0:n * NWIN, 0:H8 * n])\
                    .then_inc(s("attT_ready"), 1)

            def ctx0(t):
                n, j = n_win(t), t % 2
                dve.wait_ge(s("attended"), t + 1)
                ts(ctxT[:, 0, t * WT:t * WT + n, :],
                   bank[4 + j][:, 0:H8 * n].rearrange("p (w h) -> p w h", h=H8),
                   col("kv_g", 0), col("kv_b", 0), ALU.mult, ALU.add).then_inc(s("ctx_dve"), 1)

            for t in range(TILES + 2):
                if t < TILES:
                    masked(t)
                if 1 <= t <= TILES:
                    soft(t - 1)
                    attT(t - 1)
                if t >= 2:
                    ctx0(t - 2)

            dve.bn_stats(c_st[0:1], cols[0:1, COLS["class_row"][0]:COLS["class_row"][0] + C]).then_inc(s("c_bn"), 1)
            dve.wait_ge(s("c_bn"), 1)
            dve.bn_aggr(c_mv[0:1], c_st[0:1]).then_inc(s("c_mv_ready"), 1)
            dve.wait_ge(s("c_rs_ready"), 1)
            ts(small_row[0:1, :], cols[0:1, COLS["class_row"][0]:COLS["class_row"][0] + C], c_mv[0:1, 0:1],
               c_rs[0:1], ALU.subtract, ALU.mult).then_inc(s("c_row"), 1)
            dve.wait_ge(s("c_turned"), 1)
            for k in range(KC):
                ts(c_lnT[:, k:k + 1], bank[7][:, k:k + 1], col("gq_g", k), col("gq_b", k), ALU.mult, ALU.add)\
                    .then_inc(s("c_ln"), 1)
            dve.wait_ge(s("c_q_done"), 1)
            for k in range(KC):
                ts(c_qbd[:, k, :], headcol[:, k, :], bank[7][:, 8 + k:9 + k], None, ALU.mult)\
                    .then_inc(s("c_qbd"), 1)
            dve.wait_ge(s("c_qk_done"), 1)
            dve.tensor_copy(c_qk.rearrange("p k h -> p (k h)"), bank[7][:, 16:16 + KC * H8])\
                .then_inc(s("c_qk_ready"), 1)

            dve.wait_ge(s("agg_done"), 1)
            dve.tensor_copy(aggT.rearrange("p k w -> p (k w)"), bank[6][:, :]).then_inc(s("aggT_ready"), 1)
            for m in range(KC):
                dve.wait_ge(s("proj_done"), m + 1)
                stt(localT[:, m, :], bank[m][:, 0:C], col("proj_b", m), redT[:, m, :], ALU.add, ALU.add)\
                    .then_inc(s("local_ready"), 1)
            norm_two(bank[2], l_st, l_mv, l_rs, lox, "lo_major", "l_mv_ready", "l_rs_ready", "lox_ready", 2)
            dve.wait_ge(s("lox_turned"), 1)
            ts(lnlT[:, 0, :], bank[4][:, 0:C], col("gkv_g", 0), col("gkv_b", 0), ALU.mult, ALU.add)\
                .then_inc(s("lnlT_ready"), 1)
            dve.wait_ge(s("gscored"), 1)
            g3 = lambda v: v.rearrange("p (i w) -> p i w", w=HW)
            dve.tensor_reduce(g_mx, g3(bank[7][0:H8, 0:WINDOWS]), AX.X, ALU.max).then_inc(s("g_chain"), 1)
            dve.wait_ge(s("g_chain"), 1)
            tt(g3(gattn[:, 0, :]), g3(bank[7][0:H8, 0:WINDOWS]), g_mx.unsqueeze(2).to_broadcast([H8, IMAGES, HW]),
               ALU.subtract).then_inc(s("g_shifted"), 1)
            dve.wait_ge(s("g_exp"), 1)
            dve.tensor_reduce(g_sum, g3(gattn[:, 1, :]), AX.X, ALU.add).then_inc(s("g_chain"), 1)
            dve.wait_ge(s("g_chain"), 2)
            dve.reciprocal(g_rec, g_sum).then_inc(s("g_chain"), 1)
            dve.wait_ge(s("g_chain"), 3)
            tt(g3(gattn[:, 2, :]), g3(gattn[:, 1, :]), g_rec.unsqueeze(2).to_broadcast([H8, IMAGES, HW]), ALU.mult)\
                .then_inc(s("gattn_ready"), 1)
            dve.wait_ge(s("gspread"), 1)
            dve.wait_ge(s("gvT_ready"), 1)
            tt(gprod.rearrange("p k w -> p (k w)"), bank[0][:, :], gvT.rearrange("p k w -> p (k w)"), ALU.mult)\
                .then_inc(s("g_chain"), 1)
            dve.wait_ge(s("g_chain"), 4)
            dve.tensor_reduce(gaggT.rearrange("p k i -> p (k i)"),
                              gprod.rearrange("p k (i w) -> p (k i) w", w=HW), AX.X, ALU.add)\
                .then_inc(s("gagg_ready"), 1)
            dve.wait_ge(s("gproj_done"), 1)
            for m in range(KC):
                ts(h0T[:, m, :, T - 1], bank[1][:, m * IMAGES:(m + 1) * IMAGES], col("gproj_b", m),
                   col("class_emb", m), ALU.add, ALU.add).then_inc(s("h0T_ready"), 1)

            def norm_tokens(n, src, ready=None, ready_n=0, dst=None):
                dst = xn if dst is None else dst
                if n:
                    dve.wait_ge(s("t_rs_ready"), n)
                for t in range(TT):
                    if ready:
                        dve.wait_ge(s(ready), ready_n + t + 1)
                    dve.bn_stats(t_st[:, t, :], src(t)).then_inc(s("t_bn"), 1)
                for t in range(TT):
                    dve.wait_ge(s("t_bn"), TT * n + t + 1)
                    if t == 0 and n:
                        dve.wait_ge(s("xn_ready"), TT * n)
                    i = dve.bn_aggr(t_mv[:, t, :], t_st[:, t, :])
                    i.then_inc(s("t_mv_ready"), 1)
                dve.wait_ge(s("t_rs_ready"), n + 1)
                for t in range(TT):
                    if n and t == 0 and n < 4:
                        dve.wait_ge(s("x_turned"), n)
                        if n == 1:
                            dve.wait_ge(s("base_ready"), 1)
                    ts(dst[:, t, :], src(t), t_mv[:, t, 0:1], t_rs[:, t:t + 1], ALU.subtract, ALU.mult)\
                        .then_inc(s("xn_ready"), 1)

            norm_tokens(0, lambda t: h[:, t, :], "h0_ready")
            dve.wait_ge(s("x_turned"), 1)
            dve.tensor_copy(xT[:, 0, :], bank[6][:, 0:TOK]).then_inc(s("xT_ready"), 1)
            dve.wait_ge(s("gv_in_done"), 4)
            for m in range(KC):
                ts(val[:, m, :], bank[2 + m][:, 0:TOK], col("b_in", KC + m), None, ALU.add).then_inc(s("val_ready"), 1)
            for m in range(KC):
                dve.wait_ge(s("gate_tanh"), m + 1)
                ts(keep[:, m, :], gate_t[:, m, :], -0.5, 0.5, ALU.mult, ALU.add).then_inc(s("keep_made"), 1)
                ts(drive[:, m, :], gate_t[:, m, :], 0.5, 0.5, ALU.mult, ALU.add).then_inc(s("gate_made"), 1)
                dve.wait_ge(s("keep_made"), 2 * m + 1)
                dve.memset(keep[:, m, :].rearrange("p (i t) -> p i t", t=T)[:, :, 0:1], 0.0)\
                    .then_inc(s("keep_made"), 1)
            for m in range(KC):
                dve.wait_ge(s("sv_tanh"), m + 1)
                dve.wait_ge(s("gate_made"), 2)
                tt(sv[:, m, :], sv[:, m, :], drive[:, m, :], ALU.mult).then_inc(s("drive_made"), 1)
                dve.wait_ge(s("drive_made"), m + 1)
                dve.wait_ge(s("keep_made"), 4)
                dve.tensor_tensor_scan(scanT[:, m, :], keep[:, m, :], sv[:, m, :], 0.0, ALU.mult, ALU.add)\
                    .then_inc(s("scan_ready"), 1)

            dve.tensor_reduce(w_abs, lw["tern"].rearrange("p k c -> p (k c)"), AX.X, ALU.add,
                              apply_absolute_value=True).then_inc(s("w_abs_ready"), 1)
            dve.wait_ge(s("base_ready"), 1)
            for t in range(TT):
                dve.wait_ge(s("mix_done"), t + 1)
                tt(h[:, t, :], bank[t][:, 0:C], base[:, t, :], ALU.add).then_inc(s("h_ready"), 1)
            norm_tokens(1, lambda t: h[:, t, :], "h_ready", 0)
            dve.wait_ge(s("w_mean_done"), 1)
            ts(w_scale[:, 0:1], bank[3][:, 0:1], EPS, None, ALU.max).then_inc(s("w_chain"), 1)
            dve.wait_ge(s("w_chain"), 1)
            ts(w_scale[:, 1:2], w_scale[:, 0:1], 0.5, None, ALU.mult).then_inc(s("w_chain"), 1)
            ts(w_scale[:, 2:3], w_scale[:, 0:1], -0.5, None, ALU.mult).then_inc(s("w_chain"), 1)
            dve.wait_ge(s("w_chain"), 3)
            flat = lw["tern"].rearrange("p k c -> p (k c)")
            tmp = gate_t.rearrange("p k n -> p (k n)")[:, 0:KC * C]
            ts(tmp, flat, w_scale[:, 2:3], w_scale[:, 0:1], ALU.is_lt, ALU.mult).then_inc(s("w_chain"), 1)
            tmp2 = keep.rearrange("p k n -> p (k n)")[:, 0:KC * C]
            ts(tmp2, flat, w_scale[:, 1:2], w_scale[:, 0:1], ALU.is_gt, ALU.mult).then_inc(s("w_chain"), 1)
            dve.wait_ge(s("w_chain"), 5)
            tt(flat, tmp2, tmp, ALU.subtract).then_inc(s("tern_ready"), 1)

            dve.wait_ge(s("x_turned"), 2)
            dve.tensor_copy(xT[:, 0, :], bank[6][:, 0:TOK]).then_inc(s("xT_ready"), 1)
            for t in range(TT):
                dve.wait_ge(s("tern_done"), t + 1)
                tt(h[:, t, :], bank[t][:, 0:C], h[:, t, :], ALU.add).then_inc(s("h_ready"), 1)
            norm_tokens(2, lambda t: h[:, t, :], "h_ready", TT)
            dve.wait_ge(s("x_turned"), 3)
            dve.tensor_copy(xT[:, 0, :], bank[6][:, 0:TOK]).then_inc(s("xT_ready"), 1)
            dve.wait_ge(s("latD_clear"), 1)
            dve.wait_ge(s("lat_done"), 1)
            for p in range(2):
                dve.tensor_copy(latD[p * R:(p + 1) * R, :, p, :],
                                bank[3][p * R:(p + 1) * R, 0:TOK].rearrange("p (i t) -> p i t", t=T))\
                    .then_inc(s("lat_ready"), 1)
            for n in range(4):
                dve.wait_ge(s("lt_done"), 2 * n + 1)
                dve.tensor_copy(ltT[:, :, 2 * n], bank[(2 * n) % 3][:, 0:TOK]).then_inc(s("lt_dve"), 1)
            dve.wait_ge(s("v_done"), 1)
            ts(vT[:, 0, :], bank[4][:, 0:TOK], col("v_b", 0), None, ALU.add).then_inc(s("vT_ready"), 1)
            half_i = IMAGES // 2
            for q in range(2):
                dve.wait_ge(s("att_scored"), q + 1)
                a_v = att[0][:, q * half_i:(q + 1) * half_i, :, :].rearrange("p i a t -> p (i a) t")
                tt(a_v, bank[6 + q][0:NP2 * T, 0:half_i * 2 * T].rearrange("p (n t) -> p n t", t=T),
                   causal.unsqueeze(1).to_broadcast([NP2 * T, half_i * 2, T]), ALU.add).then_inc(s("att_chain"), 1)
            a0 = att[0].rearrange("p i a t -> p (i a) t")
            a1 = att[1].rearrange("p i a t -> p (i a) t")
            bc = lambda v: v.unsqueeze(2).to_broadcast([NP2 * T, IMAGES * 2, T])
            dve.wait_ge(s("att_chain"), 2)
            dve.tensor_reduce(a_stat[:, 0, :], a0, AX.X, ALU.max).then_inc(s("att_chain"), 1)
            dve.wait_ge(s("att_chain"), 3)
            tt(a1, a0, bc(a_stat[:, 0, :]), ALU.subtract).then_inc(s("att_shifted"), 1)
            dve.wait_ge(s("att_exp"), 1)
            dve.tensor_reduce(a_stat[:, 1, :], a1, AX.X, ALU.add).then_inc(s("att_chain"), 1)
            dve.wait_ge(s("att_chain"), 4)
            dve.reciprocal(a_stat[:, 2, :], a_stat[:, 1, :]).then_inc(s("att_chain"), 1)
            dve.wait_ge(s("att_chain"), 5)
            tt(a0, a1, bc(a_stat[:, 2, :]), ALU.mult).then_inc(s("att_probs"), 1)
            dve.wait_ge(s("vT_ready"), 2)
            v4 = vT.rearrange("p k (i t) -> p k i t", t=T)
            y4 = yT.rearrange("p k (i t) -> p k i t", t=T)
            for t in range(T):
                for p in range(2):
                    n = t * 2 + p
                    dve.wait_ge(s("spread_done"), n + 1)
                    if t == 0:
                        tt(y4[:, p, :, 0:1], bank[n % 4][:, 0:IMAGES].unsqueeze(2), v4[:, p, :, 0:1], ALU.mult)\
                            .then_inc(s("y_mul"), 1)
                        dve.wait_ge(s("y_mul"), n + 1)
                        dve.engine_nop().then_inc(s("y_ready"), 1)
                        continue
                    if n > 2:
                        dve.wait_ge(s("y_ready"), n)
                    pr = prod[:, 0:IMAGES * (t + 1)].rearrange("p (i u) -> p i u", u=t + 1)
                    tt(pr, bank[n % 4][:, 0:IMAGES * (t + 1)].rearrange("p (i u) -> p i u", u=t + 1),
                       v4[:, p, :, 0:t + 1], ALU.mult).then_inc(s("y_mul"), 1)
                    dve.wait_ge(s("y_mul"), n + 1)
                    dve.tensor_reduce(y4[:, p, :, t:t + 1], pr, AX.X, ALU.add).then_inc(s("y_ready"), 1)
            dve.wait_ge(s("base_ready"), 2)
            for t in range(TT):
                dve.wait_ge(s("lat_out_done"), t + 1)
                tt(h[:, t, :], bank[t][:, 0:C], base[:, t, :], ALU.add).then_inc(s("h_ready"), 1)
            norm_tokens(3, lambda t: h[:, t, :], "h_ready", 2 * TT)
            dve.wait_ge(s("x_turned"), 4)
            dve.tensor_copy(xT[:, 0, :], bank[6][:, 0:TOK]).then_inc(s("xT_ready"), 1)
            norm_tokens(4, lambda t: xn[:, t, :], dst=xh2)
            dve.wait_ge(s("gate_tanh2"), 1)
            ts(val8, work8[0], 1.0, 0.5, ALU.add, ALU.mult).then_inc(s("top"), 1)
            n_top = 1
            src = val8
            for r in range(CAP // 8):
                dve.wait_ge(s("top"), n_top)
                dve.max(m8[:, r, :], src).then_inc(s("top"), 1)
                dve.wait_ge(s("top"), n_top + 1)
                dst = work8[r % 2]
                dve.match_replace(dst, m8[:, r, :], src, -1.0).then_inc(s("top"), 1)
                n_top += 2
                src = dst
            assert src is work8[1]
            dve.wait_ge(s("top"), n_top)
            ts(work8[0], src, 0.0, None, ALU.is_lt).then_inc(s("top"), 1)
            dve.wait_ge(s("top"), n_top + 1)
            dve.tensor_tensor_scan(work8[1], work8[0], work8[0], 0.0, ALU.add, ALU.max).then_inc(s("top"), 1)
            dve.wait_ge(s("top"), n_top + 2)
            tt(sel8, work8[1], work8[0], ALU.mult).then_inc(s("slots_ready"), 1)
            dve.wait_ge(s("slots_turned"), 1)
            sv_ = bank[4][:, 0:TT * 16].rearrange("p (t a e) -> p t a e", t=TT, a=2)
            dve.tensor_copy(slotT, sv_[:, :, 0, :]).then_inc(s("slotT_ready"), 1)
            dve.tensor_copy(valT, sv_[:, :, 1, :]).then_inc(s("slotT_ready"), 1)
            dve.wait_ge(s("slotT_ready"), 2)
            for t in range(TT):
                tt(pick[:, t, :, :], slotT[:, t, :].unsqueeze(2).to_broadcast([P, E8, CAP]),
                   slots.unsqueeze(1).to_broadcast([P, E8, CAP]), ALU.is_equal).then_inc(s("pick_t"), 1)
            dve.wait_ge(s("pick_t"), TT)
            dve.engine_nop().then_inc(s("pick_ready"), 1)
            for t in range(TT):
                tt(wpick[:, t, :, :], pick[:, t, :, :], valT[:, t, :].unsqueeze(2).to_broadcast([P, E8, CAP]),
                   ALU.mult).then_inc(s("wpick_t"), 1)
            dve.wait_ge(s("wpick_t"), TT)
            dve.engine_nop().then_inc(s("wpick_ready"), 1)
            dve.wait_ge(s("gathered"), 1)
            ts(ysT[:, 0, :], bank[6][:, 0:TOK], col("ln_g", 0), col("ln_b", 0), ALU.mult, ALU.add)\
                .then_inc(s("ysT_ready"), 1)
            for q in range(E8 // 2):
                dve.wait_ge(s("wpick_turned"), q + 1)
                dve.tensor_copy(wpickT[:, q, :], bank[5][0:2 * CAP, 0:TOK]).then_inc(s("wpickT_ready"), 1)

            def hidden(e):
                dve.wait_ge(s("hid_done"), e + 1)
                if e >= 2:
                    dve.wait_ge(s("ha_ready"), e - 1)
                tt(hb[e % 2], bank[e % 2][:, 0:FC * CAP].rearrange("p (f c) -> p f c", f=FC),
                   col("b1", e * FC, FC).unsqueeze(2).to_broadcast([P, FC, CAP]), ALU.add).then_inc(s("hb_ready"), 1)

            def out_e(e):
                q, side = divmod(e, 2)
                dve.wait_ge(s("eo_done"), e + 1)
                if e >= 4:
                    dve.wait_ge(s("opair_turned"), q - 1)
                tt(oT[q % 2][:, :, side, :], bank[2 + e % 2][:, 0:KC * CAP].rearrange("p (k c) -> p k c", k=KC),
                   col("b2", e * KC, KC).unsqueeze(2).to_broadcast([P, KC, CAP]), ALU.add).then_inc(s("oT_ready"), 1)

            def pair(q):
                dve.wait_ge(s("opair_turned"), q + 1)
                if q >= 2:
                    dve.wait_ge(s("combined"), q - 1)
                dve.tensor_copy(opair[q % 2][:, :], bank[4][0:2 * CAP, 0:C]).then_inc(s("opair_ready"), 1)

            for e in range(E8 + 1):
                if e < E8:
                    hidden(e)
                if e >= 1:
                    out_e(e - 1)
                if e >= 2 and e % 2 == 1:
                    pair((e - 3) // 2)
            pair(E8 // 2 - 1)
            for t in range(TT):
                if t == 0:
                    dve.wait_ge(s("base_ready"), 3)
                dve.wait_ge(s("combined"), E8 // 2 - 1 + t + 1)
                tt(base[:, t, :], bank[5 + t][:, 0:C], base[:, t, :], ALU.add).then_inc(s("out_ready"), 1)

        @block.scalar
        def _(act):
            ac = act.activation

            def copy_pe(t, j):
                act.wait_ge(s("conv_done"), t + 1)
                if not (isinstance(t, int) and t < RING):
                    act.wait_ge(s("xhat_ready"), t - (RING - 1))
                    act.wait_ge(s("pool_done"), t - (RING - 1))
                ac(pe_sb[j][0:TP], conv_bank[j][0:TP, 0:C], ACT.Copy).then_inc(s("pe_copied"), 1)

            def affine(t, j):
                act.wait_ge(s("turned"), t + 1)
                for k in range(KC):
                    i = ac(winT[:, k, bass.ds(t * TP, TP)], tr_bank[j][:, k * P:k * P + TP], ACT.Identity,
                           bias=col("kv_b", k), scale=col("kv_g", k))
                i.then_inc(s("winT_ready"), 1)

            copy_pe(0, 0)
            act.wait_ge(s("x_in2"), 16)
            act.dma_start(layw[:, :], layw_d).then_inc(s("layw_in"), 16)
            for e in range(NRES):
                act.dma_start(expert(e), exp_d[e]).then_inc(s(f"expert_in{e}"), 16)
            act.wait_ge(s("cols_in"), 16)
            for t in range(1, HEAD):
                copy_pe(t, t % RING)
                if t >= RING:
                    affine(t - RING, t % RING)
            with act.Fori(HEAD // RING, TILES // RING) as r:
                for j in range(RING):
                    copy_pe(RING * r + j, j)
                    affine(RING * r + (j - RING), j)
            for t in range(TAIL, TILES):
                copy_pe(t, t % RING)
                affine(t - RING, t % RING)
            affine(TILES - 3, (TILES - 3) % RING)
            affine(TILES - 2, (TILES - 2) % RING)
            act.wait_ge(s("pool_done"), TILES)
            ac(redT[:, 1, :], red_bank[1][:, 0:WINDOWS], ACT.Copy).then_inc(s("redT_ready"), 1)
            affine(TILES - 1, (TILES - 1) % RING)
            act.wait_ge(s("redx_turned"), 1)
            ac(lnrT[:, 1, :], bank[2][:, 0:C], ACT.Identity, bias=col("q_b", 1), scale=col("q_g", 1))\
                .then_inc(s("lnrT_ready"), 1)
            for n in range(4):
                m, g = divmod(2 * n + 1, 4)
                act.wait_ge(s("qk_done"), 2 * n + 2)
                ac(qkT[:, :, :, 4 * m + g], bank[4 + g][:, :].rearrange("p (k w) -> p k w", k=KC), ACT.Copy)\
                    .then_inc(s("qk_act"), 1)

            def n_win(t):
                return WT if t < TILES - 1 else LASTW

            def expo(t):
                n, j = n_win(t), t % 2
                rows, wide = H8 * n, n * NWIN
                act.wait_ge(s("nmx_ready"), t + 1)
                if t >= 2:
                    act.wait_ge(s("att_ready"), t - 1)
                ac(s_exp[j][0:rows, 0:wide], s_msk[j][0:rows, 0:wide], ACT.Exp, bias=s_nmx[j][0:rows],
                   scale=C ** -0.5, accum_out=s_sum[j][0:rows]).then_inc(s("s_exp_ready"), 1)

            def ctx1(t):
                n, j = n_win(t), t % 2
                act.wait_ge(s("attended"), t + 1)
                ac(ctxT[:, 1, t * WT:t * WT + n, :],
                   bank[6 + j][:, 0:H8 * n].rearrange("p (w h) -> p w h", h=H8), ACT.Identity,
                   bias=col("kv_b", 1), scale=col("kv_g", 1)).then_inc(s("ctx_act"), 1)

            for t in range(TILES + 2):
                if t < TILES:
                    expo(t)
                if t >= 2:
                    ctx1(t - 2)

            act.wait_ge(s("mod_done"), 1)
            for m in range(KC):
                ac(h0T[:, m, :, 1:1 + HW], bank[3][:, m * C:(m + 1) * C].rearrange("p (i w) -> p i w", w=HW),
                   ACT.Identity, bias=col("mod_b", m)).then_inc(s("h0T_ready"), 1)
            act.wait_ge(s("lox_turned"), 1)
            ac(lnlT[:, 1, :], bank[5][:, 0:C], ACT.Identity, bias=col("gkv_b", 1), scale=col("gkv_g", 1))\
                .then_inc(s("lnlT_ready"), 1)
            act.wait_ge(s("gv_done"), 1)
            ac(gvT.rearrange("p k w -> p (k w)"), bank[6][:, :], ACT.Copy).then_inc(s("gvT_ready"), 1)
            act.wait_ge(s("g_shifted"), 1)
            ac(gattn[:, 1, :], gattn[:, 0, :], ACT.Exp, scale=C ** -0.5).then_inc(s("g_exp"), 1)

            for t in range(TT):
                act.wait_ge(s("h0_major"), t + 1)
                ac(h[:, t, :], bank[2 + t][:, 0:C], ACT.Copy).then_inc(s("h0_ready"), 1)

            def xT_copy(n):
                act.wait_ge(s("x_turned"), n + 1)
                ac(xT[:, 1, :], bank[7][:, 0:TOK], ACT.Copy).then_inc(s("xT_ready"), 1)

            xT_copy(0)
            act.wait_ge(s("bhalf_ready"), 1)
            for m in range(KC):
                act.wait_ge(s("gv_in_done"), m + 1)
                ac(gate_t[:, m, :], bank[m][:, 0:TOK], ACT.Tanh, bias=b_in_half[:, m:m + 1], scale=0.5)\
                    .then_inc(s("gate_tanh"), 1)
            for m in range(KC):
                act.wait_ge(s("sv_done"), m + 1)
                ac(sv[:, m, :], bank[4 + m][:, 0:TOK], ACT.Tanh, bias=col("b_s", m)).then_inc(s("sv_tanh"), 1)
            xT_copy(1)
            xT_copy(2)
            for n in range(4):
                act.wait_ge(s("lt_done"), 2 * n + 2)
                ac(ltT[:, :, 2 * n + 1], bank[(2 * n + 1) % 3][:, 0:TOK], ACT.Copy).then_inc(s("lt_act"), 1)
            act.wait_ge(s("v_done"), 2)
            ac(vT[:, 1, :], bank[5][:, 0:TOK], ACT.Identity, bias=col("v_b", 1)).then_inc(s("vT_ready"), 1)
            act.wait_ge(s("att_shifted"), 1)
            a1 = att[1].rearrange("p i a t -> p (i a t)")
            ac(a1, a1, ACT.Exp, scale=R ** -0.5).then_inc(s("att_exp"), 1)
            xT_copy(3)
            act.wait_ge(s("gate_done"), 1)
            ac(work8[0], bank[3][0:E8, 0:TOK], ACT.Tanh).then_inc(s("gate_tanh2"), 1)
            act.wait_ge(s("gathered"), 1)
            ac(ysT[:, 1, :], bank[7][:, 0:TOK], ACT.Identity, bias=col("ln_b", 1), scale=col("ln_g", 1))\
                .then_inc(s("ysT_ready"), 1)
            for e in range(E8):
                act.wait_ge(s("hb_ready"), e + 1)
                if e >= 2:
                    act.wait_ge(s("eo_done"), e - 1)
                ac(ha[e % 2][:, :, :], hb[e % 2], ACT.Gelu_apprx_tanh).then_inc(s("ha_ready"), 1)

        @block.gpsimd
        def _(pool):
            pool.memset(half, -0.5).then_inc(s("half_set"), 1)
            pool.memset(eps, EPS).then_inc(s("half_set"), 1)
            pool.wait_ge(s("half_set"), 2)

            def rsqrt(ve, var, rs, name, parts=P):
                n = 1 + rsqrt.n
                rsqrt.n = n
                pool.tensor_scalar(ve, var, EPS, None, ALU.add).then_inc(s("eps_added"), 1)
                pool.wait_ge(s("eps_added"), n)
                pool.tensor_tensor(rs, ve, half[0:parts, 0:rs.shape[1]], ALU.pow).then_inc(s(name), 1)

            def rs_tile(t, j):
                pool.wait_ge(s("mv_ready"), t + 1)
                if not (isinstance(t, int) and t < RING):
                    pool.wait_ge(s("xhat_ready"), t - (RING - 1))
                pool.tensor_tensor(a_ve[j][0:TP], a_mv[j][0:TP, 1:2], eps[0:TP], ALU.add).then_inc(s("a_eps"), 1)
                pool.wait_ge(s("a_eps"), t + 1)
                pool.tensor_tensor(a_rs[j][0:TP], a_ve[j][0:TP], half[0:TP, 0:1], ALU.pow).then_inc(s("rs_ready"), 1)

            def keep_xhat(t, j):
                pool.wait_ge(s("xhat_ready"), t + 1)
                pool.tensor_copy(xhat_all[0:TP, t, :], xhat[j][0:TP]).then_inc(s("xall_done"), 1)

            for t in range(HEAD):
                rs_tile(t, t % RING)
                if t:
                    keep_xhat(t - 1, (t - 1) % RING)
            with pool.Fori(HEAD // RING, TILES // RING) as r:
                for j in range(RING):
                    rs_tile(RING * r + j, j)
                    keep_xhat(RING * r + (j - 1), (j - 1) % RING)
            for t in range(TAIL, TILES):
                rs_tile(t, t % RING)
                keep_xhat(t - 1, (t - 1) % RING)
            keep_xhat(TILES - 1, (TILES - 1) % RING)

            rsqrt.n = 0
            pool.wait_ge(s("w_mv_ready"), 2)
            rsqrt(w_ve, w_mv[:, :, 1], w_rs, "w_rs_ready")
            pool.wait_ge(s("cols_in"), 16)
            for k in range(KC):
                pool.tensor_copy(h0T[:, k, :, 0], col("cls_tok", k).to_broadcast([P, IMAGES]))\
                    .then_inc(s("h0T_ready"), 1)
            pool.tensor_scalar(b_in_half, col("b_in", 0, KC), 0.5, None, ALU.mult).then_inc(s("bhalf_ready"), 1)
            pool.wait_ge(s("layw_in"), 16)
            core = w_of(layw, LAYW, "core", parts=R)
            coreT = w_of(layw, LAYW, "coreT", parts=R)
            nh = 0

            def hstep(i):
                nonlocal nh
                nh += 1
                i.then_inc(s("head_steps"), 1)
                pool.wait_ge(s("head_steps"), nh)

            hstep(pool.tensor_tensor(core, core, coreT, ALU.add))
            hstep(pool.tensor_scalar(core, core, 0.5 / NH, None, ALU.mult))
            hstep(pool.tensor_tensor(coreT, heads[:, 0, :], heads[:, 1, :], ALU.add))
            for n in range(2, NH):
                hstep(pool.tensor_tensor(coreT, coreT, heads[:, n, :], ALU.add))
            hstep(pool.tensor_scalar(coreT, coreT, 1.0 / NH, None, ALU.mult))
            hstep(pool.tensor_tensor(heads, heads, coreT.unsqueeze(1).to_broadcast([R, NH, R]), ALU.subtract))
            pool.tensor_tensor(heads, heads, core.unsqueeze(1).to_broadcast([R, NH, R]), ALU.add)\
                .then_inc(s("heads_ready"), 1)

            pool.wait_ge(s("c_mv_ready"), 1)
            rsqrt(c_ve[0:1], c_mv[0:1, 1:2], c_rs[0:1], "c_rs_ready", parts=1)
            pool.wait_ge(s("l_mv_ready"), 2)
            rsqrt(l_ve, l_mv[:, :, 1], l_rs, "l_rs_ready")

            def rs_tokens(n):
                pool.wait_ge(s("t_mv_ready"), TT * (n + 1))
                rsqrt(t_ve, t_mv[:, :, 1], t_rs, "t_rs_ready")

            bo = w_of(layw, LAYW, "bo_row").unsqueeze(1).to_broadcast([P, TT, C])
            ob = w_of(layw, LAYW, "ob_row").unsqueeze(1).to_broadcast([P, TT, C])
            rs_tokens(0)
            pool.wait_ge(s("h0_ready"), TT)
            pool.wait_ge(s("xn_ready"), TT)
            pool.tensor_tensor(base, h, xn, ALU.add).then_inc(s("base_step"), 1)
            pool.wait_ge(s("base_step"), 1)
            pool.tensor_tensor(base, base, bo, ALU.add).then_inc(s("base_ready"), 1)
            rs_tokens(1)
            rs_tokens(2)
            pool.wait_ge(s("tern_ready"), 1)
            pool.memset(latD, 0.0).then_inc(s("latD_clear"), 1)
            pool.wait_ge(s("h_ready"), 2 * TT)
            pool.tensor_tensor(base, h, ob, ALU.add).then_inc(s("base_ready"), 1)
            rs_tokens(3)
            pool.wait_ge(s("xn_ready"), 4 * TT)
            pool.wait_ge(s("h_ready"), 3 * TT)
            rs_tokens(4)
            pool.tensor_tensor(base, h, xn, ALU.add).then_inc(s("base_ready"), 1)


def chunked(w):
    w = np.asarray(w)
    return w.reshape(KC, P, -1).transpose(1, 0, 2).reshape(P, -1)


def packed(table, total, parts):
    out = np.zeros((P, total), np.float32)
    for name, a in parts.items():
        at, n = table[name]
        out[:a.shape[0], at:at + n] = a.reshape(a.shape[0], n)
    return out


def constants():
    rows = np.arange(H8 * WT)[:, None] // H8
    mask = np.where(np.arange(TP)[None] // NWIN == rows, 0.0, NEG)
    rows = np.arange(H8 * LASTW)[:, None] // H8
    mask_last = np.where(np.arange(LASTW * NWIN)[None] // NWIN == rows, 0.0, NEG)
    jt = np.arange(NP2 * T)
    causal = np.where(np.arange(T)[None] > (jt // NP2)[:, None], NEG, 0.0)
    chan = np.arange(P)
    spread = (jt[:, None, None] == np.arange(T)[None, :, None] * NP2 + chan[None, None] // HD)
    heads8 = np.arange(H8)[:, None, None] == (np.arange(KC)[:, None] * P + chan[None])[None] // DH
    headcol = (np.arange(KC)[None, :, None] * P + chan[:, None, None]) // DH == np.arange(H8)[None, None]
    f = lambda a: np.asarray(a, np.float32)
    return packed(CONS, CONS_N, {
        "ident": f(np.eye(P)), "pool": f((np.arange(TP)[:, None] // NWIN == np.arange(WT)[None]) / NWIN),
        "mask": f(mask), "mask_last": f(mask_last), "causal": f(causal),
        "slots": f(np.tile(np.arange(1, CAP + 1), (P, 1))), "spread": f(spread), "heads8": f(heads8),
        "headcol": f(headcol), "mean": f(np.full((P, P), 1.0 / (C * C)))})


def kernel(**inputs):
    import concourse.bacc as _bacc
    from concourse.bass_utils import run_bass_kernel_spmd as _run

    g = {k: np.asarray(v) for k, v in inputs.items()}
    x = g["x"].reshape(IMAGES, 3, 2, CS, PATCH, 2, CS, PATCH)
    x = x.transpose(1, 4, 7, 0, 2, 5, 3, 6).reshape(PIX, WINDOWS * NWIN)
    full = np.zeros((KX * KP, TILES * TP), np.float32)
    full[:PIX, :WINDOWS * NWIN] = x
    xs = np.ascontiguousarray(full.reshape(KX, KP, TILES, TP).transpose(2, 1, 0, 3))
    cw = np.zeros((KX * KP, C), np.float32)
    cw[:PIX] = g["L0_tok_conv_w"].reshape(C, PIX).T
    cw = np.pad(cw.reshape(KX, KP, C).transpose(1, 0, 2).reshape(KP, KX * C), ((0, P - KP), (0, 0)))

    t = lambda n: g["L0_tok_" + n]
    tokw = packed(TOKW, TOKW_N, {
        "wq": chunked(t("la_wq")), "wkT": chunked(t("la_wkv")[:, :C].T), "wv": chunked(t("la_wkv")[:, C:]),
        "proj": chunked(t("la_proj_w")), "mod": chunked(t("mod_w")), "gwq": chunked(t("ga_wq")),
        "gwkT": chunked(t("ga_wkv")[:, :C].T), "gwv": chunked(t("ga_wkv")[:, C:]),
        "gproj": chunked(t("ga_proj_w"))})
    perm = np.arange(C).reshape(NP2, 2, HD).transpose(1, 0, 2).reshape(-1)
    basis = g["L1_attn_basis_w"].T
    layw = packed(LAYW, LAYW_N, {
        "w_in": chunked(g["L0_attn_W_in"].T), "w_s": chunked(g["L0_attn_W_s"].T),
        "w_o": chunked(g["L0_attn_W_o"].T), "tern": chunked(g["L0_ffn_weight"].T),
        "basis": chunked(np.concatenate([basis, basis], 1)), "v_w": chunked(g["L1_attn_v_w"].T[:, perm]),
        "o_w": chunked(g["L1_attn_o_w"].T[perm]), "gate": chunked(g["L1_ffn_gate_w"].T),
        "heads": g["L1_attn_head_residual"].transpose(1, 0, 2), "core": g["L1_attn_core"],
        "coreT": g["L1_attn_core"].T, "bo_row": np.tile(g["L0_attn_b_o"], (P, 1)),
        "ob_row": np.tile(g["L1_attn_o_b"], (P, 1))})
    cols = packed(COLS, COLS_N, {
        "q_g": chunked(t("la_ln_q_g")), "q_b": chunked(t("la_ln_q_b")), "kv_g": chunked(t("la_ln_kv_g")),
        "kv_b": chunked(t("la_ln_kv_b")), "proj_b": chunked(t("la_proj_b")), "mod_b": chunked(t("mod_b")),
        "gq_g": chunked(t("ga_ln_q_g")), "gq_b": chunked(t("ga_ln_q_b")), "gkv_g": chunked(t("ga_ln_kv_g")),
        "gkv_b": chunked(t("ga_ln_kv_b")), "gproj_b": chunked(t("ga_proj_b")),
        "class_emb": chunked(t("class_emb")), "cls_tok": chunked(g["cls_tok"].reshape(C)),
        "b_s": chunked(g["L0_attn_b_s"]), "v_b": chunked(g["L1_attn_v_b"][perm]),
        "ln_g": chunked(g["L1_ffn_ln_gamma"]), "ln_b": chunked(g["L1_ffn_ln_beta"]),
        "b_in": g["L0_attn_b_in"].reshape(2 * KC, P).T, "b1": g["L1_ffn_b1s"].reshape(E8 * FC, P).T,
        "b2": g["L1_ffn_b2s"].reshape(E8 * KC, P).T, "class_row": np.tile(t("class_emb"), (P, 1))})
    w1 = g["L1_ffn_fc1s"].reshape(E8, FF, KC, P).transpose(0, 3, 2, 1).reshape(E8, P, KC * FF)
    w2 = g["L1_ffn_fc2s"].reshape(E8, C, FC, P).transpose(0, 3, 2, 1).reshape(E8, P, FC * C)
    experts = np.ascontiguousarray(np.concatenate([w1, w2], 2))

    nc = _bacc.Bacc("TRN2", target_bir_lowering=False, num_devices=1)
    arrays = {"patches": xs, "conv_w": cw, "columns": cols, "constants": constants(),
              "tokenizer_w": tokw, "layer_w": layw, "experts": experts}
    args = [nc.dram_tensor(n, a.shape, F32, kind="ExternalInput").ap() for n, a in arrays.items()]
    o = nc.dram_tensor("tokens", (TOK, C), F32, kind="ExternalOutput").ap()
    build(nc, *args, o)
    r = _run(nc, [arrays], core_ids=[0])
    return r.results[0]["tokens"].reshape(IMAGES, T, C)
```

```python
from contextlib import ExitStack

import numpy as np

import concourse.bass as bass
from concourse import mybir

F32 = mybir.dt.float32
ALU = mybir.AluOpType
ACT = mybir.ActivationFunctionType
AX = mybir.AxisListType

P = 128
C = 256
KC = C // P
IMAGES, PATCH, SIDE, CS = 64, 14, 6, 3
HW = (SIDE // CS) ** 2
NWIN = CS * CS
WINDOWS = IMAGES * HW
PIX = 3 * PATCH * PATCH
KX, KP = 5, 118
WT = 14
TP = WT * NWIN
TILES = -(-WINDOWS // WT)
LASTW = WINDOWS - WT * (TILES - 1)
RING = 3
HEAD, TAIL = 2 * RING, TILES // RING * RING
H8, DH = 8, 32
T = HW + 2
TOK = IMAGES * T
G = 2
GT, GI = TOK // G, IMAGES // G
TR = 96
TG = GT // TR
TT = TOK // TR
SW = 64
NH, HD, R = 16, 16, 64
NP2 = NH // 2
E8, FF, FC = 8, 1024, 8
CAP = TOK // E8
EPS = 1e-5
GELU_C, GELU_A = 0.7978845608028654, 0.044715
NEG = -1.0e30


STEPS = -(-TILES // 2)


def tiles_of(q):
    return [(t, WT if t < TILES - 1 else LASTW, t % 2) for t in range(2 * q, min(2 * q + 2, TILES))]


def steps_until(q):
    return min(2 * q, TILES)


def offsets(sizes):
    at, out = 0, {}
    for name, n in sizes:
        out[name] = (at, n)
        at += n
    return out, at


TOKW, TOKW_N = offsets([(n, KC * C) for n in (
    "wq", "wkT", "wv", "proj", "mod", "gwq", "gwkT", "gwv", "gproj")])
LAYW, LAYW_N = offsets([("w_in", KC * 2 * C), ("w_s", KC * C), ("w_o", KC * C), ("tern", KC * C),
                        ("basis", KC * 2 * R), ("v_w", KC * C), ("o_w", KC * C), ("gate", KC * E8),
                        ("heads", NH * R), ("core", R), ("coreT", R), ("bo_row", C), ("ob_row", C)])
assert LAYW_N % 5 == 0
COLS, COLS_N = offsets([(n, KC) for n in (
    "q_g", "q_b", "kv_g", "kv_b", "proj_b", "mod_b", "gq_g", "gq_b", "gkv_g", "gkv_b", "gproj_b",
    "class_emb", "cls_tok", "b_s", "v_b", "ln_g", "ln_b")] + [("b_in", 2 * KC), ("class_row", C)])
NRES, NATT = 3, 3
PIECES = 2 * NRES
CONS, CONS_N = offsets([("ident", P), ("pool", WT), ("mask", TP), ("mask_last", LASTW * NWIN),
                        ("causal", T), ("slots", SW), ("spread", T * P), ("heads8", KC * P),
                        ("headcol", KC * H8), ("mean", P)])
CONS_NOW = P + WT


def build(nc, x_d, convw_d, cols_d, cons_d, tokw_d, layw_d, exp_d, b1_d, b2_d, out):
    ctx = ExitStack()
    with ctx:
        def sb(name, shape):
            return ctx.enter_context(nc.sbuf_tensor(name, shape, F32))

        def sem(name):
            return ctx.enter_context(nc.semaphore(name))

        bank = [ctx.enter_context(nc.psum_tensor(f"bank{i}", [P, 512], F32)) for i in range(8)]

        cols = sb("cols", [P, COLS_N])
        cons = sb("cons", [P, CONS_N])
        layw = sb("layw", [P, LAYW_N])
        resident = sb("resident_experts", [P, PIECES * KC * FF])
        attic = sb("attic", [P, TILES * C + KC * TILES * TP + KC * H8 * WINDOWS + RING * KX * TP])
        desk = sb("desk", [P, 12700])

        def carve(tensor, at, *shape, parts=P):
            n = int(np.prod(shape))
            v = tensor[0:parts, at:at + n]
            names = "abcd"[:len(shape)]
            if len(shape) > 1:
                v = v.rearrange(f"p ({' '.join(names)}) -> p {' '.join(names)}",
                                **{k: s for k, s in zip(names, shape)})
            return v

        o = 0
        xhat_all = carve(attic, o, TILES, C); o += TILES * C
        winT = carve(attic, o, KC, TILES * TP); o += KC * TILES * TP
        qkT = carve(attic, o, KC, WINDOWS, H8)
        ctxT = qkT; o += KC * H8 * WINDOWS
        xt = [carve(attic, o + j * KX * TP, KX, TP) for j in range(RING)]; o += RING * KX * TP
        assert o <= attic.shape[1]

        o = 0
        tokw = desk[:, 0:TOKW_N]; o += TOKW_N
        convw = carve(desk, o, KX, C); o += KX * C
        pe_sb = [carve(desk, o + j * C, C) for j in range(RING)]; o += RING * C
        xhat = [carve(desk, o + j * C, C) for j in range(RING)]; o += RING * C
        redT = carve(desk, o, KC, WINDOWS); o += KC * WINDOWS
        redx = carve(desk, o, KC, C); o += KC * C
        lnrT = carve(desk, o, KC, WINDOWS); o += KC * WINDOWS
        qbd = carve(desk, o, KC, 4, WINDOWS)
        s_msk = [carve(desk, o + j * 2 * TP, 2, TP) for j in range(RING)]; o += 2 * RING * TP
        s_exp = [carve(desk, o + j * 2 * TP, 2, TP) for j in range(RING)]; o += 2 * RING * TP
        s_att = [carve(desk, o + j * 2 * TP, 2, TP) for j in range(RING)]; o += 2 * RING * TP
        s_attT = [carve(desk, o + j * 2 * P, 2, P) for j in range(RING)]; o += 2 * RING * P
        assert o <= desk.shape[1], o
        o = TOKW_N
        aggT = carve(desk, o, KC, WINDOWS); o += KC * WINDOWS
        localT = carve(desk, o, KC, WINDOWS); o += KC * WINDOWS
        lox = carve(desk, o, KC, C); o += KC * C
        lnlT = carve(desk, o, KC, WINDOWS); o += KC * WINDOWS
        assert o <= TOKW_N + KX * C + 2 * RING * C
        gvT = redx
        gprod = lnrT
        h0T = sb("h0T", [P, KC, IMAGES, T])
        gattn = sb("gattn", [H8, 3, WINDOWS])
        small = sb("small", [P, 900])
        zeros = sb("zeros", [P, C])
        small_row = sb("class_row_ln", [1, C])
        so = [0]

        def tiny(*shape, parts=P):
            v = carve(small, so[0], *shape, parts=parts)
            so[0] += int(np.prod(shape))
            return v

        a_st, a_mv, a_ve, a_rs = ([tiny(n) for _ in range(RING)] for n in (6, 2, 1, 1))
        half, eps = tiny(8), tiny(1)
        w_st, w_mv, w_ve, w_rs = tiny(2, 6), tiny(2, 2), tiny(2), tiny(2)
        l_st, l_mv, l_ve, l_rs = tiny(2, 6), tiny(2, 2), tiny(2), tiny(2)
        c_st, c_mv, c_ve, c_rs = tiny(6), tiny(2), tiny(1), tiny(1)
        c_lnT, c_q, c_qbd, c_qk = tiny(KC), tiny(KC), tiny(KC, H8), tiny(KC, H8)
        s_mx, s_nmx, s_sum, s_rec = ([tiny(2) for _ in range(RING)] for _ in range(4))
        g_mx, g_sum, g_rec = (tiny(IMAGES, parts=H8) for _ in range(3))
        gaggT = tiny(KC, IMAGES)
        t_st, t_mv, t_ve, t_rs = tiny(TT, 6), tiny(TT, 2), tiny(TT), tiny(TT)
        w_abs, w_scale = tiny(1), tiny(3)
        m8 = tiny(6, 8, parts=E8)
        slotT, valT = tiny(TT, E8), tiny(TT, E8)
        b_in_half, cls_fix = tiny(KC), tiny(KC)

        o = 0
        h = carve(desk, o, TT, C); o += TT * C
        xn = carve(desk, o, TT, C); o += TT * C
        base = carve(desk, o, TT, C); o += TT * C
        xT = carve(desk, o, G, KC, GT); o += KC * TOK
        U = o
        gate_t, keep, val, sv, gate_v, scanT = (carve(desk, U + i * KC * TOK, G, KC, GT) for i in range(6))
        tern_tmp = [carve(desk, U + 6 * KC * TOK + i * KC * C, KC * C) for i in range(2)]
        latD = carve(desk, o, IMAGES, 2, T); o += 2 * TOK
        latT = latD[0:R, :, 0, :]
        ltT = carve(desk, o, TOK, NP2); o += NP2 * TOK
        att = [carve(desk, o + i * 2 * TOK, IMAGES, 2, T, parts=NP2 * T) for i in range(2)]; o += 4 * TOK
        vT = carve(desk, o, G, KC, GT); o += KC * TOK
        yT = carve(desk, o, G, KC, GT); o += KC * TOK
        prod = [carve(desk, o + i * KC * GT, KC * GT) for i in range(2)]; o += 2 * KC * GT
        a_stat = carve(desk, o, 3, IMAGES * 2, parts=NP2 * T); o += 6 * IMAGES
        assert o <= desk.shape[1], o
        o = U
        val8 = carve(desk, o, TOK, parts=E8); o += TOK
        work8 = [carve(desk, o + i * TOK, TOK, parts=E8) for i in range(2)]; o += 2 * TOK
        sel8 = work8[1]
        ow = U
        opair = [carve(desk, ow + i * C, C) for i in range(2)]
        pick = carve(desk, o, TT, E8, SW)
        hid = [carve(desk, o + i * FF, FF) for i in range(2)]
        o += TT * E8 * SW
        wpick = carve(desk, o, TT, E8, SW)
        hidT = [carve(desk, o + i * FF, FC, P) for i in range(2)]
        o += TT * E8 * SW
        wpickT = carve(desk, o, E8 // 2, TOK); o += E8 // 2 * TOK
        xh2 = carve(desk, o, TT, C); o += TT * C
        ysT = carve(desk, o, KC, E8, SW); o += KC * E8 * SW
        assert o <= desk.shape[1], o
        o = NATT * 2 * KC * FF
        b1_rows = carve(attic, o, 2, FF); o += 2 * FF
        b2_rows = carve(attic, o, E8 // 2, C); o += E8 // 2 * C
        assert o <= attic.shape[1], o

        def expert_half(e, part):
            n = KC * FF
            if NRES <= e < NRES + NATT:
                at = (2 * (e - NRES) + part) * n
                return attic[:, at:at + n]
            at = (2 * (e if e < NRES else e - NRES - NATT) + part) * n
            return resident[:, at:at + n]

        def w_of(pack, table, name, *shape, parts=P):
            a, n = table[name]
            v = pack[0:parts, a:a + n]
            if shape:
                names = "abcd"[:len(shape)]
                v = v.rearrange(f"p ({' '.join(names)}) -> p {' '.join(names)}",
                                **{k: s for k, s in zip(names, shape)})
            return v

        def col(name, k=0, n=1, parts=P):
            a = COLS[name][0]
            return cols[0:parts, a + k:a + k + n]

        tw = {n: w_of(tokw, TOKW, n, KC, C) for n in TOKW}
        lw = {n: w_of(layw, LAYW, n, KC, s) for n, s in (
            ("w_in", 2 * C), ("w_s", C), ("w_o", C), ("tern", C), ("basis", 2 * R), ("v_w", C),
            ("o_w", C), ("gate", E8))}
        heads = w_of(layw, LAYW, "heads", NH, R, parts=R)
        ident = w_of(cons, CONS, "ident")
        pool_m = w_of(cons, CONS, "pool", parts=TP)
        mask = w_of(cons, CONS, "mask", parts=H8 * WT)
        mask_last = w_of(cons, CONS, "mask_last", parts=H8 * LASTW)
        causal = w_of(cons, CONS, "causal", parts=NP2 * T)
        slots = w_of(cons, CONS, "slots")
        spread = w_of(cons, CONS, "spread", T, P, parts=NP2 * T)
        heads8 = w_of(cons, CONS, "heads8", KC, P, parts=H8)
        headcol = w_of(cons, CONS, "headcol", KC, H8)
        mean_m = w_of(cons, CONS, "mean")

        S = {}

        def s(name):
            if name not in S:
                S[name] = sem(name)
            return S[name]

        conv_bank = bank[0:3]
        red_bank = bank[3:5]
        tr_bank = bank[5:8]

        block = ctx.enter_context(nc.Block())

        @block.sync
        def _(sp):
            def load_x(t, j, steady=True):
                if steady:
                    sp.wait_ge(s("conv_done"), t - (RING - 1))
                sp.dma_start(xt[j][0:KP], x_d[t]).then_inc(s(f"x_in{j}"), 16)

            load_x(0, 0, False)
            for k in range(KX):
                sp.dma_start(convw[:, k, :], convw_d[:, k * C:(k + 1) * C]).then_inc(s("convw_in"), 16)
            sp.dma_start(cons[:, 0:CONS_NOW], cons_d[:, 0:CONS_NOW]).then_inc(s("cons_in"), 16)
            load_x(1, 1, False)
            sp.dma_start(cols[:, :], cols_d).then_inc(s("cols_in"), 16)
            load_x(2, 2, False)
            third = TOKW_N // 3
            for t in range(RING, 2 * RING):
                load_x(t, t % RING)
                i = t - RING
                sp.dma_start(tokw[:, i * third:(i + 1) * third], tokw_d[:, i * third:(i + 1) * third])\
                  .then_inc(s("tokw_in"), 16)
            rounds = TILES // RING - 2
            lay = LAYW_N // (rounds + 1)
            with sp.Fori(2, TILES // RING) as r:
                for j in range(RING):
                    load_x(RING * r + j, j)
                    if j == 0:
                        sp.dma_start(layw[:, bass.ds((r - 2) * lay, lay)], layw_d[:, bass.ds((r - 2) * lay, lay)])\
                          .then_inc(s("layw_in"), 16)
                    if j == 1:
                        sp.dma_start(resident[:, bass.ds((r - 2) * KC * FF, KC * FF)], exp_d[r - 2])\
                          .then_inc(s("resident_in"), 16)
            for t in range(TAIL, TILES):
                load_x(t, t % RING)
            sp.dma_start(layw[:, rounds * lay:], layw_d[:, rounds * lay:]).then_inc(s("layw_in"), 16)
            sp.dma_start(cons[:, CONS_NOW:], cons_d[:, CONS_NOW:]).then_inc(s("cons_in"), 16)
            for i in range(rounds, PIECES):
                sp.dma_start(resident[:, i * KC * FF:(i + 1) * KC * FF], exp_d[i]).then_inc(s("resident_in"), 16)
            sp.wait_ge(s("agg_done"), 1)
            for q in range(E8 // 2):
                for side in range(2):
                    e = 2 * q + side
                    rows = slice(side * SW, (side + 1) * SW)
                    sp.dma_start(b2_rows[rows, q, :], b2_d[e:e + 1, :].to_broadcast([SW, C]))\
                      .then_inc(s("b2_in"), 16)
                    if q < 2:
                        sp.dma_start(b1_rows[rows, q, :], b1_d[e:e + 1, :].to_broadcast([SW, FF]))\
                          .then_inc(s(f"b1_in{q}"), 16)

            def load_b1(q):
                sp.wait_ge(s("hid_biased"), 2 * (q - 1))
                for side in range(2):
                    e = 2 * q + side
                    sp.dma_start(b1_rows[side * SW:(side + 1) * SW, q - 2, :], b1_d[e:e + 1, :].to_broadcast([SW, FF]))\
                      .then_inc(s(f"b1_in{q % 2}"), 16)

            def load_half(e, part, loaded):
                sp.dma_start(expert_half(e, part), exp_d[2 * e + part]).then_inc(s(loaded), 16)

            for e in range(NRES, NRES + NATT):
                for part in range(2):
                    load_half(e, part, f"expert_in{e}")
            load_b1(2)
            for part in range(2):
                sp.wait_ge(s(("hid_done", "eo_done")[part]), 2 - part)
                for e in range(NRES + NATT, E8):
                    load_half(e, part, f"last_w{part + 1}_in")
            load_b1(3)
            for g in range(G):
                sp.wait_ge(s("out_ready"), g + 1)
                sp.dma_start(out.rearrange("(t p) c -> p t c", p=TR)[:, g * TG:(g + 1) * TG, :],
                             base[0:TR, g * TG:(g + 1) * TG, :]).then_inc(s("out_sent"), 16)
            sp.wait_ge(s("out_sent"), 16 * G)

        @block.tensor
        def _(pe):
            mm = pe.matmul

            def keep_warm(b, n):
                for _ in range(n):
                    mm(bank[b][:, 0:C], zeros[:, 0:P], zeros[:, :], start=True, stop=True)

            pe.wait_ge(s("constants_set"), 1)

            def conv(r, j):
                t = RING * r + j
                pe.wait_ge(s(f"x_in{j}"), 16 * r + 16)
                if not (isinstance(t, int) and t < RING):
                    pe.wait_ge(s("pe_copied"), t - (RING - 1))
                for k in range(KX):
                    i = mm(conv_bank[j][0:TP, 0:C], xt[j][0:KP, k, :], convw[0:KP, k, :],
                           start=(k == 0), stop=(k == KX - 1))
                i.then_inc(s("conv_done"), 1)

            def window_mean(t, j):
                pe.wait_ge(s("pe_copied"), t + 1)
                for k in range(KC):
                    i = mm(red_bank[k][:, bass.ds(t * WT, WT)], pe_sb[j][0:TP, k * P:(k + 1) * P], pool_m,
                           start=True, stop=True)
                i.then_inc(s("pool_done"), 1)

            def turn(t, j):
                pe.wait_ge(s("xhat_ready"), t + 1)
                if not (isinstance(t, int) and t < RING):
                    pe.wait_ge(s("winT_ready"), t - (RING - 1))
                for k in range(KC):
                    i = pe.transpose(tr_bank[j][:, k * P:k * P + TP], xhat[j][0:TP, k * P:(k + 1) * P],
                                     ident[0:TP, 0:TP])
                i.then_inc(s("turned"), 1)

            keep_warm(7, 5)
            pe.wait_ge(s("convw_in"), 16 * KX)
            def around(t, j, before):
                if before >= 1:
                    window_mean(t - 1, (j - 1) % RING)
                if before >= 2:
                    turn(t - 2, (j - 2) % RING)

            for t in range(HEAD):
                conv(t // RING, t % RING)
                if t == 0:
                    pe.wait_ge(s("cons_in"), 16)
                around(t, t % RING, t)
            with pe.Fori(HEAD // RING, TILES // RING) as r:
                for j in range(RING):
                    conv(r, j)
                    around(RING * r + j, j, 2)
            for t in range(TAIL, TILES):
                conv(t // RING, t % RING)
                around(t, t % RING, 2)
            window_mean(TILES - 1, (TILES - 1) % RING)
            turn(TILES - 2, (TILES - 2) % RING)
            turn(TILES - 1, (TILES - 1) % RING)

            pe.wait_ge(s("redT_ready"), 2)
            for w in range(2):
                for k in range(KC):
                    i = pe.transpose(bank[0][:, w * C + k * P:w * C + (k + 1) * P],
                                     redT[:, k, w * P:(w + 1) * P], ident)
            i.then_inc(s("red_major"), 1)
            pe.wait_ge(s("winT_ready"), TILES)
            pe.wait_ge(s("c_norm"), 3)
            for k in range(KC):
                i = mm(bank[5][:, k:k + 1], small_row[0:1, k * P:(k + 1) * P], ident[0:1, 0:1], start=True, stop=True)
            i.then_inc(s("c_turned"), 1)
            keep_warm(4, 3)
            pe.wait_ge(s("tokw_in"), 48)
            pe.wait_ge(s("redx_ready"), 2)
            for k in range(KC):
                for w in range(2):
                    i = pe.transpose(bank[1 + k][:, w * P:(w + 1) * P],
                                     redx[:, w, k * P:(k + 1) * P], ident)
            i.then_inc(s("redx_turned"), 1)
            keep_warm(4, 2)
            pe.wait_ge(s("c_ln"), 2)
            for m in range(KC):
                for k in range(KC):
                    i = mm(bank[5][:, 8 + m:9 + m], tw["gwq"][:, k, m * P:(m + 1) * P], c_lnT[:, k:k + 1],
                           start=(k == 0), stop=(k == KC - 1))
            i.then_inc(s("c_q_done"), 1)
            pe.wait_ge(s("lnrT_ready"), 2)
            for m in range(KC):
                for k in range(KC):
                    i = mm(bank[(3, 1)[m]][:, 0:C], tw["wq"][:, k, m * P:(m + 1) * P], lnrT[:, k, :],
                           start=(k == 0), stop=(k == KC - 1))
                i.then_inc(s("q_done"), 1)
            pe.wait_ge(s("c_qbd"), 2)
            for k in range(KC):
                for m in range(KC):
                    i = mm(bank[5][:, 16 + k * H8:16 + (k + 1) * H8], tw["gwkT"][:, m, k * P:(k + 1) * P],
                           c_qbd[:, m, :], start=(m == 0), stop=(m == KC - 1))
            i.then_inc(s("c_qk_done"), 1)
            pe.wait_ge(s("c_qk_ready"), 1)
            for m in range(KC):
                pe.wait_ge(s(("qbd_dve", "qbd_act")[m]), (1, 4)[m])
                for g in range(4):
                    for k in range(KC):
                        i = mm(bank[4 - 4 * m + g][:, k * C:(k + 1) * C],
                               tw["wkT"][:, m, k * P:(k + 1) * P], qbd[:, m, g, :], start=True, stop=True)
                    i.then_inc(s("qk_done"), 1)

            pe.wait_ge(s("qk_dve"), 4)
            pe.wait_ge(s("qk_act"), 4)

            def scores(q):
                if q >= 2:
                    pe.wait_ge(s("masked"), steps_until(q - 1))
                for t, n, u in tiles_of(q):
                    for k in range(KC):
                        i = mm(bank[q % 2][0:H8 * n, u * TP:u * TP + n * NWIN], qkT[:, k, t * WT:t * WT + n, :],
                               winT[:, k, t * TP:t * TP + n * NWIN], start=(k == 0), stop=(k == KC - 1))
                i.then_inc(s("scored"), 1)

            def turn_att(q):
                pe.wait_ge(s("att_ready"), q + 1)
                if q >= 2:
                    pe.wait_ge(s("attT_ready"), q - 1)
                for t, n, u in tiles_of(q):
                    i = pe.transpose(bank[2 + q % 2][0:n * NWIN, u * P:u * P + H8 * n],
                                     s_att[q % RING][0:H8 * n, u, 0:n * NWIN], ident[0:H8 * n, 0:H8 * n])
                i.then_inc(s("att_turned"), 1)

            def attend(q):
                pe.wait_ge(s("attT_ready"), q + 1)
                if q == 0:
                    pe.wait_ge(s("xall_done"), TILES)
                if q >= 2:
                    pe.wait_ge(s("ctx_act"), q - 1)
                    pe.wait_ge(s("ctx_dve"), q - 1)
                for k in range(KC):
                    for t, n, u in tiles_of(q):
                        i = mm(bank[4 + 2 * k + q % 2][:, u * H8 * WT:u * H8 * WT + H8 * n],
                               xhat_all[0:n * NWIN, t, k * P:(k + 1) * P],
                               s_attT[q % RING][0:n * NWIN, u, 0:H8 * n], start=True, stop=True)
                i.then_inc(s("attended"), 1)

            for q in range(STEPS + 3):
                if q < STEPS:
                    scores(q)
                if 2 <= q < STEPS + 2:
                    turn_att(q - 2)
                if q >= 3:
                    attend(q - 3)
            pe.wait_ge(s("ctx_act"), STEPS)
            pe.wait_ge(s("ctx_dve"), STEPS)

            for m in range(KC):
                for k in range(KC):
                    for g in range(4):
                        hh = 4 * m + g
                        i = mm(bank[6][g * DH:(g + 1) * DH, m * C:(m + 1) * C],
                               tw["wv"][:, k, hh * DH:(hh + 1) * DH], ctxT[:, k, :, hh],
                               start=(k == 0), stop=(k == KC - 1))
            i.then_inc(s("agg_done"), 1)
            pe.wait_ge(s("w_abs_ready"), 1)
            mm(bank[3][:, 0:1], mean_m, w_abs, start=True, stop=True).then_inc(s("w_mean_done"), 1)
            keep_warm(0, 2)
            pe.wait_ge(s("aggT_ready"), 1)
            for m in range(KC):
                for k in range(KC):
                    i = mm(bank[m][:, 0:C], tw["proj"][:, k, m * P:(m + 1) * P], aggT[:, k, :],
                           start=(k == 0), stop=(k == KC - 1))
                i.then_inc(s("proj_done"), 1)
            keep_warm(7, 1)
            pe.wait_ge(s("local_ready"), 2)
            for w in range(2):
                for k in range(KC):
                    i = pe.transpose(bank[2][:, w * C + k * P:w * C + (k + 1) * P],
                                     localT[:, k, w * P:(w + 1) * P], ident)
            i.then_inc(s("lo_major"), 1)
            pe.wait_ge(s("w_chain"), 1)
            for m in range(KC):
                for k in range(KC):
                    i = mm(bank[3][:, m * C:(m + 1) * C], tw["mod"][:, k, m * P:(m + 1) * P], localT[:, k, :],
                           start=(k == 0), stop=(k == KC - 1))
            i.then_inc(s("mod_done"), 1)
            keep_warm(7, 3)
            pe.wait_ge(s("lox_ready"), 2)
            for k in range(KC):
                for w in range(2):
                    i = pe.transpose(bank[4 + k][:, w * P:(w + 1) * P],
                                     lox[:, w, k * P:(k + 1) * P], ident)
            i.then_inc(s("lox_turned"), 1)
            keep_warm(7, 2)
            pe.wait_ge(s("lnlT_ready"), 2)
            for k in range(KC):
                i = mm(bank[7][0:H8, 0:WINDOWS], c_qk[:, k, :], lnlT[:, k, :], start=(k == 0), stop=(k == KC - 1))
            i.then_inc(s("gscored"), 1)
            for m in range(KC):
                for k in range(KC):
                    i = mm(bank[6][:, m * C:(m + 1) * C], tw["gwv"][:, k, m * P:(m + 1) * P], lnlT[:, k, :],
                           start=(k == 0), stop=(k == KC - 1))
            i.then_inc(s("gv_done"), 1)
            keep_warm(1, 6)
            pe.wait_ge(s("gattn_ready"), 1)
            for m in range(KC):
                i = mm(bank[0][:, m * C:(m + 1) * C], heads8[:, m, :], gattn[:, 2, :], start=True, stop=True)
            i.then_inc(s("gspread"), 1)
            keep_warm(1, 3)
            pe.wait_ge(s("gagg_ready"), 1)
            for m in range(KC):
                for k in range(KC):
                    i = mm(bank[1][:, m * IMAGES:(m + 1) * IMAGES], tw["gproj"][:, k, m * P:(m + 1) * P],
                           gaggT[:, k, :], start=(k == 0), stop=(k == KC - 1))
            i.then_inc(s("gproj_done"), 1)

            keep_warm(2, 2)
            pe.wait_ge(s("h0T_ready"), 6)
            h0T_v = h0T[:, :, :, :].rearrange("p k i t -> p k (i t)")
            for g in range(G):
                for u in range(TG):
                    for k in range(KC):
                        a = g * GT + u * TR
                        i = pe.transpose(bank[4 * g][0:TR, u * C + k * P:u * C + (k + 1) * P],
                                         h0T_v[:, k, a:a + TR], ident)
                i.then_inc(s("h0_major"), 1)

            def turn_x(n, g):
                pe.wait_ge(s("xn_ready"), TT * n + TG * (g + 1))
                for u in range(TG):
                    for k in range(KC):
                        i = pe.transpose(bank[4 * g + 1][:, k * GT + u * TR:k * GT + (u + 1) * TR],
                                         xn[0:TR, TG * g + u, k * P:(k + 1) * P], ident[0:TR, 0:TR])
                i.then_inc(s("x_turned"), 1)

            def channels(b, at, w, cols_, src, done=None):
                for k in range(KC):
                    i = mm(bank[b][:, at:at + GT], w[:, k, cols_:cols_ + P], src[:, k, :],
                           start=(k == 0), stop=(k == KC - 1))
                if done:
                    i.then_inc(s(done), 1)

            def tokens(b, srcT, w, done):
                for u in range(TG):
                    for k in range(KC):
                        i = mm(bank[b][0:TR, u * C:(u + 1) * C], srcT[:, k, u * TR:(u + 1) * TR], w[:, k, :],
                               start=(k == 0), stop=(k == KC - 1))
                i.then_inc(s(done), 1)

            groups = range(G)
            pe.wait_ge(s("layw_in"), 16 * 5)
            keep_warm(3, 5)
            for g in groups:
                turn_x(0, g)
            keep_warm(3, 1)
            for g in groups:
                pe.wait_ge(s("xT_ready"), g + 1)
                for m in range(KC):
                    channels(4 * g + 3, m * GT, lw["w_in"], C + m * P, xT[:, g], "val_mm")
                for m in range(KC):
                    channels(4 * g + 2, m * GT, lw["w_in"], m * P, xT[:, g], "gate_mm")
            for g in groups:
                pe.wait_ge(s("val_ready"), KC * (g + 1))
                for m in range(KC):
                    channels(4 * g, m * GT, lw["w_s"], m * P, val[:, g], "sv_mm")
            keep_warm(7, 3)
            for g in groups:
                pe.wait_ge(s("scan_ready"), g + 1)
                tokens(4 * g + 1, scanT[:, g], lw["w_o"], "mix_done")
            keep_warm(7, 8)
            for g in groups:
                turn_x(1, g)
            for g in groups:
                pe.wait_ge(s("xT_ready"), G + g + 1)
                if g == 0:
                    pe.wait_ge(s("tern_ready"), 1)
                tokens(4 * g + 2, xT[:, g], lw["tern"], "tern_done")
            keep_warm(7, 9)
            for g in groups:
                turn_x(2, g)
            for g in groups:
                pe.wait_ge(s("xT_ready"), 2 * G + g + 1)
                channels(4 * g + 3, 0, lw["basis"], 0, xT[:, g], "lat_done")
                for m in range(KC):
                    channels(4 * g + 2, m * GT, lw["v_w"], m * P, xT[:, g], "v_done")
            pe.wait_ge(s("heads_ready"), 1)
            for g in groups:
                pe.wait_ge(s("lat_ready"), 2 * (g + 1))
                for j in range(NP2):
                    if j == 4:
                        pe.wait_ge(s("vT_ready"), 2 * (g + 1))
                    mm(bank[4 * g + (0, 1, 3, 2)[j // 2]][:, (j % 2) * GT:(j % 2 + 1) * GT],
                       heads[:, 2 * j:2 * j + 2, :], latT[:, g * GI:(g + 1) * GI, :], start=True, stop=True)\
                        .then_inc(s("lt_done"), 1)
            for g in groups:
                pe.wait_ge(s("lt_act"), 2 * (g + 1))
                pe.wait_ge(s("lt_dve"), 2 * (g + 1))
                for i_ in range(GI):
                    im = g * GI + i_
                    i = mm(bank[4 * g][0:NP2 * T, i_ * 2 * T:(i_ + 1) * 2 * T],
                           ltT[:, im * T:(im + 1) * T, :], latD[:, im, :, :], start=True, stop=True)
                i.then_inc(s("att_scored"), 1)
            keep_warm(7, 4)
            for g in groups:
                pe.wait_ge(s("att_probs"), g + 1)
                for t in range(T):
                    if t >= 3:
                        pe.wait_ge(s("y_mul"), T * g + t - 2)
                    for p in range(2):
                        i = mm(bank[4 * g + 1 + t % 3][:, p * GT:p * GT + GI * (t + 1)], spread[:, t, :],
                               att[0][:, g * GI:(g + 1) * GI, p, 0:t + 1], start=True, stop=True)
                    i.then_inc(s("spread_done"), 1)
            for g in groups:
                pe.wait_ge(s("y_ready"), T * (g + 1))
                tokens(4 * g, yT[:, g], lw["o_w"], "lat_out_done")
            keep_warm(7, 9)
            for g in groups:
                turn_x(3, g)
            for g in groups:
                pe.wait_ge(s("xT_ready"), 3 * G + g + 1)
                for k in range(KC):
                    i = mm(bank[4 * g + 2][0:E8, 0:GT], lw["gate"][:, k, :], xT[:, g, k, :],
                           start=(k == 0), stop=(k == KC - 1))
                i.then_inc(s("gate_done"), 1)
            keep_warm(3, 26)
            pe.wait_ge(s("slots_ready"), 1)
            for t in range(TT):
                pe.transpose(bank[4][0:TR, t * 16:t * 16 + E8], sel8[:, t * TR:(t + 1) * TR], ident[0:E8, 0:E8])
                i = pe.transpose(bank[4][0:TR, t * 16 + E8:t * 16 + 2 * E8], val8[:, t * TR:(t + 1) * TR],
                                 ident[0:E8, 0:E8])
            i.then_inc(s("slots_turned"), 1)
            keep_warm(3, 2)
            pe.wait_ge(s("xn_ready"), 5 * TT)
            for t in range(TT):
                pe.wait_ge(s("pick_t"), t + 1)
                for k in range(KC):
                    i = mm(bank[6 + k][:, 0:TOK], xh2[0:TR, t, k * P:(k + 1) * P],
                           pick[0:TR, t, :, 0:CAP], start=(t == 0), stop=(t == TT - 1))
            i.then_inc(s("gathered"), 1)

            def turn_weights(q):
                if q >= 2:
                    pe.wait_ge(s("wpickT_ready"), q - 1)
                for t in range(TT):
                    pe.wait_ge(s("wpick_t"), t + 1)
                    i = pe.transpose(bank[4 + q % 2][:, t * TR:(t + 1) * TR], wpick[0:TR, t, 2 * q:2 * q + 2, :],
                                     ident[0:TR, 0:TR])
                i.then_inc(s("wpick_turned"), 1)

            def hidden(q):
                for side in range(2):
                    e = 2 * q + side
                    if e < NRES:
                        pe.wait_ge(s("resident_in"), 16 * PIECES)
                    elif e < NRES + NATT:
                        pe.wait_ge(s(f"expert_in{e}"), 32)
                    else:
                        pe.wait_ge(s("last_w1_in"), 32)
                if q >= 1:
                    pe.wait_ge(s("hid_biased"), 2 * q)
                for c in range(2):
                    for k in range(KC):
                        for side in range(2):
                            e = 2 * q + side
                            w1 = expert_half(e, 0).rearrange("p (k f) -> p k f", k=KC)
                            i = mm(bank[c][side * SW:(side + 1) * SW, :], ysT[:, k, e, :],
                                   w1[:, k, c * 512:(c + 1) * 512], start=(k == 0), stop=(k == KC - 1))
                    i.then_inc(s("hid_done"), 1)

            def turn_hidden(q):
                for c in range(2):
                    pe.wait_ge(s("hid_ready"), 2 * q + c + 1)
                    if q >= 1:
                        pe.wait_ge(s("hidT_dve" if c == 0 else "hidT_act"), q)
                    for f in range(4):
                        i = pe.transpose(bank[2 + c][:, f * P:(f + 1) * P],
                                         hid[q % 2][:, (4 * c + f) * P:(4 * c + f + 1) * P], ident)
                    i.then_inc(s("hid_turned"), 1)

            def outputs(q):
                if q >= 1:
                    pe.wait_ge(s("opair_ready"), q)
                if 2 * q >= NRES + NATT:
                    pe.wait_ge(s("last_w2_in"), 32)
                for f in range(FC):
                    if f == 0:
                        pe.wait_ge(s("hidT_dve"), q + 1)
                    if f == 4:
                        pe.wait_ge(s("hidT_act"), q + 1)
                    for side in range(2):
                        w2 = expert_half(2 * q + side, 1).rearrange("p (f c) -> p f c", f=FC)
                        i = mm(bank[4][side * SW:(side + 1) * SW, 0:C], hidT[q % 2][:, f, side * SW:(side + 1) * SW],
                               w2[:, f, :], start=(f == 0), stop=(f == FC - 1))
                i.then_inc(s("eo_done"), 1)

            def combine(q):
                pe.wait_ge(s("opair_ready"), q + 1)
                for t in range(TT):
                    i = mm(bank[5 + t // TG][0:TR, (t % TG) * C:(t % TG + 1) * C], wpickT[:, q, t * TR:(t + 1) * TR],
                           opair[q % 2], start=(q == 0 and t % TG == 0), stop=(q == E8 // 2 - 1),
                           skip_group_check=True)
                    if t % TG == TG - 1:
                        i.then_inc(s("combined"), 1)

            keep_warm(3, 2)
            pe.wait_ge(s("ysT_ready"), 2)
            hidden(0)
            for q in range(E8 // 2):
                turn_weights(q)
            pe.wait_ge(s("wpickT_ready"), E8 // 2)
            for q in range(E8 // 2):
                if q + 1 < E8 // 2:
                    hidden(q + 1)
                turn_hidden(q)
                if q:
                    combine(q - 1)
                outputs(q)
            combine(E8 // 2 - 1)

        @block.vector
        def _(dve):
            ts, tt, stt = dve.tensor_scalar, dve.tensor_tensor, dve.scalar_tensor_tensor

            def stats(t, j):
                dve.wait_ge(s("pe_copied"), t + 1)
                dve.bn_stats(a_st[j][0:TP], pe_sb[j][0:TP]).then_inc(s("bn_done"), 1)

            def norm(t, j):
                dve.wait_ge(s("rs_ready"), t + 1)
                if not (isinstance(t, int) and t < RING):
                    dve.wait_ge(s("turned"), t - (RING - 1))
                    dve.wait_ge(s("xall_done"), t - (RING - 1))
                ts(xhat[j][0:TP], pe_sb[j][0:TP], a_mv[j][0:TP, 0:1], a_rs[j][0:TP], ALU.subtract, ALU.mult)\
                    .then_inc(s("xhat_ready"), 1)

            def patch_step(t, j, first=False):
                stats(t, j)
                dve.wait_ge(s("bn_done"), t + 1)
                if not first:
                    norm(t - 1, (j - 1) % RING)
                dve.bn_aggr(a_mv[j][0:TP], a_st[j][0:TP]).then_inc(s("mv_ready"), 1)

            class_row = cols[0:1, COLS["class_row"][0]:COLS["class_row"][0] + C]
            for t in range(HEAD):
                patch_step(t, t % RING, t == 0)
                if t == 2:
                    dve.wait_ge(s("cols_in"), 16)
                    dve.bn_stats(c_st[0:1], class_row).then_inc(s("c_norm"), 1)
                    dve.wait_ge(s("c_norm"), 1)
                    dve.bn_aggr(c_mv[0:1], c_st[0:1]).then_inc(s("c_norm"), 1)
                if t == 4:
                    dve.wait_ge(s("c_rs_ready"), 1)
                    ts(small_row[0:1, :], class_row, c_mv[0:1, 0:1], c_rs[0:1], ALU.subtract, ALU.mult)\
                        .then_inc(s("c_norm"), 1)
            with dve.Fori(HEAD // RING, TILES // RING) as r:
                for j in range(RING):
                    patch_step(RING * r + j, j)
            for t in range(TAIL, TILES):
                patch_step(t, t % RING)
            norm(TILES - 1, (TILES - 1) % RING)
            dve.wait_ge(s("pool_done"), TILES)
            dve.tensor_copy(redT[:, 0, :], red_bank[0][:, 0:WINDOWS]).then_inc(s("redT_ready"), 1)

            def norm_two(src_bank, st, mv, rs, dst, major, mv_name, rs_name, out_name, n_bn):
                dve.wait_ge(s(major), 1)
                for w in range(2):
                    dve.bn_stats(st[:, w, :], src_bank[:, w * C:(w + 1) * C]).then_inc(s("bn2_done"), 1)
                for w in range(2):
                    dve.wait_ge(s("bn2_done"), n_bn + w + 1)
                    dve.bn_aggr(mv[:, w, :], st[:, w, :]).then_inc(s(mv_name), 1)
                dve.wait_ge(s(rs_name), 1)
                for w in range(2):
                    ts(dst[:, w, :], src_bank[:, w * C:(w + 1) * C], mv[:, w, 0:1], rs[:, w:w + 1],
                       ALU.subtract, ALU.mult).then_inc(s(out_name), 1)

            norm_two(bank[0], w_st, w_mv, w_rs, redx, "red_major", "w_mv_ready", "w_rs_ready", "redx_ready", 0)
            dve.wait_ge(s("c_turned"), 1)
            for k in range(KC):
                ts(c_lnT[:, k:k + 1], bank[5][:, k:k + 1], col("gq_g", k), col("gq_b", k), ALU.mult, ALU.add)\
                    .then_inc(s("c_ln"), 1)
            dve.wait_ge(s("redx_turned"), 1)
            ts(lnrT[:, 0, :], bank[1][:, 0:C], col("q_g", 0), col("q_b", 0), ALU.mult, ALU.add)\
                .then_inc(s("lnrT_ready"), 1)
            dve.wait_ge(s("cons_in"), 32)
            dve.wait_ge(s("c_q_done"), 1)
            for k in range(KC):
                ts(c_qbd[:, k, :], headcol[:, k, :], bank[5][:, 8 + k:9 + k], None, ALU.mult)\
                    .then_inc(s("c_qbd"), 1)
            dve.wait_ge(s("q_done"), 1)
            tt(qbd[:, 0], bank[3][:, 0:C].unsqueeze(1).to_broadcast([P, 4, C]),
               headcol[:, 0, 0:4].unsqueeze(2).to_broadcast([P, 4, C]), ALU.mult).then_inc(s("qbd_dve"), 1)
            dve.wait_ge(s("c_qk_done"), 1)
            dve.tensor_copy(c_qk.rearrange("p k h -> p (k h)"), bank[5][:, 16:16 + KC * H8])\
                .then_inc(s("c_qk_ready"), 1)
            for n in range(4):
                m, g = divmod(2 * n, 4)
                dve.wait_ge(s("qk_done"), 2 * n + 1)
                dve.tensor_copy(qkT[:, :, :, 4 * m + g], bank[4 - 4 * m + g][:, :].rearrange("p (k w) -> p k w", k=KC))\
                    .then_inc(s("qk_dve"), 1)

            def masked(q):
                j = q % RING
                dve.wait_ge(s("scored"), q + 1)
                if q >= RING:
                    dve.wait_ge(s("s_exp_ready"), steps_until(q - RING + 1))
                for t, n, u in tiles_of(q):
                    rows, wide = H8 * n, n * NWIN
                    mk = mask if n == WT else mask_last
                    dve.tensor_tensor_reduce(s_msk[j][0:rows, u, 0:wide], bank[q % 2][0:rows, u * TP:u * TP + wide],
                                             mk[0:rows, 0:wide], 1.0, NEG, ALU.add, ALU.max,
                                             s_mx[j][0:rows, u:u + 1]).then_inc(s("masked"), 1)
                dve.wait_ge(s("masked"), steps_until(q + 1))
                _, n, u = tiles_of(q)[-1]
                ts(s_nmx[j][0:H8 * n, 0:u + 1], s_mx[j][0:H8 * n, 0:u + 1], -C ** -0.5, None, ALU.mult)\
                    .then_inc(s("nmx_ready"), 1)

            def recip(q):
                _, n, u = tiles_of(q)[-1]
                dve.wait_ge(s("s_exp_ready"), steps_until(q + 1))
                if q >= RING:
                    dve.wait_ge(s("att_ready"), q - RING + 1)
                dve.reciprocal(s_rec[q % RING][0:H8 * n, 0:u + 1], s_sum[q % RING][0:H8 * n, 0:u + 1])\
                    .then_inc(s("rec_ready"), 1)

            def attT(q):
                _, n, u = tiles_of(q)[-1]
                dve.wait_ge(s("att_turned"), q + 1)
                if q >= RING:
                    dve.wait_ge(s("attended"), q - RING + 1)
                dve.tensor_copy(s_attT[q % RING][0:n * NWIN, 0:u + 1, 0:H8 * n],
                                bank[2 + q % 2][0:n * NWIN, 0:2 * P].rearrange("p (u r) -> p u r", u=2)
                                [:, 0:u + 1, 0:H8 * n]).then_inc(s("attT_ready"), 1)

            def ctx0(q):
                t, n = 2 * q, sum(n for _, n, _ in tiles_of(q))
                dve.wait_ge(s("attended"), q + 1)
                ts(ctxT[:, 0, t * WT:t * WT + n, :].rearrange("p w h -> p (w h)"), bank[4 + q % 2][:, 0:H8 * n],
                   col("kv_g", 0), col("kv_b", 0), ALU.mult, ALU.add).then_inc(s("ctx_dve"), 1)

            for q in range(STEPS + 3):
                if q < STEPS:
                    masked(q)
                if 1 <= q < STEPS + 1:
                    recip(q - 1)
                if 2 <= q < STEPS + 2:
                    attT(q - 2)
                if q >= 3:
                    ctx0(q - 3)

            dve.wait_ge(s("layw_in"), 16 * 5)
            flat = lw["tern"].rearrange("p k c -> p (k c)")
            dve.tensor_reduce(w_abs, flat, AX.X, ALU.add, apply_absolute_value=True).then_inc(s("w_abs_ready"), 1)
            dve.wait_ge(s("agg_done"), 1)
            dve.tensor_copy(aggT.rearrange("p k w -> p (k w)"), bank[6][:, :]).then_inc(s("aggT_ready"), 1)
            dve.wait_ge(s("w_mean_done"), 1)
            ts(w_scale[:, 0:1], bank[3][:, 0:1], EPS, None, ALU.max).then_inc(s("w_chain"), 1)
            dve.wait_ge(s("w_chain"), 1)
            ts(w_scale[:, 1:2], w_scale[:, 0:1], 0.5, None, ALU.mult).then_inc(s("w_chain"), 1)
            ts(w_scale[:, 2:3], w_scale[:, 0:1], -0.5, None, ALU.mult).then_inc(s("w_chain"), 1)
            for m in range(KC):
                dve.wait_ge(s("proj_done"), m + 1)
                stt(localT[:, m, :], bank[m][:, 0:C], col("proj_b", m), redT[:, m, :], ALU.add, ALU.add)\
                    .then_inc(s("local_ready"), 1)
            norm_two(bank[2], l_st, l_mv, l_rs, lox, "lo_major", "l_mv_ready", "l_rs_ready", "lox_ready", 2)
            dve.wait_ge(s("lox_turned"), 1)
            ts(lnlT[:, 0, :], bank[4][:, 0:C], col("gkv_g", 0), col("gkv_b", 0), ALU.mult, ALU.add)\
                .then_inc(s("lnlT_ready"), 1)
            dve.wait_ge(s("gscored"), 1)
            g3 = lambda v: v.rearrange("p (i w) -> p i w", w=HW)
            dve.tensor_reduce(g_mx, g3(bank[7][0:H8, 0:WINDOWS]), AX.X, ALU.max).then_inc(s("g_chain"), 1)
            dve.wait_ge(s("g_chain"), 1)
            tt(g3(gattn[:, 0, :]), g3(bank[7][0:H8, 0:WINDOWS]), g_mx.unsqueeze(2).to_broadcast([H8, IMAGES, HW]),
               ALU.subtract).then_inc(s("g_shifted"), 1)
            dve.wait_ge(s("g_exp"), 1)
            dve.tensor_reduce(g_sum, g3(gattn[:, 1, :]), AX.X, ALU.add).then_inc(s("g_chain"), 1)
            dve.wait_ge(s("g_chain"), 2)
            dve.reciprocal(g_rec, g_sum).then_inc(s("g_chain"), 1)
            dve.wait_ge(s("g_chain"), 3)
            tt(g3(gattn[:, 2, :]), g3(gattn[:, 1, :]), g_rec.unsqueeze(2).to_broadcast([H8, IMAGES, HW]), ALU.mult)\
                .then_inc(s("gattn_ready"), 1)
            dve.wait_ge(s("gspread"), 1)
            dve.wait_ge(s("gvT_ready"), 1)
            tt(gprod.rearrange("p k w -> p (k w)"), bank[0][:, :], gvT.rearrange("p k w -> p (k w)"), ALU.mult)\
                .then_inc(s("g_chain"), 1)
            dve.wait_ge(s("g_chain"), 4)
            dve.tensor_reduce(gaggT.rearrange("p k i -> p (k i)"),
                              gprod.rearrange("p k (i w) -> p (k i) w", w=HW), AX.X, ALU.add)\
                .then_inc(s("gagg_ready"), 1)
            dve.wait_ge(s("gproj_done"), 1)
            for m in range(KC):
                ts(h0T[:, m, :, T - 1], bank[1][:, m * IMAGES:(m + 1) * IMAGES], col("gproj_b", m),
                   col("class_emb", m), ALU.add, ALU.add).then_inc(s("h0T_ready"), 1)

            def norm_stats(n, g, src=None):
                src = h if src is None else src
                for u in range(TG):
                    dve.bn_stats(t_st[0:TR, TG * g + u, :], src[0:TR, TG * g + u, :]).then_inc(s("t_bn"), 1)
                for u in range(TG):
                    dve.wait_ge(s("t_bn"), TT * n + TG * g + u + 1)
                    dve.bn_aggr(t_mv[0:TR, TG * g + u, :], t_st[0:TR, TG * g + u, :]).then_inc(s("t_mv_ready"), 1)

            def norm(n, g, src=None, dst=None):
                src, dst = (h if src is None else src), (xn if dst is None else dst)
                dve.wait_ge(s("t_rs_ready"), G * n + g + 1)
                if 1 <= n < 4:
                    dve.wait_ge(s("x_turned"), G * (n - 1) + g + 1)
                if n == 1:
                    dve.wait_ge(s("base_ready"), g + 1)
                for u in range(TG):
                    t = TG * g + u
                    ts(dst[0:TR, t, :], src[0:TR, t, :], t_mv[0:TR, t, 0:1], t_rs[0:TR, t:t + 1],
                       ALU.subtract, ALU.mult).then_inc(s("xn_ready"), 1)

            def add_to_h(g, b, other, ready, n):
                dve.wait_ge(s(ready), n)
                sl = slice(TG * g, TG * (g + 1))
                tt(h[0:TR, sl, :], bank[b][0:TR, 0:TG * C].rearrange("p (u c) -> p u c", u=TG), other[0:TR, sl, :],
                   ALU.add).then_inc(s("h_ready"), 1)

            groups = range(G)
            for g in groups:
                dve.wait_ge(s("h0_ready"), g + 1)
                norm_stats(0, g)
            for g in groups:
                norm(0, g)
            for g in groups:
                for m in range(KC):
                    dve.wait_ge(s("val_mm"), KC * (g + 1))
                    ts(val[:, g, m, :], bank[4 * g + 3][:, m * GT:(m + 1) * GT], col("b_in", KC + m), None, ALU.add)\
                        .then_inc(s("val_ready"), 1)
            f = lambda v: v.rearrange("p k n -> p (k n)")
            for g in groups:
                dve.wait_ge(s("gate_tanh"), KC * (g + 1))
                ts(f(keep[:, g]), f(gate_t[:, g]), -0.5, 0.5, ALU.mult, ALU.add).then_inc(s("keep_made"), 1)
                ts(f(gate_v[:, g]), f(gate_t[:, g]), 0.5, 0.5, ALU.mult, ALU.add).then_inc(s("gate_made"), 1)
                dve.wait_ge(s("keep_made"), 2 * g + 1)
                dve.memset(f(keep[:, g]).rearrange("p (i t) -> p i t", t=T)[:, :, 0:1], 0.0)\
                    .then_inc(s("keep_made"), 1)
            for g in groups:
                dve.wait_ge(s("sv_tanh"), KC * (g + 1))
                dve.wait_ge(s("gate_made"), g + 1)
                tt(f(sv[:, g]), f(sv[:, g]), f(gate_v[:, g]), ALU.mult).then_inc(s("drive_made"), 1)
                dve.wait_ge(s("drive_made"), g + 1)
                dve.wait_ge(s("keep_made"), 2 * g + 2)
                dve.tensor_tensor_scan(f(scanT[:, g]), f(keep[:, g]), f(sv[:, g]), 0.0, ALU.mult, ALU.add)\
                    .then_inc(s("scan_ready"), 1)
            tmp, tmp2 = tern_tmp
            ts(tmp, flat, w_scale[:, 2:3], w_scale[:, 0:1], ALU.is_lt, ALU.mult).then_inc(s("w_chain"), 1)
            ts(tmp2, flat, w_scale[:, 1:2], w_scale[:, 0:1], ALU.is_gt, ALU.mult).then_inc(s("w_chain"), 1)
            dve.wait_ge(s("w_chain"), 5)
            tt(flat, tmp2, tmp, ALU.subtract).then_inc(s("tern_ready"), 1)
            for g in groups:
                dve.wait_ge(s("base_ready"), g + 1)
                add_to_h(g, 4 * g + 1, base, "mix_done", g + 1)
                dve.wait_ge(s("h_ready"), g + 1)
                norm_stats(1, g)
            for g in groups:
                norm(1, g)
            for g in groups:
                add_to_h(g, 4 * g + 2, h, "tern_done", g + 1)
                dve.wait_ge(s("h_ready"), G + g + 1)
                norm_stats(2, g)
            for g in groups:
                norm(2, g)
            dve.wait_ge(s("latD_clear"), 1)
            for g in groups:
                dve.wait_ge(s("lat_done"), g + 1)
                for p in range(2):
                    dve.tensor_copy(latD[p * R:(p + 1) * R, g * GI:(g + 1) * GI, p, :],
                                    bank[4 * g + 3][p * R:(p + 1) * R, 0:GT].rearrange("p (i t) -> p i t", t=T))\
                        .then_inc(s("lat_ready"), 1)
            for g in groups:
                for n in range(2):
                    dve.wait_ge(s("lt_done"), NP2 * g + 4 * n + 2)
                    b = 4 * g + (0, 3)[n]
                    dve.tensor_copy(ltT[:, g * GT:(g + 1) * GT, 4 * n:4 * n + 2].rearrange("p n j -> p j n"),
                                    bank[b][:, 0:2 * GT].rearrange("p (j n) -> p j n", j=2)).then_inc(s("lt_dve"), 1)
            a3 = lambda i, g: att[i][:, g * GI:(g + 1) * GI].rearrange("p i a t -> p (i a) t")
            st = lambda i, g: a_stat[:, i, g * GI * 2:(g + 1) * GI * 2]
            bc = lambda v: v.unsqueeze(2).to_broadcast([NP2 * T, GI * 2, T])
            for g in groups:
                dve.wait_ge(s("att_scored"), g + 1)
                tt(a3(0, g), bank[4 * g][0:NP2 * T, 0:2 * GT].rearrange("p (n t) -> p n t", t=T),
                   causal.unsqueeze(1).to_broadcast([NP2 * T, GI * 2, T]), ALU.add).then_inc(s("att_chain"), 1)
                dve.wait_ge(s("att_chain"), 2 * g + 1)
                dve.tensor_reduce(st(0, g), a3(0, g), AX.X, ALU.max).then_inc(s("att_chain"), 1)
                dve.wait_ge(s("att_chain"), 2 * g + 2)
                tt(a3(1, g), a3(0, g), bc(st(0, g)), ALU.subtract).then_inc(s("att_shifted"), 1)
            for g in groups:
                dve.wait_ge(s("att_exp"), g + 1)
                dve.tensor_reduce(st(1, g), a3(1, g), AX.X, ALU.add).then_inc(s("att_sum"), 1)
                dve.wait_ge(s("att_sum"), 2 * g + 1)
                dve.reciprocal(st(2, g), st(1, g)).then_inc(s("att_sum"), 1)
                dve.wait_ge(s("att_sum"), 2 * g + 2)
                tt(a3(0, g), a3(1, g), bc(st(2, g)), ALU.mult).then_inc(s("att_probs"), 1)
            for g in groups:
                dve.wait_ge(s("vT_ready"), KC * (g + 1))
                v4 = vT[:, g].rearrange("p k (i t) -> p k i t", t=T)
                y4 = yT[:, g].rearrange("p k (i t) -> p k i t", t=T)
                for t in range(T):
                    n = T * g + t
                    dve.wait_ge(s("spread_done"), n + 1)
                    if n >= 2:
                        dve.wait_ge(s("y_ready"), n - 1)
                    pr = prod[t % 2][:, 0:KC * GI * (t + 1)].rearrange("p (k i u) -> p k i u", k=KC, u=t + 1)
                    sp_ = bank[4 * g + 1 + t % 3][:, 0:KC * GT].rearrange("p (k n) -> p k n", k=KC)
                    sp_ = sp_[:, :, 0:GI * (t + 1)].rearrange("p k (i u) -> p k i u", u=t + 1)
                    tt(pr, sp_, v4[:, :, :, 0:t + 1], ALU.mult).then_inc(s("y_mul"), 1)
                    dve.wait_ge(s("y_mul"), n + 1)
                    dve.tensor_reduce(y4[:, :, :, t], pr, AX.X, ALU.add).then_inc(s("y_ready"), 1)
            for g in groups:
                dve.wait_ge(s("base_ready"), G + g + 1)
                add_to_h(g, 4 * g, base, "lat_out_done", g + 1)
                dve.wait_ge(s("h_ready"), 2 * G + g + 1)
                norm_stats(3, g)
            for g in groups:
                norm(3, g)
            dve.memset(ysT, 0.0).then_inc(s("ysT_clear"), 1)
            for g in groups:
                dve.wait_ge(s("xn_ready"), 3 * TT + TG * (g + 1))
                norm_stats(4, g, xn)
            dve.wait_ge(s("gate_tanh2"), G)
            ts(val8, work8[0], 1.0, 0.5, ALU.add, ALU.mult).then_inc(s("top"), 1)
            n_top = 1
            src = val8
            for r in range(CAP // 8):
                dve.wait_ge(s("top"), n_top)
                dve.max(m8[:, r, :], src).then_inc(s("top"), 1)
                if r < G:
                    norm(4, r, xn, xh2)
                dve.wait_ge(s("top"), n_top + 1)
                dst = work8[r % 2]
                dve.match_replace(dst, m8[:, r, :], src, -1.0).then_inc(s("top"), 1)
                n_top += 2
                src = dst
            assert src is work8[1]
            dve.wait_ge(s("top"), n_top)
            ts(work8[0], src, 0.0, None, ALU.is_lt).then_inc(s("top"), 1)
            dve.wait_ge(s("top"), n_top + 1)
            dve.tensor_tensor_scan(work8[1], work8[0], work8[0], 0.0, ALU.add, ALU.max).then_inc(s("top"), 1)
            dve.wait_ge(s("top"), n_top + 2)
            tt(sel8, work8[1], work8[0], ALU.mult).then_inc(s("slots_ready"), 1)
            dve.wait_ge(s("slots_turned"), 1)
            sv_ = bank[4][0:TR, 0:TT * 16].rearrange("p (t a e) -> p t a e", t=TT, a=2)
            dve.tensor_copy(slotT[0:TR], sv_[:, :, 0, :]).then_inc(s("slotT_ready"), 1)
            dve.tensor_copy(valT[0:TR], sv_[:, :, 1, :]).then_inc(s("slotT_ready"), 1)
            dve.wait_ge(s("slotT_ready"), 2)
            for t in range(TT):
                tt(pick[0:TR, t, :, :], slotT[0:TR, t, :].unsqueeze(2).to_broadcast([TR, E8, SW]),
                   slots[0:TR].unsqueeze(1).to_broadcast([TR, E8, SW]), ALU.is_equal).then_inc(s("pick_t"), 1)
            dve.wait_ge(s("gathered"), 1)
            dve.wait_ge(s("ysT_clear"), 1)
            ts(ysT[:, 0, :, 0:CAP], bank[6][:, 0:TOK].rearrange("p (e c) -> p e c", e=E8), col("ln_g", 0),
               col("ln_b", 0), ALU.mult, ALU.add).then_inc(s("ysT_ready"), 1)
            for q in range(E8 // 2):
                dve.wait_ge(s("wpick_turned"), q + 1)
                dve.tensor_copy(wpickT[:, q, :], bank[4 + q % 2][:, 0:TOK]).then_inc(s("wpickT_ready"), 1)

            def bias(q):
                for c in range(2):
                    dve.wait_ge(s("hid_done"), 2 * q + c + 1)
                    dve.wait_ge(s(f"b1_in{q % 2}"), 32 * (q // 2 + 1))
                    if q >= 2:
                        dve.wait_ge(s("hid_turned"), 2 * (q - 2) + c + 1)
                    tt(hid[q % 2][:, c * 512:(c + 1) * 512], bank[c][:, :], b1_rows[:, q % 2, c * 512:(c + 1) * 512],
                       ALU.add).then_inc(s("hid_biased"), 1)

            def turned(q):
                dve.wait_ge(s("hid_turned"), 2 * q + 1)
                if q >= 2:
                    dve.wait_ge(s("eo_done"), q - 1)
                dve.tensor_copy(hidT[q % 2][:, 0:4, :].rearrange("p f n -> p (f n)"), bank[2][:, :])\
                    .then_inc(s("hidT_dve"), 1)

            def pair(q):
                dve.wait_ge(s("eo_done"), q + 1)
                if q == 0:
                    dve.wait_ge(s("b2_in"), 16 * E8)
                if q >= 2:
                    dve.wait_ge(s("combined"), G * (q - 1))
                tt(opair[q % 2], bank[4][:, 0:C], b2_rows[:, q, :], ALU.add).then_inc(s("opair_ready"), 1)

            bias(0)
            for q in range(E8 // 2):
                if q + 1 < E8 // 2:
                    bias(q + 1)
                turned(q)
                pair(q)
            for g in groups:
                dve.wait_ge(s("base_ready"), 2 * G + g + 1)
                dve.wait_ge(s("combined"), G * (E8 // 2 - 1) + g + 1)
                sl = slice(TG * g, TG * (g + 1))
                tt(base[0:TR, sl, :], bank[5 + g][0:TR, :].rearrange("p (u c) -> p u c", u=TG), base[0:TR, sl, :],
                   ALU.add).then_inc(s("out_ready"), 1)

        @block.scalar
        def _(act):
            ac = act.activation

            def copy_pe(t, j):
                act.wait_ge(s("conv_done"), t + 1)
                if not (isinstance(t, int) and t < RING):
                    act.wait_ge(s("xhat_ready"), t - (RING - 1))
                    act.wait_ge(s("pool_done"), t - (RING - 1))
                ac(pe_sb[j][0:TP], conv_bank[j][0:TP, 0:C], ACT.Copy).then_inc(s("pe_copied"), 1)

            def affine(t, j):
                act.wait_ge(s("turned"), t + 1)
                for k in range(KC):
                    i = ac(winT[:, k, bass.ds(t * TP, TP)], tr_bank[j][:, k * P:k * P + TP], ACT.Identity,
                           bias=col("kv_b", k), scale=col("kv_g", k))
                i.then_inc(s("winT_ready"), 1)

            copy_pe(0, 0)
            act.wait_ge(s("cols_in"), 16)
            for t in range(1, HEAD):
                copy_pe(t, t % RING)
                if t >= RING:
                    affine(t - RING, t % RING)
            with act.Fori(HEAD // RING, TILES // RING) as r:
                for j in range(RING):
                    copy_pe(RING * r + j, j)
                    affine(RING * r + (j - RING), j)
            for t in range(TAIL, TILES):
                copy_pe(t, t % RING)
                affine(t - RING, t % RING)
            affine(TILES - 3, (TILES - 3) % RING)
            affine(TILES - 2, (TILES - 2) % RING)
            act.wait_ge(s("pool_done"), TILES)
            ac(redT[:, 1, :], red_bank[1][:, 0:WINDOWS], ACT.Copy).then_inc(s("redT_ready"), 1)
            affine(TILES - 1, (TILES - 1) % RING)
            act.wait_ge(s("redx_turned"), 1)
            ac(lnrT[:, 1, :], bank[2][:, 0:C], ACT.Identity, bias=col("q_b", 1), scale=col("q_g", 1))\
                .then_inc(s("lnrT_ready"), 1)
            act.wait_ge(s("q_done"), 2)
            act.wait_ge(s("cons_in"), 32)
            for g in range(4):
                ac(qbd[:, 1, g, :], bank[1][:, 0:C], ACT.Identity, scale=headcol[:, 1, 4 + g:5 + g])\
                    .then_inc(s("qbd_act"), 1)
            for n in range(4):
                m, g = divmod(2 * n + 1, 4)
                act.wait_ge(s("qk_done"), 2 * n + 2)
                ac(qkT[:, :, :, 4 * m + g], bank[4 - 4 * m + g][:, :].rearrange("p (k w) -> p k w", k=KC), ACT.Copy)\
                    .then_inc(s("qk_act"), 1)

            def expo(q):
                j = q % RING
                act.wait_ge(s("nmx_ready"), q + 1)
                if q >= RING:
                    act.wait_ge(s("att_ready"), q - RING + 1)
                for t, n, u in tiles_of(q):
                    rows, wide = H8 * n, n * NWIN
                    ac(s_exp[j][0:rows, u, 0:wide], s_msk[j][0:rows, u, 0:wide], ACT.Exp,
                       bias=s_nmx[j][0:rows, u:u + 1], scale=C ** -0.5, accum_out=s_sum[j][0:rows, u:u + 1])\
                        .then_inc(s("s_exp_ready"), 1)

            def ctx1(q):
                t, n = 2 * q, sum(n for _, n, _ in tiles_of(q))
                act.wait_ge(s("attended"), q + 1)
                ac(ctxT[:, 1, t * WT:t * WT + n, :].rearrange("p w h -> p (w h)"), bank[6 + q % 2][:, 0:H8 * n],
                   ACT.Identity, bias=col("kv_b", 1), scale=col("kv_g", 1)).then_inc(s("ctx_act"), 1)

            for q in range(STEPS + 3):
                if q < STEPS:
                    expo(q)
                if q >= 3:
                    ctx1(q - 3)

            act.wait_ge(s("mod_done"), 1)
            for m in range(KC):
                ac(h0T[:, m, :, 1:1 + HW], bank[3][:, m * C:(m + 1) * C].rearrange("p (i w) -> p i w", w=HW),
                   ACT.Identity, bias=col("mod_b", m)).then_inc(s("h0T_ready"), 1)
            act.wait_ge(s("lox_turned"), 1)
            ac(lnlT[:, 1, :], bank[5][:, 0:C], ACT.Identity, bias=col("gkv_b", 1), scale=col("gkv_g", 1))\
                .then_inc(s("lnlT_ready"), 1)
            act.wait_ge(s("gv_done"), 1)
            ac(gvT.rearrange("p k w -> p (k w)"), bank[6][:, :], ACT.Copy).then_inc(s("gvT_ready"), 1)
            act.wait_ge(s("g_shifted"), 1)
            ac(gattn[:, 1, :], gattn[:, 0, :], ACT.Exp, scale=C ** -0.5).then_inc(s("g_exp"), 1)

            groups = range(G)
            for g in groups:
                act.wait_ge(s("h0_major"), g + 1)
                ac(h[0:TR, TG * g:TG * (g + 1), :], bank[4 * g][0:TR, :].rearrange("p (u c) -> p u c", u=TG), ACT.Copy)\
                    .then_inc(s("h0_ready"), 1)

            def xT_copy(n):
                for g in groups:
                    act.wait_ge(s("x_turned"), G * n + g + 1)
                    ac(xT[:, g].rearrange("p k n -> p (k n)"), bank[4 * g + 1][:, 0:KC * GT], ACT.Copy)\
                        .then_inc(s("xT_ready"), 1)

            xT_copy(0)
            act.wait_ge(s("bhalf_ready"), 1)
            for g in groups:
                for m in range(KC):
                    act.wait_ge(s("gate_mm"), KC * (g + 1))
                    ac(gate_t[:, g, m, :], bank[4 * g + 2][:, m * GT:(m + 1) * GT], ACT.Tanh,
                       bias=b_in_half[:, m:m + 1], scale=0.5).then_inc(s("gate_tanh"), 1)
            for g in groups:
                for m in range(KC):
                    act.wait_ge(s("sv_mm"), KC * (g + 1))
                    ac(sv[:, g, m, :], bank[4 * g][:, m * GT:(m + 1) * GT], ACT.Tanh, bias=col("b_s", m))\
                        .then_inc(s("sv_tanh"), 1)
            xT_copy(1)
            xT_copy(2)
            for g in groups:
                act.wait_ge(s("v_done"), KC * (g + 1))
                for m in range(KC):
                    ac(vT[:, g, m, :], bank[4 * g + 2][:, m * GT:(m + 1) * GT], ACT.Identity, bias=col("v_b", m))\
                        .then_inc(s("vT_ready"), 1)
            for g in groups:
                for n in range(2):
                    act.wait_ge(s("lt_done"), NP2 * g + 4 * n + 4)
                    b = 4 * g + (1, 2)[n]
                    ac(ltT[:, g * GT:(g + 1) * GT, 4 * n + 2:4 * n + 4].rearrange("p n j -> p j n"),
                       bank[b][:, 0:2 * GT].rearrange("p (j n) -> p j n", j=2), ACT.Copy).then_inc(s("lt_act"), 1)
            for g in groups:
                act.wait_ge(s("att_shifted"), g + 1)
                a1 = att[1][:, g * GI:(g + 1) * GI].rearrange("p i a t -> p (i a t)")
                ac(a1, a1, ACT.Exp, scale=R ** -0.5).then_inc(s("att_exp"), 1)
            xT_copy(3)
            for g in groups:
                act.wait_ge(s("gate_done"), g + 1)
                ac(work8[0][:, g * GT:(g + 1) * GT], bank[4 * g + 2][0:E8, 0:GT], ACT.Tanh)\
                    .then_inc(s("gate_tanh2"), 1)
            act.wait_ge(s("gathered"), 1)
            act.wait_ge(s("ysT_clear"), 1)
            ac(ysT[:, 1, :, 0:CAP], bank[7][:, 0:TOK].rearrange("p (e c) -> p e c", e=E8), ACT.Identity,
               bias=col("ln_b", 1), scale=col("ln_g", 1)).then_inc(s("ysT_ready"), 1)

            def gelu(q):
                for c in range(2):
                    act.wait_ge(s("hid_biased"), 2 * q + c + 1)
                    hc = hid[q % 2][:, c * 512:(c + 1) * 512]
                    ac(hc, hc, ACT.Gelu_apprx_tanh).then_inc(s("hid_ready"), 1)

            gelu(0)
            for q in range(E8 // 2):
                if q + 1 < E8 // 2:
                    gelu(q + 1)
                act.wait_ge(s("hid_turned"), 2 * q + 2)
                if q >= 2:
                    act.wait_ge(s("eo_done"), q - 1)
                ac(hidT[q % 2][:, 4:8, :].rearrange("p f n -> p (f n)"), bank[3][:, :], ACT.Copy)\
                    .then_inc(s("hidT_act"), 1)

        @block.gpsimd
        def _(pool):
            pool.memset(zeros[:, :], 0.0).then_inc(s("constants_set"), 1)
            pool.memset(half, -0.5).then_inc(s("constants_set"), 1)
            pool.memset(eps, EPS).then_inc(s("constants_set"), 1)
            pool.wait_ge(s("constants_set"), 3)

            def rsqrt(ve, var, rs, name, parts=P):
                n = 1 + rsqrt.n
                rsqrt.n = n
                pool.tensor_scalar(ve, var, EPS, None, ALU.add).then_inc(s("eps_added"), 1)
                pool.wait_ge(s("eps_added"), n)
                pool.tensor_tensor(rs, ve, half[0:parts, 0:rs.shape[1]], ALU.pow).then_inc(s(name), 1)

            rsqrt.n = 0

            def rs_tile(t, j):
                pool.wait_ge(s("mv_ready"), t + 1)
                if not (isinstance(t, int) and t < RING):
                    pool.wait_ge(s("xhat_ready"), t - (RING - 1))
                pool.tensor_tensor(a_ve[j][0:TP], a_mv[j][0:TP, 1:2], eps[0:TP], ALU.add).then_inc(s("a_eps"), 1)
                pool.wait_ge(s("a_eps"), t + 1)
                pool.tensor_tensor(a_rs[j][0:TP], a_ve[j][0:TP], half[0:TP, 0:1], ALU.pow).then_inc(s("rs_ready"), 1)

            def keep_xhat(t, j):
                pool.wait_ge(s("xhat_ready"), t + 1)
                pool.tensor_copy(xhat_all[0:TP, t, :], xhat[j][0:TP]).then_inc(s("xall_done"), 1)

            for t in range(HEAD):
                rs_tile(t, t % RING)
                if t:
                    keep_xhat(t - 1, (t - 1) % RING)
                if t == 3:
                    pool.wait_ge(s("c_norm"), 2)
                    rsqrt(c_ve[0:1], c_mv[0:1, 1:2], c_rs[0:1], "c_rs_ready", parts=1)
            with pool.Fori(HEAD // RING, TILES // RING) as r:
                for j in range(RING):
                    rs_tile(RING * r + j, j)
                    keep_xhat(RING * r + (j - 1), (j - 1) % RING)
            for t in range(TAIL, TILES):
                rs_tile(t, t % RING)
                keep_xhat(t - 1, (t - 1) % RING)
            keep_xhat(TILES - 1, (TILES - 1) % RING)

            pool.wait_ge(s("w_mv_ready"), 2)
            rsqrt(w_ve, w_mv[:, :, 1], w_rs, "w_rs_ready")
            pool.wait_ge(s("layw_in"), 16 * 5)
            core = w_of(layw, LAYW, "core", parts=R)
            coreT = w_of(layw, LAYW, "coreT", parts=R)
            tree = h0T[0:R, :, :, :].rearrange("p k i t -> p (k i t)")[:, 0:NH // 2 * R]
            tree = tree.rearrange("p (n r) -> p n r", r=R)
            nh = 1

            def hstep(i):
                nonlocal nh
                nh += 1
                i.then_inc(s("head_steps"), 1)
                pool.wait_ge(s("head_steps"), nh)

            pool.tensor_tensor(core, core, coreT, ALU.add).then_inc(s("head_steps"), 1)
            hstep(pool.tensor_tensor(tree, heads[:, 0:NH // 2, :], heads[:, NH // 2:NH, :], ALU.add))
            n = NH // 4
            while n:
                hstep(pool.tensor_tensor(tree[:, 0:n, :], tree[:, 0:n, :], tree[:, n:2 * n, :], ALU.add))
                n //= 2
            hstep(pool.tensor_scalar(core, core, 0.5 / NH, None, ALU.mult))
            hstep(pool.tensor_scalar(tree[:, 0, :], tree[:, 0, :], 1.0 / NH, None, ALU.mult))
            hstep(pool.tensor_tensor(heads, heads, tree[:, 0:1, :].to_broadcast([R, NH, R]), ALU.subtract))
            pool.tensor_tensor(heads, heads, core.unsqueeze(1).to_broadcast([R, NH, R]), ALU.add)\
                .then_inc(s("heads_ready"), 1)
            for k in range(KC):
                pool.tensor_copy(h0T[:, k, :, 0], col("cls_tok", k).to_broadcast([P, IMAGES]))\
                    .then_inc(s("h0T_ready"), 1)
            pool.tensor_scalar(b_in_half, col("b_in", 0, KC), 0.5, None, ALU.mult).then_inc(s("bhalf_ready"), 1)

            for q in range(STEPS):
                _, n, u = tiles_of(q)[-1]
                rows, wide, j = H8 * n, n * NWIN, q % RING
                pool.wait_ge(s("rec_ready"), q + 1)
                if q >= RING:
                    pool.wait_ge(s("att_turned"), q - RING + 1)
                pool.tensor_tensor(s_att[j][0:rows, 0:u + 1, 0:wide], s_exp[j][0:rows, 0:u + 1, 0:wide],
                                   s_rec[j][0:rows, 0:u + 1].unsqueeze(2).to_broadcast([rows, u + 1, wide]),
                                   ALU.mult).then_inc(s("att_ready"), 1)

            pool.wait_ge(s("l_mv_ready"), 2)
            rsqrt(l_ve, l_mv[:, :, 1], l_rs, "l_rs_ready")

            def rs_tokens(n, g):
                sl = slice(TG * g, TG * (g + 1))
                pool.wait_ge(s("t_mv_ready"), TT * n + TG * (g + 1))
                rsqrt(t_ve[0:TR, sl], t_mv[0:TR, sl, 1], t_rs[0:TR, sl], "t_rs_ready", parts=TR)

            bo = w_of(layw, LAYW, "bo_row")[0:TR].unsqueeze(1).to_broadcast([TR, TG, C])
            ob = w_of(layw, LAYW, "ob_row")[0:TR].unsqueeze(1).to_broadcast([TR, TG, C])
            groups = range(G)
            part = lambda v, g: v[0:TR, TG * g:TG * (g + 1), :]
            for g in groups:
                rs_tokens(0, g)
            for g in groups:
                pool.wait_ge(s("xn_ready"), TG * (g + 1))
                pool.wait_ge(s("h0_ready"), g + 1)
                pool.tensor_tensor(part(base, g), part(h, g), part(xn, g), ALU.add).then_inc(s("base_step"), 1)
                pool.wait_ge(s("base_step"), g + 1)
                pool.tensor_tensor(part(base, g), part(base, g), bo, ALU.add).then_inc(s("base_ready"), 1)
            for n in (1, 2):
                for g in groups:
                    rs_tokens(n, g)
                if n == 1:
                    pool.wait_ge(s("h_ready"), G)
                    pool.memset(latD, 0.0).then_inc(s("latD_clear"), 1)
            for g in groups:
                pool.wait_ge(s("h_ready"), G + g + 1)
                pool.tensor_tensor(part(base, g), part(h, g), ob, ALU.add).then_inc(s("base_ready"), 1)
            for n in (3, 4):
                for g in groups:
                    rs_tokens(n, g)
            for g in groups:
                pool.wait_ge(s("h_ready"), 2 * G + g + 1)
                pool.wait_ge(s("xn_ready"), 3 * TT + TG * (g + 1))
                pool.tensor_tensor(part(base, g), part(h, g), part(xn, g), ALU.add).then_inc(s("base_ready"), 1)
            pool.wait_ge(s("slotT_ready"), 2)
            for t in range(TT):
                pool.wait_ge(s("pick_t"), t + 1)
                pool.tensor_tensor(wpick[0:TR, t, :, :], pick[0:TR, t, :, :],
                                   valT[0:TR, t, :].unsqueeze(2).to_broadcast([TR, E8, SW]), ALU.mult)\
                    .then_inc(s("wpick_t"), 1)


def chunked(w):
    w = np.asarray(w)
    return w.reshape(KC, P, -1).transpose(1, 0, 2).reshape(P, -1)


def packed(table, total, parts):
    out = np.zeros((P, total), np.float32)
    for name, a in parts.items():
        at, n = table[name]
        out[:a.shape[0], at:at + n] = a.reshape(a.shape[0], n)
    return out


def constants():
    rows = np.arange(H8 * WT)[:, None] // H8
    mask = np.where(np.arange(TP)[None] // NWIN == rows, 0.0, NEG)
    rows = np.arange(H8 * LASTW)[:, None] // H8
    mask_last = np.where(np.arange(LASTW * NWIN)[None] // NWIN == rows, 0.0, NEG)
    jt = np.arange(NP2 * T)
    causal = np.where(np.arange(T)[None] > (jt // NP2)[:, None], NEG, 0.0)
    chan = np.arange(P)
    spread = (jt[:, None, None] == np.arange(T)[None, :, None] * NP2 + chan[None, None] // HD)
    heads8 = np.arange(H8)[:, None, None] == (np.arange(KC)[:, None] * P + chan[None])[None] // DH
    headcol = (np.arange(KC)[None, :, None] * P + chan[:, None, None]) // DH == np.arange(H8)[None, None]
    f = lambda a: np.asarray(a, np.float32)
    return packed(CONS, CONS_N, {
        "ident": f(np.eye(P)), "pool": f((np.arange(TP)[:, None] // NWIN == np.arange(WT)[None]) / NWIN),
        "mask": f(mask), "mask_last": f(mask_last), "causal": f(causal),
        "slots": f(np.tile(np.arange(1, SW + 1), (P, 1))), "spread": f(spread), "heads8": f(heads8),
        "headcol": f(headcol), "mean": f(np.full((P, P), 1.0 / (C * C)))})


def kernel(**inputs):
    import concourse.bacc as _bacc
    from concourse.bass_utils import run_bass_kernel_spmd as _run

    g = {k: np.asarray(v) for k, v in inputs.items()}
    x = g["x"].reshape(IMAGES, 3, 2, CS, PATCH, 2, CS, PATCH)
    x = x.transpose(1, 4, 7, 0, 2, 5, 3, 6).reshape(PIX, WINDOWS * NWIN)
    full = np.zeros((KX * KP, TILES * TP), np.float32)
    full[:PIX, :WINDOWS * NWIN] = x
    xs = np.ascontiguousarray(full.reshape(KX, KP, TILES, TP).transpose(2, 1, 0, 3))
    cw = np.zeros((KX * KP, C), np.float32)
    cw[:PIX] = g["L0_tok_conv_w"].reshape(C, PIX).T
    cw = np.pad(cw.reshape(KX, KP, C).transpose(1, 0, 2).reshape(KP, KX * C), ((0, P - KP), (0, 0)))

    t = lambda n: g["L0_tok_" + n]
    tokw = packed(TOKW, TOKW_N, {
        "wq": chunked(t("la_wq")), "wkT": chunked(t("la_wkv")[:, :C].T), "wv": chunked(t("la_wkv")[:, C:]),
        "proj": chunked(t("la_proj_w")), "mod": chunked(t("mod_w")), "gwq": chunked(t("ga_wq")),
        "gwkT": chunked(t("ga_wkv")[:, :C].T), "gwv": chunked(t("ga_wkv")[:, C:]),
        "gproj": chunked(t("ga_proj_w"))})
    perm = np.arange(C).reshape(NP2, 2, HD).transpose(1, 0, 2).reshape(-1)
    basis = g["L1_attn_basis_w"].T
    layw = packed(LAYW, LAYW_N, {
        "w_in": chunked(g["L0_attn_W_in"].T), "w_s": chunked(g["L0_attn_W_s"].T),
        "w_o": chunked(g["L0_attn_W_o"].T), "tern": chunked(g["L0_ffn_weight"].T),
        "basis": chunked(np.concatenate([basis, basis], 1)), "v_w": chunked(g["L1_attn_v_w"].T[:, perm]),
        "o_w": chunked(g["L1_attn_o_w"].T[perm]), "gate": chunked(g["L1_ffn_gate_w"].T),
        "heads": g["L1_attn_head_residual"].transpose(1, 0, 2), "core": g["L1_attn_core"],
        "coreT": g["L1_attn_core"].T, "bo_row": np.tile(g["L0_attn_b_o"], (P, 1)),
        "ob_row": np.tile(g["L1_attn_o_b"], (P, 1))})
    cols = packed(COLS, COLS_N, {
        "q_g": chunked(t("la_ln_q_g")), "q_b": chunked(t("la_ln_q_b")), "kv_g": chunked(t("la_ln_kv_g")),
        "kv_b": chunked(t("la_ln_kv_b")), "proj_b": chunked(t("la_proj_b")), "mod_b": chunked(t("mod_b")),
        "gq_g": chunked(t("ga_ln_q_g")), "gq_b": chunked(t("ga_ln_q_b")), "gkv_g": chunked(t("ga_ln_kv_g")),
        "gkv_b": chunked(t("ga_ln_kv_b")), "gproj_b": chunked(t("ga_proj_b")),
        "class_emb": chunked(t("class_emb")), "cls_tok": chunked(g["cls_tok"].reshape(C)),
        "b_s": chunked(g["L0_attn_b_s"]), "v_b": chunked(g["L1_attn_v_b"][perm]),
        "ln_g": chunked(g["L1_ffn_ln_gamma"]), "ln_b": chunked(g["L1_ffn_ln_beta"]),
        "b_in": g["L0_attn_b_in"].reshape(2 * KC, P).T, "class_row": np.tile(t("class_emb"), (P, 1))})
    w1 = g["L1_ffn_fc1s"].reshape(E8, FF, KC, P).transpose(0, 3, 2, 1).reshape(E8, P, KC * FF)
    w2 = g["L1_ffn_fc2s"].reshape(E8, C, FC, P).transpose(0, 3, 2, 1).reshape(E8, P, FC * C)
    experts = np.ascontiguousarray(np.stack([w1, w2], 1).reshape(2 * E8, P, KC * FF))

    nc = _bacc.Bacc("TRN2", target_bir_lowering=False, num_devices=1)
    arrays = {"patches": xs, "conv_w": cw, "columns": cols, "constants": constants(),
              "tokenizer_w": tokw, "layer_w": layw, "experts": experts,
              "bias1": np.ascontiguousarray(g["L1_ffn_b1s"]), "bias2": np.ascontiguousarray(g["L1_ffn_b2s"])}
    args = [nc.dram_tensor(n, a.shape, F32, kind="ExternalInput").ap() for n, a in arrays.items()]
    o = nc.dram_tensor("tokens", (TOK, C), F32, kind="ExternalOutput").ap()
    build(nc, *args, o)
    r = _run(nc, [arrays], core_ids=[0])
    return r.results[0]["tokens"].reshape(IMAGES, T, C)
```

```python
from contextlib import ExitStack

import numpy as np

import concourse.bass as bass
from concourse import mybir

F32 = mybir.dt.float32
ALU = mybir.AluOpType
ACT = mybir.ActivationFunctionType
AX = mybir.AxisListType

P = 128
C = 256
KC = C // P
IMAGES, PATCH, SIDE, CS = 64, 14, 6, 3
HW = (SIDE // CS) ** 2
NWIN = CS * CS
WINDOWS = IMAGES * HW
PIX = 3 * PATCH * PATCH
KX, KP = 5, 118
WT = 14
TP = WT * NWIN
TILES = -(-WINDOWS // WT)
LASTW = WINDOWS - WT * (TILES - 1)
RING = 3
HEAD, MID = 2 * RING, 4 * RING
XH = -(-P // WT)
H8, DH = 8, 32
T = HW + 2
TOK = IMAGES * T
G = 2
GT, GI = TOK // G, IMAGES // G
TR = 96
TG = GT // TR
TT = TOK // TR
SW = 64
NH, HD, R = 16, 16, 64
NP2 = NH // 2
E8, FF, FC = 8, 1024, 8
CAP = TOK // E8
EPS = 1e-5
GELU_C, GELU_A = 0.7978845608028654, 0.044715
NEG = -1.0e30


STEPS = -(-TILES // 2)
HALF_DONE = -(-XH // 2) + 2


def tiles_of(q):
    return [(t, WT if t < TILES - 1 else LASTW, t % 2) for t in range(2 * q, min(2 * q + 2, TILES))]


def steps_until(q):
    return min(2 * q, TILES)


def offsets(sizes):
    at, out = 0, {}
    for name, n in sizes:
        out[name] = (at, n)
        at += n
    return out, at


TOKW, TOKW_N = offsets([(n, KC * C) for n in (
    "wq", "wkT", "wv", "proj", "mod", "gwq", "gwkT", "gwv", "gproj")])
LAYW, LAYW_N = offsets([("w_in", KC * 2 * C), ("w_s", KC * C), ("w_o", KC * C), ("tern", KC * C),
                        ("basis", KC * 2 * R), ("v_w", KC * C), ("o_w", KC * C), ("gate", KC * E8),
                        ("heads", NH * R), ("core", R), ("coreT", R), ("bo_row", C), ("ob_row", C)])
assert TOKW_N % 4 == 0
COLS, COLS_N = offsets([(n, KC) for n in (
    "q_g", "q_b", "kv_g", "kv_b", "proj_b", "mod_b", "gq_g", "gq_b", "gkv_g", "gkv_b", "gproj_b",
    "class_emb", "cls_tok", "b_s", "v_b", "ln_g", "ln_b")] + [("b_in", 2 * KC), ("class_row", C)])
NRES, NATT = 3, 3
PIECES = 2 * NRES
CONS, CONS_N = offsets([("ident", P), ("headcol", KC * H8), ("mask", TP), ("mask_last", LASTW * NWIN),
                        ("causal", T), ("slots", SW), ("spread", T * P), ("heads8", KC * P), ("mean", P)])
CONS_NOW = P + KC * H8


def build(nc, x_d, convw_d, cols_d, cons_d, tokw_d, layw_d, exp_d, b1_d, b2_d, out):
    ctx = ExitStack()
    with ctx:
        def sb(name, shape):
            return ctx.enter_context(nc.sbuf_tensor(name, shape, F32))

        def sem(name):
            return ctx.enter_context(nc.semaphore(name))

        bank = [ctx.enter_context(nc.psum_tensor(f"bank{i}", [P, 512], F32)) for i in range(8)]

        cols = sb("cols", [P, COLS_N])
        cons = sb("cons", [P, CONS_N])
        layw = sb("layw", [P, LAYW_N])
        resident = sb("resident_experts", [P, PIECES * KC * FF])
        attic = sb("attic", [P, TILES * C + KC * TILES * TP + KC * H8 * WINDOWS + RING * KX * TP])
        desk = sb("desk", [P, 12700])

        assert NH // 2 * R <= TILES * KX * WT

        def carve(tensor, at, *shape, parts=P):
            n = int(np.prod(shape))
            v = tensor[0:parts, at:at + n]
            names = "abcd"[:len(shape)]
            if len(shape) > 1:
                v = v.rearrange(f"p ({' '.join(names)}) -> p {' '.join(names)}",
                                **{k: s for k, s in zip(names, shape)})
            return v

        o = 0
        xhat_all = carve(attic, o, TILES, C); o += TILES * C
        winT = carve(attic, o, KC, TILES * TP); o += KC * TILES * TP
        qkT = carve(attic, o, KC, WINDOWS, H8)
        ctxT = qkT; o += KC * H8 * WINDOWS
        xt = [carve(attic, o + j * KX * TP, KX, TP) for j in range(RING)]; o += RING * KX * TP
        assert o <= attic.shape[1]

        o = 0
        tokw = desk[:, 0:TOKW_N]; o += TOKW_N
        convw = carve(desk, o, KX, C); o += KX * C
        pe_sb = [carve(desk, o + j * C, C) for j in range(RING)]; o += RING * C
        xhat = [carve(desk, o + j * C, C) for j in range(RING)]; o += RING * C
        redT = carve(desk, o, KC, WINDOWS); o += KC * WINDOWS
        redx = carve(desk, o, KC, C); o += KC * C
        lnrT = carve(desk, o, KC, WINDOWS); o += KC * WINDOWS
        qbd = [carve(desk, at, KC, 4, P) for at in (o, TOKW_N)]
        s_msk = [carve(desk, o + j * 2 * TP, 2, TP) for j in range(RING)]; o += 2 * RING * TP
        s_exp = [carve(desk, o + j * 2 * TP, 2, TP) for j in range(RING)]; o += 2 * RING * TP
        s_att = [carve(desk, o + j * 2 * TP, 2, TP) for j in range(RING)]; o += 2 * RING * TP
        s_attT = [carve(desk, o + j * 2 * P, 2, P) for j in range(RING)]; o += 2 * RING * P
        assert o <= desk.shape[1], o
        o = TOKW_N
        aggT = carve(desk, o, KC, WINDOWS); o += KC * WINDOWS
        localT = carve(desk, o, KC, WINDOWS); o += KC * WINDOWS
        lox = carve(desk, o, KC, C); o += KC * C
        lnlT = carve(desk, o, KC, WINDOWS); o += KC * WINDOWS
        assert o <= TOKW_N + KX * C + 2 * RING * C
        gvT = redx
        gprod = lnrT
        h0T = sb("h0T", [P, KC, IMAGES, T])
        gattn = sb("gattn", [H8, 3, WINDOWS])
        small = sb("small", [P, 900])
        zeros = sb("zeros", [P, C])
        sums = sb("window_sums", [P, TILES * KX * WT])
        xsum = carve(sums, 0, TILES, KX, WT)
        tree = carve(sums, 0, NH // 2, R, parts=R)
        small_row = sb("class_row_ln", [1, C])
        so = [0]

        def tiny(*shape, parts=P):
            v = carve(small, so[0], *shape, parts=parts)
            so[0] += int(np.prod(shape))
            return v

        a_st, a_mv, a_ve, a_rs = ([tiny(n) for _ in range(RING)] for n in (6, 2, 1, 1))
        half, eps = tiny(8), tiny(1)
        w_st, w_mv, w_ve, w_rs = tiny(2, 6), tiny(2, 2), tiny(2), tiny(2)
        l_st, l_mv, l_ve, l_rs = tiny(2, 6), tiny(2, 2), tiny(2), tiny(2)
        c_st, c_mv, c_ve, c_rs = tiny(6), tiny(2), tiny(1), tiny(1)
        c_lnT, c_q, c_qbd, c_qk = tiny(KC), tiny(KC), tiny(KC, H8), tiny(KC, H8)
        s_mx, s_nmx, s_sum, s_rec = ([tiny(2) for _ in range(RING)] for _ in range(4))
        g_mx, g_sum, g_rec = (tiny(IMAGES, parts=H8) for _ in range(3))
        gaggT = tiny(KC, IMAGES)
        t_st, t_mv, t_ve, t_rs = tiny(TT, 6), tiny(TT, 2), tiny(TT), tiny(TT)
        w_abs, w_scale = tiny(1), tiny(3)
        m8 = tiny(6, 8, parts=E8)
        slotT, valT = tiny(TT, E8), tiny(TT, E8)
        b_in_half, cls_fix = tiny(KC), tiny(KC)

        o = 0
        h = carve(desk, o, TT, C); o += TT * C
        xn = carve(desk, o, TT, C); o += TT * C
        base = carve(desk, o, TT, C); o += TT * C
        xT = carve(desk, o, G, KC, GT); o += KC * TOK
        U = o
        gate_t, keep, val, sv, gate_v, scanT = (carve(desk, U + i * KC * TOK, G, KC, GT) for i in range(6))
        tern_tmp = [carve(desk, U + 6 * KC * TOK + i * KC * C, KC * C) for i in range(2)]
        latD = carve(desk, o, IMAGES, 2, T); o += 2 * TOK
        latT = latD[0:R, :, 0, :]
        ltT = carve(desk, o, TOK, NP2); o += NP2 * TOK
        att = [carve(desk, o + i * 2 * TOK, IMAGES, 2, T, parts=NP2 * T) for i in range(2)]; o += 4 * TOK
        vT = carve(desk, o, G, KC, GT); o += KC * TOK
        yT = carve(desk, o, G, KC, GT); o += KC * TOK
        prod = [carve(desk, o + i * KC * GT, KC * GT) for i in range(RING)]; o += RING * KC * GT
        a_stat = carve(desk, o, 3, IMAGES * 2, parts=NP2 * T); o += 6 * IMAGES
        assert o <= desk.shape[1], o
        o = U
        val8 = carve(desk, o, TOK, parts=E8); o += TOK
        work8 = [carve(desk, o + i * TOK, TOK, parts=E8) for i in range(2)]; o += 2 * TOK
        sel8 = work8[1]
        ow = U
        opair = [carve(desk, ow + i * C, C) for i in range(2)]
        pick = carve(desk, o, TT, E8, SW)
        hid = [carve(desk, o + i * FF, FF) for i in range(2)]
        o += TT * E8 * SW
        wpick = carve(desk, o, TT, E8, SW)
        hidT = [carve(desk, o + i * FF, FC, P) for i in range(2)]
        o += TT * E8 * SW
        wpickT = carve(desk, o, E8 // 2, TOK); o += E8 // 2 * TOK
        xh2 = carve(desk, o, TT, C); o += TT * C
        ysT = carve(desk, o, KC, E8, SW); o += KC * E8 * SW
        assert o <= desk.shape[1], o
        o = NATT * 2 * KC * FF
        b1_rows = carve(attic, o, 2, FF); o += 2 * FF
        b2_rows = carve(attic, o, E8 // 2, C); o += E8 // 2 * C
        assert o <= attic.shape[1], o

        def expert_half(e, part):
            n = KC * FF
            if NRES <= e < NRES + NATT:
                at = (2 * (e - NRES) + part) * n
                return attic[:, at:at + n]
            at = (2 * (e if e < NRES else e - NRES - NATT) + part) * n
            return resident[:, at:at + n]

        def w_of(pack, table, name, *shape, parts=P):
            a, n = table[name]
            v = pack[0:parts, a:a + n]
            if shape:
                names = "abcd"[:len(shape)]
                v = v.rearrange(f"p ({' '.join(names)}) -> p {' '.join(names)}",
                                **{k: s for k, s in zip(names, shape)})
            return v

        def col(name, k=0, n=1, parts=P):
            a = COLS[name][0]
            return cols[0:parts, a + k:a + k + n]

        tw = {n: w_of(tokw, TOKW, n, KC, C) for n in TOKW}
        lw = {n: w_of(layw, LAYW, n, KC, s) for n, s in (
            ("w_in", 2 * C), ("w_s", C), ("w_o", C), ("tern", C), ("basis", 2 * R), ("v_w", C),
            ("o_w", C), ("gate", E8))}
        heads = w_of(layw, LAYW, "heads", NH, R, parts=R)
        ident = w_of(cons, CONS, "ident")
        mask = w_of(cons, CONS, "mask", parts=H8 * WT)
        mask_last = w_of(cons, CONS, "mask_last", parts=H8 * LASTW)
        causal = w_of(cons, CONS, "causal", parts=NP2 * T)
        slots = w_of(cons, CONS, "slots")
        spread = w_of(cons, CONS, "spread", T, P, parts=NP2 * T)
        heads8 = w_of(cons, CONS, "heads8", KC, P, parts=H8)
        headcol = w_of(cons, CONS, "headcol", KC, H8)
        mean_m = w_of(cons, CONS, "mean")

        S = {}

        def s(name):
            if name not in S:
                S[name] = sem(name)
            return S[name]

        half_banks = ((6, 7, 3), (4, 5, 2))
        conv_bank = bank[0:3]
        red_bank = bank[3:5]
        tr_bank = bank[5:8]

        block = ctx.enter_context(nc.Block())

        @block.sync
        def _(sp):
            def load_x(t, j, steady=True):
                if steady:
                    sp.wait_ge(s("conv_done"), t - (RING - 1))
                    sp.wait_ge(s("sums_done"), t - (RING - 1))
                sp.dma_start(xt[j][0:KP], x_d[t]).then_inc(s(f"x_in{j}"), 16)

            load_x(0, 0, False)
            for k in range(KX):
                sp.dma_start(convw[:, k, :], convw_d[:, k * C:(k + 1) * C]).then_inc(s("convw_in"), 16)
            sp.dma_start(cons[:, 0:CONS_NOW], cons_d[:, 0:CONS_NOW]).then_inc(s("cons_in"), 16)
            load_x(1, 1, False)
            sp.dma_start(cols[:, :], cols_d).then_inc(s("cols_in"), 16)
            load_x(2, 2, False)
            rounds = TILES // RING - 2
            part = TOKW_N // rounds
            with sp.Fori(1, rounds + 1) as r:
                for j in range(RING):
                    load_x(RING * r + j, j)
                    if j == RING - 1:
                        sp.dma_start(tokw[:, bass.ds((r - 1) * part, part)], tokw_d[:, bass.ds((r - 1) * part, part)])\
                          .then_inc(s("tokw_in"), 16)
            for t in range((rounds + 1) * RING, TILES):
                load_x(t, t % RING)
            sp.dma_start(cons[:, CONS_NOW:], cons_d[:, CONS_NOW:]).then_inc(s("cons_in"), 16)
            sp.dma_start(layw[:, :], layw_d).then_inc(s("layw_in"), 16)
            for i in range(PIECES):
                sp.dma_start(resident[:, i * KC * FF:(i + 1) * KC * FF], exp_d[i]).then_inc(s("resident_in"), 16)
            sp.wait_ge(s("agg_done"), 2)
            for q in range(E8 // 2):
                for side in range(2):
                    e = 2 * q + side
                    rows = slice(side * SW, (side + 1) * SW)
                    sp.dma_start(b2_rows[rows, q, :], b2_d[e:e + 1, :].to_broadcast([SW, C]))\
                      .then_inc(s("b2_in"), 16)
                    if q < 2:
                        sp.dma_start(b1_rows[rows, q, :], b1_d[e:e + 1, :].to_broadcast([SW, FF]))\
                          .then_inc(s(f"b1_in{q}"), 16)

            def load_b1(q):
                sp.wait_ge(s("hid_biased"), 2 * (q - 1))
                for side in range(2):
                    e = 2 * q + side
                    sp.dma_start(b1_rows[side * SW:(side + 1) * SW, q - 2, :], b1_d[e:e + 1, :].to_broadcast([SW, FF]))\
                      .then_inc(s(f"b1_in{q % 2}"), 16)

            def load_half(e, part, loaded):
                sp.dma_start(expert_half(e, part), exp_d[2 * e + part]).then_inc(s(loaded), 16)

            for e in range(NRES, NRES + NATT):
                for part in range(2):
                    load_half(e, part, f"expert_in{e}")
            load_b1(2)
            for part in range(2):
                sp.wait_ge(s(("hid_done", "eo_done")[part]), 2 - part)
                for e in range(NRES + NATT, E8):
                    load_half(e, part, f"last_w{part + 1}_in")
            load_b1(3)
            for g in range(G):
                sp.wait_ge(s("out_ready"), g + 1)
                sp.dma_start(out.rearrange("(t p) c -> p t c", p=TR)[:, g * TG:(g + 1) * TG, :],
                             base[0:TR, g * TG:(g + 1) * TG, :]).then_inc(s("out_sent"), 16)
            sp.wait_ge(s("out_sent"), 16 * G)

        @block.tensor
        def _(pe):
            mm = pe.matmul

            def keep_warm(b, n):
                for _ in range(n):
                    mm(bank[b][:, 0:C], zeros[:, 0:P], zeros[:, :], start=True, stop=True)

            pe.wait_ge(s("constants_set"), 1)

            def conv(r, j):
                t = RING * r + j
                pe.wait_ge(s(f"x_in{j}"), 16 * r + 16)
                if not (isinstance(t, int) and t < RING):
                    pe.wait_ge(s("pe_copied"), t - (RING - 1))
                for k in range(KX):
                    i = mm(conv_bank[j][0:TP, 0:C], xt[j][0:KP, k, :], convw[0:KP, k, :],
                           start=(k == 0), stop=(k == KX - 1))
                i.then_inc(s("conv_done"), 1)

            def window_means(w):
                a, b = ((0, XH), (XH, TILES))[w]
                pe.wait_ge(s("sums_done"), b)
                for m in range(KC):
                    for k in range(KX):
                        i = mm(red_bank[w][:, m * C:m * C + (b - a) * WT], convw[0:KP, k, m * P:(m + 1) * P],
                               xsum[0:KP, a:b, k, :], start=(k == 0), stop=(k == KX - 1))
                i.then_inc(s("means_done"), 1)

            def turn(t, j):
                pe.wait_ge(s("xhat_ready"), t + 1)
                if not (isinstance(t, int) and t < RING):
                    pe.wait_ge(s("winT_ready"), t - (RING - 1))
                for k in range(KC):
                    i = pe.transpose(tr_bank[j][:, k * P:k * P + TP], xhat[j][0:TP, k * P:(k + 1) * P],
                                     ident[0:TP, 0:TP])
                i.then_inc(s("turned"), 1)

            keep_warm(7, 5)
            pe.wait_ge(s("convw_in"), 16 * KX)
            for t in range(HEAD):
                conv(t // RING, t % RING)
                if t == 0:
                    pe.wait_ge(s("cons_in"), 16)
                if t >= 2:
                    turn(t - 2, (t - 2) % RING)
            with pe.Fori(HEAD // RING, MID // RING) as r:
                for j in range(RING):
                    conv(r, j)
                    turn(RING * r + (j - 2), (j - 2) % RING)

            def means_major(w):
                pe.wait_ge(s("redT_ready"), w + 1)
                for k in range(KC):
                    i = pe.transpose(red_bank[w][:, k * P:(k + 1) * P], redT[:, k, w * P:(w + 1) * P], ident)
                i.then_inc(s("red_major"), 1)

            def means_back(w):
                pe.wait_ge(s("redx_ready"), w + 1)
                for k in range(KC):
                    i = pe.transpose(red_bank[w][:, k * P:(k + 1) * P], redx[:, w, k * P:(k + 1) * P], ident)
                i.then_inc(s("redx_turned"), 1)

            def queries(w):
                pe.wait_ge(s("lnrT_ready"), 2 * (w + 1))
                for m in range(KC):
                    for k in range(KC):
                        i = mm(red_bank[w][:, m * P:(m + 1) * P], tw["wq"][:, k, m * P:(m + 1) * P],
                               lnrT[:, k, w * P:(w + 1) * P], start=(k == 0), stop=(k == KC - 1))
                i.then_inc(s("q_done"), 1)

            def project_keys(w, m, banks):
                pe.wait_ge(s("qbd_ready"), KC * w + m + 1)
                for k in range(KC):
                    mm(bank[banks[k]][:, :], tw["wkT"][:, m, k * P:(k + 1) * P],
                       qbd[w][:, m, :, :], start=True, stop=True).then_inc(s("qk_done"), 1)

            cbank = red_bank[0]
            for t in range(MID, TILES):
                if t == TILES - 1:
                    window_means(1)
                conv(t // RING, t % RING)
                turn(t - 2, (t - 2) % RING)
                if t == MID:
                    window_means(0)
                if t == MID + 1:
                    pe.wait_ge(s("c_norm"), 3)
                    pe.wait_ge(s("redT_ready"), 1)
                    for k in range(KC):
                        i = mm(cbank[:, 2 * P + k:2 * P + k + 1], small_row[0:1, k * P:(k + 1) * P],
                               ident[0:1, 0:1], start=True, stop=True)
                    i.then_inc(s("c_turned"), 1)
                    means_major(0)
                if t == MID + 3:
                    pe.wait_ge(s("c_ln"), 2)
                    pe.wait_ge(s("tokw_in"), 16 * (TILES // RING - 2))
                    for m in range(KC):
                        for k in range(KC):
                            i = mm(cbank[:, 2 * P + 8 + m:2 * P + 9 + m], tw["gwq"][:, k, m * P:(m + 1) * P],
                                   c_lnT[:, k:k + 1], start=(k == 0), stop=(k == KC - 1))
                    i.then_inc(s("c_q_done"), 1)
                    means_back(0)
                if t == MID + 4:
                    pe.wait_ge(s("c_qbd"), 2)
                    for k in range(KC):
                        for m in range(KC):
                            i = mm(cbank[:, 2 * P + 16 + k * H8:2 * P + 16 + (k + 1) * H8],
                                   tw["gwkT"][:, m, k * P:(k + 1) * P], c_qbd[:, m, :],
                                   start=(m == 0), stop=(m == KC - 1))
                    i.then_inc(s("c_qk_done"), 1)
                    queries(0)
            means_major(1)
            pe.wait_ge(s("pe_copied"), TILES)
            project_keys(0, 0, (1, 2))
            turn(TILES - 2, (TILES - 2) % RING)
            turn(TILES - 1, (TILES - 1) % RING)
            pe.wait_ge(s("winT_ready"), TILES - 2)
            project_keys(0, 1, (0, 6))
            means_back(1)

            def scores(q):
                if q == 0:
                    pe.wait_ge(s("qk_dve"), 2)
                    pe.wait_ge(s("qk_act"), 2)
                if q >= 2:
                    pe.wait_ge(s("masked"), steps_until(q - 1))
                for t, n, u in tiles_of(q):
                    for k in range(KC):
                        i = mm(bank[q % 2][0:H8 * n, u * TP:u * TP + n * NWIN], qkT[:, k, t * WT:t * WT + n, :],
                               winT[:, k, t * TP:t * TP + n * NWIN], start=(k == 0), stop=(k == KC - 1))
                i.then_inc(s("scored"), 1)

            def turn_att(q):
                pe.wait_ge(s("att_ready"), q + 1)
                if q >= 1:
                    pe.wait_ge(s("attT_ready"), q)
                for t, n, u in tiles_of(q):
                    i = pe.transpose(bank[2][0:n * NWIN, u * P:u * P + H8 * n],
                                     s_att[q % RING][0:H8 * n, u, 0:n * NWIN], ident[0:H8 * n, 0:H8 * n])
                i.then_inc(s("att_turned"), 1)

            def attend(q):
                pe.wait_ge(s("attT_ready"), q + 1)
                if q == 0:
                    pe.wait_ge(s("xall_done"), TILES)
                    pe.wait_ge(s("qk_dve"), 4)
                    pe.wait_ge(s("qk_act"), 4)
                if q >= 1:
                    pe.wait_ge(s("ctx_act"), q)
                    pe.wait_ge(s("ctx_dve"), q)
                for k in range(KC):
                    for t, n, u in tiles_of(q):
                        i = mm(bank[4 + k][:, u * H8 * WT:u * H8 * WT + H8 * n],
                               xhat_all[0:n * NWIN, t, k * P:(k + 1) * P],
                               s_attT[q % RING][0:n * NWIN, u, 0:H8 * n], start=True, stop=True)
                i.then_inc(s("attended"), 1)

            def values(w):
                pe.wait_ge(s("ctx_act"), (HALF_DONE - 2, STEPS)[w])
                pe.wait_ge(s("ctx_dve"), (HALF_DONE - 2, STEPS)[w])
                for m in range(KC):
                    for k in range(KC):
                        for g in range(4):
                            hh = 4 * m + g
                            i = mm(bank[half_banks[w][0]][g * DH:(g + 1) * DH, m * P:(m + 1) * P],
                                   tw["wv"][:, k, hh * DH:(hh + 1) * DH], ctxT[:, k, w * P:(w + 1) * P, hh],
                                   start=(k == 0), stop=(k == KC - 1))
                i.then_inc(s("agg_done"), 1)

            def project(b, w_, src, w, width, name):
                for m in range(KC):
                    for k in range(KC):
                        i = mm(bank[b][:, m * width:(m + 1) * width], w_[:, k, m * P:(m + 1) * P],
                               src[:, k, w * width:(w + 1) * width], start=(k == 0), stop=(k == KC - 1))
                i.then_inc(s(name), 1)

            def local_proj(w):
                pe.wait_ge(s("aggT_ready"), w + 1)
                project(half_banks[w][1], tw["proj"], aggT, w, P, "proj_done")

            def local_major(w):
                pe.wait_ge(s("local_ready"), KC * (w + 1))
                for k in range(KC):
                    i = pe.transpose(bank[half_banks[w][2]][:, k * P:(k + 1) * P], localT[:, k, w * P:(w + 1) * P],
                                     ident)
                i.then_inc(s("lo_major"), 1)
                project(half_banks[w][0], tw["mod"], localT, w, P, "mod_done")

            def local_back(w):
                pe.wait_ge(s("lox_ready"), w + 1)
                for k in range(KC):
                    i = pe.transpose(bank[half_banks[w][2]][:, k * P:(k + 1) * P], lox[:, w, k * P:(k + 1) * P],
                                     ident)
                i.then_inc(s("lox_turned"), 1)

            def global_scores(w):
                pe.wait_ge(s("lnlT_ready"), KC * (w + 1))
                pe.wait_ge(s("c_qk_ready"), 1)
                for k in range(KC):
                    i = mm(bank[half_banks[w][1]][0:H8, 0:P], c_qk[:, k, :], lnlT[:, k, w * P:(w + 1) * P],
                           start=(k == 0), stop=(k == KC - 1))
                i.then_inc(s("gscored"), 1)

            def global_values(w):
                pe.wait_ge(s("h0T_act"), KC * (w + 1))
                project(half_banks[w][0], tw["gwv"], lnlT, w, P, "gv_done")

            def global_spread(w):
                pe.wait_ge(s("gattn_ready"), w + 1)
                for m in range(KC):
                    i = mm(bank[half_banks[w][1]][:, m * P:(m + 1) * P], heads8[:, m, :],
                           gattn[:, 2, w * P:(w + 1) * P], start=True, stop=True)
                i.then_inc(s("gspread"), 1)

            def global_proj(w):
                pe.wait_ge(s("gagg_ready"), w + 1)
                project(half_banks[w][1], tw["gproj"], gaggT, w, GI, "gproj_done")

            h0T_v = h0T[:, :, :, :].rearrange("p k i t -> p k (i t)")

            def tokens_major(g):
                pe.wait_ge(s("cls_set"), KC)
                pe.wait_ge(s("h0T_act"), KC * (g + 1))
                pe.wait_ge(s("h0T_dve"), KC * (g + 1))
                for u in range(TG):
                    for k in range(KC):
                        a = g * GT + u * TR
                        i = pe.transpose(bank[4 * g][0:TR, u * C + k * P:u * C + (k + 1) * P],
                                         h0T_v[:, k, a:a + TR], ident)
                i.then_inc(s("h0_major"), 1)

            for q in range(STEPS + 3):
                if q == 0:
                    pe.wait_ge(s("winT_ready"), TILES)
                if q == 1:
                    queries(1)
                if q < STEPS:
                    scores(q)
                if q == 1:
                    project_keys(1, 0, (5, 6))
                    project_keys(1, 1, (7, 4))
                if q == HALF_DONE + 1:
                    values(0)
                if q == HALF_DONE + 2:
                    local_proj(0)
                if q == HALF_DONE + 3:
                    local_major(0)
                if 2 <= q < STEPS + 2:
                    turn_att(q - 2)
                if q >= 3:
                    attend(q - 3)
            local_back(0)
            values(1)
            global_scores(0)
            local_proj(1)
            global_values(0)
            pe.wait_ge(s("w_abs_ready"), 1)
            mm(bank[0][:, 0:1], mean_m, w_abs, start=True, stop=True).then_inc(s("w_mean_done"), 1)
            local_major(1)
            global_spread(0)
            keep_warm(1, 1)
            local_back(1)
            global_proj(0)
            global_scores(1)
            global_values(1)
            tokens_major(0)
            keep_warm(1, 1)
            global_spread(1)
            keep_warm(1, 1)
            global_proj(1)
            tokens_major(1)

            def turn_x(n, g):
                pe.wait_ge(s("xn_ready"), TT * n + TG * (g + 1))
                for u in range(TG):
                    for k in range(KC):
                        i = pe.transpose(bank[4 * g + 1][:, k * GT + u * TR:k * GT + (u + 1) * TR],
                                         xn[0:TR, TG * g + u, k * P:(k + 1) * P], ident[0:TR, 0:TR])
                i.then_inc(s("x_turned"), 1)

            def channels(b, at, w, cols_, src, done=None):
                for k in range(KC):
                    i = mm(bank[b][:, at:at + GT], w[:, k, cols_:cols_ + P], src[:, k, :],
                           start=(k == 0), stop=(k == KC - 1))
                if done:
                    i.then_inc(s(done), 1)

            def tokens(b, srcT, w, done):
                for u in range(TG):
                    for k in range(KC):
                        i = mm(bank[b][0:TR, u * C:(u + 1) * C], srcT[:, k, u * TR:(u + 1) * TR], w[:, k, :],
                               start=(k == 0), stop=(k == KC - 1))
                i.then_inc(s(done), 1)

            groups = range(G)
            pe.wait_ge(s("layw_in"), 16)
            for g in groups:
                turn_x(0, g)
                if g == 0:
                    keep_warm(7, 2)
                pe.wait_ge(s("xT_ready"), g + 1)
                for m in range(KC):
                    channels(4 * g + 3, m * GT, lw["w_in"], C + m * P, xT[:, g], "val_mm")
                for m in range(KC):
                    channels(4 * g + 2, m * GT, lw["w_in"], m * P, xT[:, g], "gate_mm")
            for g in groups:
                pe.wait_ge(s("val_ready"), KC * (g + 1))
                for m in range(KC):
                    channels(4 * g, m * GT, lw["w_s"], m * P, val[:, g], "sv_mm")
            keep_warm(7, 3)
            for g in groups:
                pe.wait_ge(s("scan_ready"), g + 1)
                tokens(4 * g + 1, scanT[:, g], lw["w_o"], "mix_done")
            keep_warm(7, 8)
            for g in groups:
                turn_x(1, g)
            for g in groups:
                pe.wait_ge(s("xT_ready"), G + g + 1)
                if g == 0:
                    pe.wait_ge(s("tern_ready"), 1)
                tokens(4 * g + 2, xT[:, g], lw["tern"], "tern_done")
            keep_warm(7, 9)
            for g in groups:
                turn_x(2, g)
            for g in groups:
                pe.wait_ge(s("xT_ready"), 2 * G + g + 1)
                channels(4 * g + 3, 0, lw["basis"], 0, xT[:, g], "lat_done")
                for m in range(KC):
                    channels(4 * g + 2, m * GT, lw["v_w"], m * P, xT[:, g], "v_done")
            pe.wait_ge(s("heads_ready"), 1)
            for g in groups:
                pe.wait_ge(s("lat_ready"), 2 * (g + 1))
                for j in range(NP2):
                    if j == 4:
                        pe.wait_ge(s("vT_ready"), 2 * (g + 1))
                    mm(bank[4 * g + (0, 1, 3, 2)[j // 2]][:, (j % 2) * GT:(j % 2 + 1) * GT],
                       heads[:, 2 * j:2 * j + 2, :], latT[:, g * GI:(g + 1) * GI, :], start=True, stop=True)\
                        .then_inc(s("lt_done"), 1)
            for g in groups:
                pe.wait_ge(s("lt_act"), 2 * (g + 1))
                pe.wait_ge(s("lt_dve"), 2 * (g + 1))
                for i_ in range(GI):
                    im = g * GI + i_
                    i = mm(bank[4 * g][0:NP2 * T, i_ * 2 * T:(i_ + 1) * 2 * T],
                           ltT[:, im * T:(im + 1) * T, :], latD[:, im, :, :], start=True, stop=True)
                i.then_inc(s("att_scored"), 1)
            keep_warm(3, 3)
            for g in groups:
                pe.wait_ge(s("att_probs"), g + 1)
                for t in range(T):
                    if g == 1 and t == T - 1:
                        turn_x(3, 0)
                    if g == 1 and t >= 2:
                        keep_warm(3, 1)
                    if t >= 3:
                        pe.wait_ge(s("y_mul"), T * g + t - 2)
                    for p in range(2):
                        i = mm(bank[4 * g + 1 + t % 3][:, p * GT:p * GT + GI * (t + 1)], spread[:, t, :],
                               att[0][:, g * GI:(g + 1) * GI, p, 0:t + 1], start=True, stop=True)
                    i.then_inc(s("spread_done"), 1)
                if g == 0:
                    pe.wait_ge(s("y_ready"), T - 1)
                    tokens(0, yT[:, 0], lw["o_w"], "lat_out_done")
            keep_warm(3, 1)
            pe.wait_ge(s("y_ready"), (T - 1) * G)
            tokens(4, yT[:, 1], lw["o_w"], "lat_out_done")
            keep_warm(7, 5)
            turn_x(3, 1)
            for g in groups:
                pe.wait_ge(s("xT_ready"), 3 * G + g + 1)
                for k in range(KC):
                    i = mm(bank[4 * g + 2][0:E8, 0:GT], lw["gate"][:, k, :], xT[:, g, k, :],
                           start=(k == 0), stop=(k == KC - 1))
                i.then_inc(s("gate_done"), 1)
            keep_warm(3, 24)
            pe.wait_ge(s("slots_ready"), 1)
            for t in range(TT):
                pe.transpose(bank[4][0:TR, t * 16:t * 16 + E8], sel8[:, t * TR:(t + 1) * TR], ident[0:E8, 0:E8])
                i = pe.transpose(bank[4][0:TR, t * 16 + E8:t * 16 + 2 * E8], val8[:, t * TR:(t + 1) * TR],
                                 ident[0:E8, 0:E8])
            i.then_inc(s("slots_turned"), 1)
            keep_warm(3, 2)
            pe.wait_ge(s("xn_ready"), 5 * TT)
            for t in range(TT):
                pe.wait_ge(s("pick_t"), t + 1)
                for k in range(KC):
                    i = mm(bank[6 + k][:, 0:TOK], xh2[0:TR, t, k * P:(k + 1) * P],
                           pick[0:TR, t, :, 0:CAP], start=(t == 0), stop=(t == TT - 1))
            i.then_inc(s("gathered"), 1)

            def turn_weights(q):
                for t in range(TT):
                    pe.wait_ge(s("wpick_t"), t + 1)
                    i = pe.transpose(bank[4 + q][:, t * TR:(t + 1) * TR], wpick[0:TR, t, 2 * q:2 * q + 2, :],
                                     ident[0:TR, 0:TR])
                i.then_inc(s("wpick_turned"), 1)

            def hidden(q):
                for side in range(2):
                    e = 2 * q + side
                    if e < NRES:
                        pe.wait_ge(s("resident_in"), 16 * PIECES)
                    elif e < NRES + NATT:
                        pe.wait_ge(s(f"expert_in{e}"), 32)
                    else:
                        pe.wait_ge(s("last_w1_in"), 32)
                if q >= 1:
                    pe.wait_ge(s("hid_biased"), 2 * q)
                for c in range(2):
                    for k in range(KC):
                        for side in range(2):
                            e = 2 * q + side
                            w1 = expert_half(e, 0).rearrange("p (k f) -> p k f", k=KC)
                            i = mm(bank[c][side * SW:(side + 1) * SW, :], ysT[:, k, e, :],
                                   w1[:, k, c * 512:(c + 1) * 512], start=(k == 0), stop=(k == KC - 1))
                    i.then_inc(s("hid_done"), 1)

            def turn_hidden(q):
                for c in range(2):
                    pe.wait_ge(s("hid_ready"), 2 * q + c + 1)
                    if q >= 1:
                        pe.wait_ge(s("hidT_dve" if c == 0 else "hidT_act"), q)
                    for f in range(4):
                        i = pe.transpose(bank[2 + c][:, f * P:(f + 1) * P],
                                         hid[q % 2][:, (4 * c + f) * P:(4 * c + f + 1) * P], ident)
                    i.then_inc(s("hid_turned"), 1)

            def outputs(q):
                if q >= 1:
                    pe.wait_ge(s("opair_ready"), q)
                if 2 * q >= NRES + NATT:
                    pe.wait_ge(s("last_w2_in"), 32)
                for f in range(FC):
                    if f == 0:
                        pe.wait_ge(s("hidT_dve"), q + 1)
                    if f == 4:
                        pe.wait_ge(s("hidT_act"), q + 1)
                    for side in range(2):
                        w2 = expert_half(2 * q + side, 1).rearrange("p (f c) -> p f c", f=FC)
                        i = mm(bank[4][side * SW:(side + 1) * SW, 0:C], hidT[q % 2][:, f, side * SW:(side + 1) * SW],
                               w2[:, f, :], start=(f == 0), stop=(f == FC - 1))
                i.then_inc(s("eo_done"), 1)

            def combine(q, g):
                pe.wait_ge(s("opair_ready"), q + 1)
                for t in range(TG * g, TG * (g + 1)):
                    i = mm(bank[5 + t // TG][0:TR, (t % TG) * C:(t % TG + 1) * C], wpickT[:, q, t * TR:(t + 1) * TR],
                           opair[q % 2], start=(q == 0 and t % TG == 0), stop=(q == E8 // 2 - 1),
                           skip_group_check=True)
                    if t % TG == TG - 1:
                        i.then_inc(s("combined"), 1)

            keep_warm(3, 2)
            pe.wait_ge(s("ysT_ready"), 2)
            hidden(0)
            for q in range(E8 // 2):
                turn_weights(q)
            for q in range(E8 // 2):
                if q + 1 < E8 // 2:
                    hidden(q + 1)
                turn_hidden(q)
                if q == 0:
                    pe.wait_ge(s("wpickT_ready"), E8 // 2)
                if q:
                    combine(q - 1, 0)
                outputs(q)
                if q:
                    combine(q - 1, 1)
            for g in groups:
                combine(E8 // 2 - 1, g)

        @block.vector
        def _(dve):
            ts, tt, stt = dve.tensor_scalar, dve.tensor_tensor, dve.scalar_tensor_tensor

            def stats(t, j):
                dve.wait_ge(s("pe_copied"), t + 1)
                dve.bn_stats(a_st[j][0:TP], pe_sb[j][0:TP]).then_inc(s("bn_done"), 1)

            def norm(t, j):
                dve.wait_ge(s("rs_ready"), t + 1)
                if not (isinstance(t, int) and t < RING):
                    dve.wait_ge(s("turned"), t - (RING - 1))
                    dve.wait_ge(s("xall_done"), t - (RING - 1))
                ts(xhat[j][0:TP], pe_sb[j][0:TP], a_mv[j][0:TP, 0:1], a_rs[j][0:TP], ALU.subtract, ALU.mult)\
                    .then_inc(s("xhat_ready"), 1)

            def window_sums(t, j, n):
                dve.wait_ge(s(f"x_in{j}"), 16 * n + 16)
                dve.tensor_reduce(sums[0:KP][:, bass.ds(t * (KX * WT), KX * WT)],
                                  xt[j][0:KP].rearrange("p k (w n) -> p (k w) n", n=NWIN), AX.X, ALU.add)\
                    .then_inc(s("sums_done"), 1)

            def patch_step(t, j, first=False):
                stats(t, j)
                dve.wait_ge(s("bn_done"), t + 1)
                if not first:
                    norm(t - 1, (j - 1) % RING)
                dve.bn_aggr(a_mv[j][0:TP], a_st[j][0:TP]).then_inc(s("mv_ready"), 1)

            class_row = cols[0:1, COLS["class_row"][0]:COLS["class_row"][0] + C]
            for t in range(HEAD):
                window_sums(t, t % RING, t // RING)
                patch_step(t, t % RING, t == 0)
                if t == 2:
                    dve.wait_ge(s("cols_in"), 16)
                    dve.bn_stats(c_st[0:1], class_row).then_inc(s("c_norm"), 1)
                    dve.wait_ge(s("c_norm"), 1)
                    dve.bn_aggr(c_mv[0:1], c_st[0:1]).then_inc(s("c_norm"), 1)
                if t == 4:
                    dve.wait_ge(s("c_rs_ready"), 1)
                    ts(small_row[0:1, :], class_row, c_mv[0:1, 0:1], c_rs[0:1], ALU.subtract, ALU.mult)\
                        .then_inc(s("c_norm"), 1)
            with dve.Fori(HEAD // RING, MID // RING) as r:
                for j in range(RING):
                    window_sums(RING * r + j, j, r)
                    patch_step(RING * r + j, j)
            halves = ((0, XH * WT), (XH * WT, WINDOWS))

            def means_out(w):
                a, b = halves[w]
                dve.wait_ge(s("means_done"), w + 1)
                ts(redT[:, :, a:b], red_bank[w][:, :].rearrange("p (k w) -> p k w", k=KC)[:, :, 0:b - a],
                   1.0 / NWIN, None, ALU.mult).then_inc(s("redT_ready"), 1)

            def means_stats(w):
                dve.wait_ge(s("red_major"), w + 1)
                dve.bn_stats(w_st[:, w, :], red_bank[w][:, 0:C]).then_inc(s("bn2_done"), 1)
                dve.wait_ge(s("bn2_done"), w + 1)
                dve.bn_aggr(w_mv[:, w, :], w_st[:, w, :]).then_inc(s("win_mv_ready"), 1)

            def means_norm(w):
                dve.wait_ge(s("win_rs_ready"), w + 1)
                ts(redx[:, w, :], red_bank[w][:, 0:C], w_mv[:, w, 0:1], w_rs[:, w:w + 1],
                   ALU.subtract, ALU.mult).then_inc(s("redx_ready"), 1)

            def means_affine(w):
                dve.wait_ge(s("redx_turned"), w + 1)
                for k in range(KC):
                    ts(lnrT[:, k, w * P:(w + 1) * P], red_bank[w][:, k * P:(k + 1) * P], col("q_g", k),
                       col("q_b", k), ALU.mult, ALU.add).then_inc(s("lnrT_ready"), 1)

            def queries_apart(w):
                dve.wait_ge(s("q_done"), w + 1)
                for m in range(KC):
                    tt(qbd[w][:, m, :, :], red_bank[w][:, m * P:(m + 1) * P].unsqueeze(1).to_broadcast([P, 4, P]),
                       headcol[:, m, 4 * m:4 * m + 4].unsqueeze(2).to_broadcast([P, 4, P]), ALU.mult)\
                        .then_inc(s("qbd_ready"), 1)

            def keys_out(w, m):
                b = ((1, 0), (5, 7))[w][m]
                dve.wait_ge(s("qk_done"), 4 * w + 2 * m + 1)
                dve.tensor_copy(qkT[:, 0, w * P:(w + 1) * P, 4 * m:4 * m + 4].rearrange("p w g -> p g w"),
                                bank[b][:, :].rearrange("p (g w) -> p g w", g=4)).then_inc(s("qk_dve"), 1)

            window_sums(MID, MID % RING, MID // RING)
            for t in range(MID, TILES):
                if t + 1 < TILES:
                    window_sums(t + 1, (t + 1) % RING, (t + 1) // RING)
                else:
                    means_out(1)
                if t == MID + 2:
                    means_norm(0)
                    dve.wait_ge(s("c_turned"), 1)
                    for k in range(KC):
                        ts(c_lnT[:, k:k + 1], red_bank[0][:, 2 * P + k:2 * P + k + 1], col("gq_g", k),
                           col("gq_b", k), ALU.mult, ALU.add).then_inc(s("c_ln"), 1)
                patch_step(t, t % RING)
                if t == MID:
                    means_out(0)
                if t == MID + 1:
                    means_stats(0)
                if t == MID + 3:
                    means_affine(0)
                    dve.wait_ge(s("cons_in"), 16)
                    dve.wait_ge(s("c_q_done"), 1)
                    for k in range(KC):
                        ts(c_qbd[:, k, :], headcol[:, k, :], red_bank[0][:, 2 * P + 8 + k:2 * P + 9 + k], None,
                           ALU.mult).then_inc(s("c_qbd"), 1)
                if t == MID + 5:
                    dve.wait_ge(s("c_qk_done"), 1)
                    queries_apart(0)
                    dve.tensor_copy(c_qk.rearrange("p k h -> p (k h)"), red_bank[0][:, 2 * P + 16:2 * P + 16 + KC * H8])\
                        .then_inc(s("c_qk_ready"), 1)
            means_stats(1)
            norm(TILES - 1, (TILES - 1) % RING)
            keys_out(0, 0)
            means_norm(1)
            keys_out(0, 1)
            means_affine(1)

            def masked(q):
                j = q % RING
                dve.wait_ge(s("scored"), q + 1)
                if q == 0:
                    dve.wait_ge(s("cons_in"), 32)
                if q >= RING:
                    dve.wait_ge(s("s_exp_ready"), steps_until(q - RING + 1))
                for t, n, u in tiles_of(q):
                    rows, wide = H8 * n, n * NWIN
                    mk = mask if n == WT else mask_last
                    dve.tensor_tensor_reduce(s_msk[j][0:rows, u, 0:wide], bank[q % 2][0:rows, u * TP:u * TP + wide],
                                             mk[0:rows, 0:wide], 1.0, NEG, ALU.add, ALU.max,
                                             s_mx[j][0:rows, u:u + 1]).then_inc(s("masked"), 1)
                dve.wait_ge(s("masked"), steps_until(q + 1))
                _, n, u = tiles_of(q)[-1]
                ts(s_nmx[j][0:H8 * n, 0:u + 1], s_mx[j][0:H8 * n, 0:u + 1], -C ** -0.5, None, ALU.mult)\
                    .then_inc(s("nmx_ready"), 1)

            def recip(q):
                _, n, u = tiles_of(q)[-1]
                dve.wait_ge(s("s_exp_ready"), steps_until(q + 1))
                if q >= RING:
                    dve.wait_ge(s("att_ready"), q - RING + 1)
                dve.reciprocal(s_rec[q % RING][0:H8 * n, 0:u + 1], s_sum[q % RING][0:H8 * n, 0:u + 1])\
                    .then_inc(s("rec_ready"), 1)

            def attT(q):
                _, n, u = tiles_of(q)[-1]
                dve.wait_ge(s("att_turned"), q + 1)
                if q >= RING:
                    dve.wait_ge(s("attended"), q - RING + 1)
                dve.tensor_copy(s_attT[q % RING][0:n * NWIN, 0:u + 1, 0:H8 * n],
                                bank[2][0:n * NWIN, 0:2 * P].rearrange("p (u r) -> p u r", u=2)
                                [:, 0:u + 1, 0:H8 * n]).then_inc(s("attT_ready"), 1)

            def ctx0(q):
                t, n = 2 * q, sum(n for _, n, _ in tiles_of(q))
                dve.wait_ge(s("attended"), q + 1)
                ts(ctxT[:, 0, t * WT:t * WT + n, :].rearrange("p w h -> p (w h)"), bank[4][:, 0:H8 * n],
                   col("kv_g", 0), col("kv_b", 0), ALU.mult, ALU.add).then_inc(s("ctx_dve"), 1)


            def local_out(w):
                dve.wait_ge(s("proj_done"), w + 1)
                for m in range(KC):
                    sl = slice(w * P, (w + 1) * P)
                    stt(localT[:, m, sl], bank[half_banks[w][1]][:, m * P:(m + 1) * P], col("proj_b", m),
                        redT[:, m, sl], ALU.add, ALU.add).then_inc(s("local_ready"), 1)

            def agg_out(w):
                dve.wait_ge(s("agg_done"), w + 1)
                dve.tensor_copy(aggT[:, :, w * P:(w + 1) * P],
                                bank[half_banks[w][0]][:, 0:C].rearrange("p (k w) -> p k w", k=KC))\
                    .then_inc(s("aggT_ready"), 1)

            def local_stats(w):
                src = bank[half_banks[w][2]][:, 0:C]
                dve.wait_ge(s("lo_major"), w + 1)
                dve.bn_stats(l_st[:, w, :], src).then_inc(s("bn2_done"), 1)
                dve.wait_ge(s("bn2_done"), 2 + w + 1)
                dve.bn_aggr(l_mv[:, w, :], l_st[:, w, :]).then_inc(s("win_mv_ready"), 1)

            def local_norm(w):
                dve.wait_ge(s("win_rs_ready"), 2 + w + 1)
                ts(lox[:, w, :], bank[half_banks[w][2]][:, 0:C], l_mv[:, w, 0:1], l_rs[:, w:w + 1],
                   ALU.subtract, ALU.mult).then_inc(s("lox_ready"), 1)

            def global_shift(w):
                src = bank[half_banks[w][1]][0:H8, 0:P].rearrange("p (i w) -> p i w", w=HW)
                dve.wait_ge(s("gscored"), w + 1)
                dve.tensor_reduce(g_mx[:, w * GI:(w + 1) * GI], src, AX.X, ALU.max).then_inc(s("g_chain"), 1)
                dve.wait_ge(s("g_chain"), 4 * w + 1)
                tt(g3(0, w), src, g_bc(g_mx, w), ALU.subtract).then_inc(s("g_shifted"), 1)

            def global_norm(w):
                dve.wait_ge(s("g_exp"), w + 1)
                sl = slice(w * GI, (w + 1) * GI)
                dve.tensor_reduce(g_sum[:, sl], g3(1, w), AX.X, ALU.add).then_inc(s("g_chain"), 1)
                dve.wait_ge(s("g_chain"), 4 * w + 2)
                dve.reciprocal(g_rec[:, sl], g_sum[:, sl]).then_inc(s("g_chain"), 1)
                dve.wait_ge(s("g_chain"), 4 * w + 3)
                tt(g3(2, w), g3(1, w), g_bc(g_rec, w), ALU.mult).then_inc(s("gattn_ready"), 1)

            def global_mix(w):
                sl = slice(w * P, (w + 1) * P)
                dve.wait_ge(s("gspread"), w + 1)
                dve.wait_ge(s("gvT_ready"), w + 1)
                tt(gprod[:, :, sl], bank[half_banks[w][1]][:, 0:C].rearrange("p (k w) -> p k w", k=KC),
                   gvT[:, :, sl], ALU.mult).then_inc(s("g_chain"), 1)
                dve.wait_ge(s("g_chain"), 4 * w + 4)
                dve.tensor_reduce(gaggT[:, :, w * GI:(w + 1) * GI],
                                  gprod[:, :, sl].rearrange("p k (i w) -> p k i w", w=HW), AX.X, ALU.add)\
                    .then_inc(s("gagg_ready"), 1)

            def class_out(w):
                dve.wait_ge(s("gproj_done"), w + 1)
                for m in range(KC):
                    ts(h0T[:, m, w * GI:(w + 1) * GI, T - 1], bank[half_banks[w][1]][:, m * GI:(m + 1) * GI],
                       col("gproj_b", m), col("class_emb", m), ALU.add, ALU.add).then_inc(s("h0T_dve"), 1)

            g3 = lambda i, w: gattn[:, i, w * P:(w + 1) * P].rearrange("p (i w) -> p i w", w=HW)
            g_bc = lambda v, w: v[:, w * GI:(w + 1) * GI].unsqueeze(2).to_broadcast([H8, GI, HW])
            flat = lw["tern"].rearrange("p k c -> p (k c)")

            for q in range(STEPS + 3):
                if q < STEPS:
                    masked(q)
                if q == 0:
                    queries_apart(1)
                if 1 <= q < STEPS + 1:
                    recip(q - 1)
                if q == 1:
                    keys_out(1, 0)
                    keys_out(1, 1)
                if 2 <= q < STEPS + 2:
                    attT(q - 2)
                if q == HALF_DONE - 2:
                    dve.wait_ge(s("layw_in"), 16)
                    dve.tensor_reduce(w_abs, flat, AX.X, ALU.add, apply_absolute_value=True)\
                        .then_inc(s("w_abs_ready"), 1)
                if q == HALF_DONE + 1:
                    agg_out(0)
                if q == HALF_DONE + 2:
                    local_out(0)
                if q == HALF_DONE + 3:
                    local_stats(0)
                if q >= 3:
                    ctx0(q - 3)
                if q == HALF_DONE + 4:
                    local_norm(0)

            agg_out(1)
            global_shift(0)
            local_out(1)
            global_norm(0)
            dve.wait_ge(s("w_mean_done"), 1)
            ts(w_scale[:, 0:1], bank[0][:, 0:1], EPS, None, ALU.max).then_inc(s("w_chain"), 1)
            local_stats(1)
            global_mix(0)
            local_norm(1)
            class_out(0)
            dve.wait_ge(s("w_chain"), 1)
            ts(w_scale[:, 1:2], w_scale[:, 0:1], 0.5, None, ALU.mult).then_inc(s("w_chain"), 1)
            ts(w_scale[:, 2:3], w_scale[:, 0:1], -0.5, None, ALU.mult).then_inc(s("w_chain"), 1)
            global_shift(1)

            def norm_stats(n, g, src=None):
                src = h if src is None else src
                for u in range(TG):
                    dve.bn_stats(t_st[0:TR, TG * g + u, :], src[0:TR, TG * g + u, :]).then_inc(s("t_bn"), 1)
                for u in range(TG):
                    dve.wait_ge(s("t_bn"), TT * n + TG * g + u + 1)
                    dve.bn_aggr(t_mv[0:TR, TG * g + u, :], t_st[0:TR, TG * g + u, :]).then_inc(s("t_mv_ready"), 1)

            def norm(n, g, src=None, dst=None):
                src, dst = (h if src is None else src), (xn if dst is None else dst)
                dve.wait_ge(s("t_rs_ready"), G * n + g + 1)
                if 1 <= n < 4:
                    dve.wait_ge(s("x_turned"), G * (n - 1) + g + 1)
                if n == 1:
                    dve.wait_ge(s("base_ready"), g + 1)
                for u in range(TG):
                    t = TG * g + u
                    ts(dst[0:TR, t, :], src[0:TR, t, :], t_mv[0:TR, t, 0:1], t_rs[0:TR, t:t + 1],
                       ALU.subtract, ALU.mult).then_inc(s("xn_ready"), 1)

            def add_to_h(g, b, other, ready, n):
                dve.wait_ge(s(ready), n)
                sl = slice(TG * g, TG * (g + 1))
                tt(h[0:TR, sl, :], bank[b][0:TR, 0:TG * C].rearrange("p (u c) -> p u c", u=TG), other[0:TR, sl, :],
                   ALU.add).then_inc(s("h_ready"), 1)

            groups = range(G)
            global_norm(1)
            dve.wait_ge(s("h0_ready"), 1)
            norm_stats(0, 0)
            global_mix(1)
            class_out(1)
            norm(0, 0)
            dve.wait_ge(s("h0_ready"), 2)
            norm_stats(0, 1)
            norm(0, 1)
            for g in groups:
                for m in range(KC):
                    dve.wait_ge(s("val_mm"), KC * (g + 1))
                    ts(val[:, g, m, :], bank[4 * g + 3][:, m * GT:(m + 1) * GT], col("b_in", KC + m), None, ALU.add)\
                        .then_inc(s("val_ready"), 1)
            f = lambda v: v.rearrange("p k n -> p (k n)")
            for g in groups:
                dve.wait_ge(s("gate_tanh"), KC * (g + 1))
                ts(f(keep[:, g]), f(gate_t[:, g]), -0.5, 0.5, ALU.mult, ALU.add).then_inc(s("keep_made"), 1)
                ts(f(gate_v[:, g]), f(gate_t[:, g]), 0.5, 0.5, ALU.mult, ALU.add).then_inc(s("gate_made"), 1)
                dve.wait_ge(s("keep_made"), 2 * g + 1)
                dve.memset(f(keep[:, g]).rearrange("p (i t) -> p i t", t=T)[:, :, 0:1], 0.0)\
                    .then_inc(s("keep_made"), 1)
            for g in groups:
                dve.wait_ge(s("sv_tanh"), KC * (g + 1))
                dve.wait_ge(s("gate_made"), g + 1)
                tt(f(sv[:, g]), f(sv[:, g]), f(gate_v[:, g]), ALU.mult).then_inc(s("drive_made"), 1)
                dve.wait_ge(s("drive_made"), g + 1)
                dve.wait_ge(s("keep_made"), 2 * g + 2)
                dve.tensor_tensor_scan(f(scanT[:, g]), f(keep[:, g]), f(sv[:, g]), 0.0, ALU.mult, ALU.add)\
                    .then_inc(s("scan_ready"), 1)
            tmp, tmp2 = tern_tmp
            ts(tmp, flat, w_scale[:, 2:3], w_scale[:, 0:1], ALU.is_lt, ALU.mult).then_inc(s("w_chain"), 1)
            ts(tmp2, flat, w_scale[:, 1:2], w_scale[:, 0:1], ALU.is_gt, ALU.mult).then_inc(s("w_chain"), 1)
            dve.wait_ge(s("w_chain"), 5)
            tt(flat, tmp2, tmp, ALU.subtract).then_inc(s("tern_ready"), 1)
            for g in groups:
                dve.wait_ge(s("base_ready"), g + 1)
                add_to_h(g, 4 * g + 1, base, "mix_done", g + 1)
                dve.wait_ge(s("h_ready"), g + 1)
                norm_stats(1, g)
            for g in groups:
                norm(1, g)
            for g in groups:
                add_to_h(g, 4 * g + 2, h, "tern_done", g + 1)
                dve.wait_ge(s("h_ready"), G + g + 1)
                norm_stats(2, g)
            for g in groups:
                norm(2, g)
            dve.wait_ge(s("latD_clear"), 1)
            for g in groups:
                dve.wait_ge(s("lat_done"), g + 1)
                for p in range(2):
                    dve.tensor_copy(latD[p * R:(p + 1) * R, g * GI:(g + 1) * GI, p, :],
                                    bank[4 * g + 3][p * R:(p + 1) * R, 0:GT].rearrange("p (i t) -> p i t", t=T))\
                        .then_inc(s("lat_ready"), 1)
            for g in groups:
                for n in range(2):
                    dve.wait_ge(s("lt_done"), NP2 * g + 4 * n + 2)
                    b = 4 * g + (0, 3)[n]
                    dve.tensor_copy(ltT[:, g * GT:(g + 1) * GT, 4 * n:4 * n + 2].rearrange("p n j -> p j n"),
                                    bank[b][:, 0:2 * GT].rearrange("p (j n) -> p j n", j=2)).then_inc(s("lt_dve"), 1)
            a3 = lambda i, g: att[i][:, g * GI:(g + 1) * GI].rearrange("p i a t -> p (i a) t")
            st = lambda i, g: a_stat[:, i, g * GI * 2:(g + 1) * GI * 2]
            bc = lambda v: v.unsqueeze(2).to_broadcast([NP2 * T, GI * 2, T])
            def att_shift(g):
                dve.wait_ge(s("att_scored"), g + 1)
                tt(a3(0, g), bank[4 * g][0:NP2 * T, 0:2 * GT].rearrange("p (n t) -> p n t", t=T),
                   causal.unsqueeze(1).to_broadcast([NP2 * T, GI * 2, T]), ALU.add).then_inc(s("att_chain"), 1)
                dve.wait_ge(s("att_chain"), 2 * g + 1)
                dve.tensor_reduce(st(0, g), a3(0, g), AX.X, ALU.max).then_inc(s("att_chain"), 1)
                dve.wait_ge(s("att_chain"), 2 * g + 2)
                tt(a3(1, g), a3(0, g), bc(st(0, g)), ALU.subtract).then_inc(s("att_shifted"), 1)

            def att_norm(g):
                dve.wait_ge(s("att_exp"), g + 1)
                dve.tensor_reduce(st(1, g), a3(1, g), AX.X, ALU.add).then_inc(s("att_sum"), 1)
                dve.wait_ge(s("att_sum"), 2 * g + 1)
                dve.reciprocal(st(2, g), st(1, g)).then_inc(s("att_sum"), 1)
                dve.wait_ge(s("att_sum"), 2 * g + 2)
                tt(a3(0, g), a3(1, g), bc(st(2, g)), ALU.mult).then_inc(s("att_probs"), 1)

            def weigh(g, t):
                y4 = yT[:, g].rearrange("p k (i t) -> p k i t", t=T)
                v4 = vT[:, g].rearrange("p k (i t) -> p k i t", t=T)
                dve.wait_ge(s("vT_ready"), KC * (g + 1))
                dve.wait_ge(s("spread_done"), T * g + t + 1)
                i = (T - 1) * g + t - 1
                if t and i >= RING:
                    dve.wait_ge(s("y_ready"), i - RING + 1)
                sp_ = bank[4 * g + 1 + t % 3][:, 0:KC * GT].rearrange("p (k n) -> p k n", k=KC)
                sp_ = sp_[:, :, 0:GI * (t + 1)].rearrange("p k (i u) -> p k i u", u=t + 1)
                tt(product(i, t) if t else y4[:, :, :, 0:1], sp_, v4[:, :, :, 0:t + 1], ALU.mult)\
                    .then_inc(s("y_mul"), 1)

            def product(i, t):
                return prod[i % RING][:, 0:KC * GI * (t + 1)].rearrange("p (k i u) -> p k i u", k=KC, u=t + 1)

            def sum_keys(g, t):
                dve.wait_ge(s("y_mul"), T * g + t + 1)
                dve.tensor_reduce(yT[:, g].rearrange("p k (i t) -> p k i t", t=T)[:, :, :, t],
                                  product((T - 1) * g + t - 1, t), AX.X, ALU.add).then_inc(s("y_ready"), 1)

            def mix(g, first, last):
                for t in range(first, last):
                    weigh(g, t)
                    if t - 1 >= max(first, 1):
                        sum_keys(g, t - 1)
                if last > 1:
                    sum_keys(g, last - 1)

            att_shift(0)
            att_norm(0)
            mix(0, 0, 3)
            att_shift(1)
            mix(0, 3, T)
            att_norm(1)

            def add_mixed(g):
                dve.wait_ge(s("base_ready"), G + g + 1)
                add_to_h(g, 4 * g, base, "lat_out_done", g + 1)
                dve.wait_ge(s("h_ready"), 2 * G + g + 1)
                norm_stats(3, g)

            mix(1, 0, 1)
            add_mixed(0)
            mix(1, 1, 3)
            norm(3, 0)
            mix(1, 3, T)
            add_mixed(1)
            norm(3, 1)
            for g in groups:
                dve.wait_ge(s("xn_ready"), 3 * TT + TG * (g + 1))
                norm_stats(4, g, xn)
            dve.wait_ge(s("gate_tanh2"), G)
            ts(val8, work8[0], 1.0, 0.5, ALU.add, ALU.mult).then_inc(s("top"), 1)
            n_top = 1
            src = val8
            for r in range(CAP // 8):
                dve.wait_ge(s("top"), n_top)
                dve.max(m8[:, r, :], src).then_inc(s("top"), 1)
                if r < G:
                    norm(4, r, xn, xh2)
                dve.wait_ge(s("top"), n_top + 1)
                dst = work8[r % 2]
                dve.match_replace(dst, m8[:, r, :], src, -1.0).then_inc(s("top"), 1)
                n_top += 2
                src = dst
            assert src is work8[1]
            dve.wait_ge(s("top"), n_top)
            ts(work8[0], src, 0.0, None, ALU.is_lt).then_inc(s("top"), 1)
            dve.wait_ge(s("top"), n_top + 1)
            dve.tensor_tensor_scan(work8[1], work8[0], work8[0], 0.0, ALU.add, ALU.max).then_inc(s("top"), 1)
            dve.wait_ge(s("top"), n_top + 2)
            tt(sel8, work8[1], work8[0], ALU.mult).then_inc(s("slots_ready"), 1)
            dve.wait_ge(s("slots_turned"), 1)
            sv_ = bank[4][0:TR, 0:TT * 16].rearrange("p (t a e) -> p t a e", t=TT, a=2)
            dve.tensor_copy(slotT[0:TR], sv_[:, :, 0, :]).then_inc(s("slotT_ready"), 1)
            dve.tensor_copy(valT[0:TR], sv_[:, :, 1, :]).then_inc(s("slotT_ready"), 1)
            dve.wait_ge(s("slotT_ready"), 2)
            for t in range(TT):
                tt(pick[0:TR, t, :, :], slotT[0:TR, t, :].unsqueeze(2).to_broadcast([TR, E8, SW]),
                   slots[0:TR].unsqueeze(1).to_broadcast([TR, E8, SW]), ALU.is_equal).then_inc(s("pick_t"), 1)
            dve.wait_ge(s("gathered"), 1)
            dve.wait_ge(s("ysT_clear"), 1)
            ts(ysT[:, 0, :, 0:CAP], bank[6][:, 0:TOK].rearrange("p (e c) -> p e c", e=E8), col("ln_g", 0),
               col("ln_b", 0), ALU.mult, ALU.add).then_inc(s("ysT_ready"), 1)
            def bias(q):
                for c in range(2):
                    dve.wait_ge(s("hid_done"), 2 * q + c + 1)
                    dve.wait_ge(s(f"b1_in{q % 2}"), 32 * (q // 2 + 1))
                    if q >= 2:
                        dve.wait_ge(s("hid_turned"), 2 * (q - 2) + c + 1)
                    tt(hid[q % 2][:, c * 512:(c + 1) * 512], bank[c][:, :], b1_rows[:, q % 2, c * 512:(c + 1) * 512],
                       ALU.add).then_inc(s("hid_biased"), 1)

            def turned(q):
                dve.wait_ge(s("hid_turned"), 2 * q + 1)
                if q >= 2:
                    dve.wait_ge(s("eo_done"), q - 1)
                dve.tensor_copy(hidT[q % 2][:, 0:4, :].rearrange("p f n -> p (f n)"), bank[2][:, :])\
                    .then_inc(s("hidT_dve"), 1)

            def pair(q):
                dve.wait_ge(s("eo_done"), q + 1)
                if q == 0:
                    dve.wait_ge(s("b2_in"), 16 * E8)
                if q >= 2:
                    dve.wait_ge(s("combined"), G * (q - 1))
                tt(opair[q % 2], bank[4][:, 0:C], b2_rows[:, q, :], ALU.add).then_inc(s("opair_ready"), 1)

            dve.wait_ge(s("wpick_t"), TT)
            bias(0)
            for q in range(E8 // 2):
                dve.wait_ge(s("wpick_turned"), q + 1)
                dve.tensor_copy(wpickT[:, q, :], bank[4 + q][:, 0:TOK]).then_inc(s("wpickT_ready"), 1)
            for q in range(E8 // 2):
                if q + 1 < E8 // 2:
                    bias(q + 1)
                turned(q)
                pair(q)
            for g in groups:
                dve.wait_ge(s("base_ready"), 2 * G + g + 1)
                dve.wait_ge(s("combined"), G * (E8 // 2 - 1) + g + 1)
                sl = slice(TG * g, TG * (g + 1))
                tt(base[0:TR, sl, :], bank[5 + g][0:TR, :].rearrange("p (u c) -> p u c", u=TG), base[0:TR, sl, :],
                   ALU.add).then_inc(s("out_ready"), 1)

        @block.scalar
        def _(act):
            ac = act.activation

            def copy_pe(t, j):
                act.wait_ge(s("conv_done"), t + 1)
                if not (isinstance(t, int) and t < RING):
                    act.wait_ge(s("xhat_ready"), t - (RING - 1))
                ac(pe_sb[j][0:TP], conv_bank[j][0:TP, 0:C], ACT.Copy).then_inc(s("pe_copied"), 1)

            def affine(t, j):
                act.wait_ge(s("turned"), t + 1)
                for k in range(KC):
                    i = ac(winT[:, k, bass.ds(t * TP, TP)], tr_bank[j][:, k * P:k * P + TP], ACT.Identity,
                           bias=col("kv_b", k), scale=col("kv_g", k))
                i.then_inc(s("winT_ready"), 1)

            copy_pe(0, 0)
            act.wait_ge(s("cols_in"), 16)
            for t in range(1, HEAD):
                copy_pe(t, t % RING)
                if t >= RING:
                    affine(t - RING, t % RING)
            with act.Fori(HEAD // RING, MID // RING) as r:
                for j in range(RING):
                    copy_pe(RING * r + j, j)
                    affine(RING * r + (j - RING), j)
            for t in range(MID, TILES):
                copy_pe(t, t % RING)
                affine(t - RING, t % RING)
            def keys_out(w, m):
                b = ((2, 6), (6, 4))[w][m]
                act.wait_ge(s("qk_done"), 4 * w + 2 * m + 2)
                ac(qkT[:, 1, w * P:(w + 1) * P, 4 * m:4 * m + 4].rearrange("p w g -> p g w"),
                   bank[b][:, :].rearrange("p (g w) -> p g w", g=4), ACT.Copy).then_inc(s("qk_act"), 1)

            affine(TILES - 3, (TILES - 3) % RING)
            keys_out(0, 0)
            affine(TILES - 2, (TILES - 2) % RING)
            affine(TILES - 1, (TILES - 1) % RING)
            keys_out(0, 1)

            def expo(q):
                j = q % RING
                act.wait_ge(s("nmx_ready"), q + 1)
                if q >= RING:
                    act.wait_ge(s("att_ready"), q - RING + 1)
                for t, n, u in tiles_of(q):
                    rows, wide = H8 * n, n * NWIN
                    ac(s_exp[j][0:rows, u, 0:wide], s_msk[j][0:rows, u, 0:wide], ACT.Exp,
                       bias=s_nmx[j][0:rows, u:u + 1], scale=C ** -0.5, accum_out=s_sum[j][0:rows, u:u + 1])\
                        .then_inc(s("s_exp_ready"), 1)

            def ctx1(q):
                t, n = 2 * q, sum(n for _, n, _ in tiles_of(q))
                act.wait_ge(s("attended"), q + 1)
                ac(ctxT[:, 1, t * WT:t * WT + n, :].rearrange("p w h -> p (w h)"), bank[5][:, 0:H8 * n],
                   ACT.Identity, bias=col("kv_b", 1), scale=col("kv_g", 1)).then_inc(s("ctx_act"), 1)

            def mod_out(w):
                act.wait_ge(s("mod_done"), w + 1)
                for m in range(KC):
                    ac(h0T[:, m, w * GI:(w + 1) * GI, 1:1 + HW],
                       bank[half_banks[w][0]][:, m * P:(m + 1) * P].rearrange("p (i w) -> p i w", w=HW),
                       ACT.Identity, bias=col("mod_b", m)).then_inc(s("h0T_act"), 1)

            def keys_in(w):
                act.wait_ge(s("lox_turned"), w + 1)
                for k in range(KC):
                    ac(lnlT[:, k, w * P:(w + 1) * P], bank[half_banks[w][2]][:, k * P:(k + 1) * P], ACT.Identity,
                       bias=col("gkv_b", k), scale=col("gkv_g", k)).then_inc(s("lnlT_ready"), 1)

            def values_out(w):
                act.wait_ge(s("gv_done"), w + 1)
                ac(gvT[:, :, w * P:(w + 1) * P],
                   bank[half_banks[w][0]][:, 0:C].rearrange("p (k w) -> p k w", k=KC), ACT.Copy)\
                    .then_inc(s("gvT_ready"), 1)

            def global_exp(w):
                act.wait_ge(s("g_shifted"), w + 1)
                ac(gattn[:, 1, w * P:(w + 1) * P], gattn[:, 0, w * P:(w + 1) * P], ACT.Exp, scale=C ** -0.5)\
                    .then_inc(s("g_exp"), 1)

            def tokens_out(g):
                act.wait_ge(s("h0_major"), g + 1)
                ac(h[0:TR, TG * g:TG * (g + 1), :], bank[4 * g][0:TR, :].rearrange("p (u c) -> p u c", u=TG), ACT.Copy)\
                    .then_inc(s("h0_ready"), 1)

            for q in range(STEPS + 3):
                if q < STEPS:
                    expo(q)
                if q == 1:
                    keys_out(1, 0)
                    keys_out(1, 1)
                if q == HALF_DONE + 3:
                    mod_out(0)
                if q >= 3:
                    ctx1(q - 3)

            groups = range(G)
            keys_in(0)
            global_exp(0)
            values_out(0)
            mod_out(1)
            keys_in(1)
            global_exp(1)
            values_out(1)
            tokens_out(0)

            def xT_out(n, g):
                act.wait_ge(s("x_turned"), G * n + g + 1)
                ac(xT[:, g].rearrange("p k n -> p (k n)"), bank[4 * g + 1][:, 0:KC * GT], ACT.Copy)\
                    .then_inc(s("xT_ready"), 1)

            def xT_copy(n):
                for g in groups:
                    xT_out(n, g)

            xT_out(0, 0)
            tokens_out(1)
            xT_out(0, 1)
            act.wait_ge(s("bhalf_ready"), 1)
            for g in groups:
                for m in range(KC):
                    act.wait_ge(s("gate_mm"), KC * (g + 1))
                    ac(gate_t[:, g, m, :], bank[4 * g + 2][:, m * GT:(m + 1) * GT], ACT.Tanh,
                       bias=b_in_half[:, m:m + 1], scale=0.5).then_inc(s("gate_tanh"), 1)
            for g in groups:
                for m in range(KC):
                    act.wait_ge(s("sv_mm"), KC * (g + 1))
                    ac(sv[:, g, m, :], bank[4 * g][:, m * GT:(m + 1) * GT], ACT.Tanh, bias=col("b_s", m))\
                        .then_inc(s("sv_tanh"), 1)
            xT_copy(1)
            xT_copy(2)
            for g in groups:
                act.wait_ge(s("v_done"), KC * (g + 1))
                for m in range(KC):
                    ac(vT[:, g, m, :], bank[4 * g + 2][:, m * GT:(m + 1) * GT], ACT.Identity, bias=col("v_b", m))\
                        .then_inc(s("vT_ready"), 1)
            for g in groups:
                for n in range(2):
                    act.wait_ge(s("lt_done"), NP2 * g + 4 * n + 4)
                    b = 4 * g + (1, 2)[n]
                    ac(ltT[:, g * GT:(g + 1) * GT, 4 * n + 2:4 * n + 4].rearrange("p n j -> p j n"),
                       bank[b][:, 0:2 * GT].rearrange("p (j n) -> p j n", j=2), ACT.Copy).then_inc(s("lt_act"), 1)
            for g in groups:
                act.wait_ge(s("att_shifted"), g + 1)
                a1 = att[1][:, g * GI:(g + 1) * GI].rearrange("p i a t -> p (i a t)")
                ac(a1, a1, ACT.Exp, scale=R ** -0.5).then_inc(s("att_exp"), 1)
            xT_copy(3)
            for g in groups:
                act.wait_ge(s("gate_done"), g + 1)
                ac(work8[0][:, g * GT:(g + 1) * GT], bank[4 * g + 2][0:E8, 0:GT], ACT.Tanh)\
                    .then_inc(s("gate_tanh2"), 1)
            act.wait_ge(s("gathered"), 1)
            act.wait_ge(s("ysT_clear"), 1)
            ac(ysT[:, 1, :, 0:CAP], bank[7][:, 0:TOK].rearrange("p (e c) -> p e c", e=E8), ACT.Identity,
               bias=col("ln_b", 1), scale=col("ln_g", 1)).then_inc(s("ysT_ready"), 1)

            def gelu(q):
                for c in range(2):
                    act.wait_ge(s("hid_biased"), 2 * q + c + 1)
                    hc = hid[q % 2][:, c * 512:(c + 1) * 512]
                    ac(hc, hc, ACT.Gelu_apprx_tanh).then_inc(s("hid_ready"), 1)

            gelu(0)
            for q in range(E8 // 2):
                if q + 1 < E8 // 2:
                    gelu(q + 1)
                act.wait_ge(s("hid_turned"), 2 * q + 2)
                if q >= 2:
                    act.wait_ge(s("eo_done"), q - 1)
                ac(hidT[q % 2][:, 4:8, :].rearrange("p f n -> p (f n)"), bank[3][:, :], ACT.Copy)\
                    .then_inc(s("hidT_act"), 1)

        @block.gpsimd
        def _(pool):
            pool.memset(zeros[:, :], 0.0).then_inc(s("constants_set"), 1)
            pool.memset(half, -0.5).then_inc(s("constants_set"), 1)
            pool.memset(eps, EPS).then_inc(s("constants_set"), 1)
            pool.wait_ge(s("constants_set"), 3)

            def rsqrt(ve, var, rs, name, parts=P):
                n = 1 + rsqrt.n
                rsqrt.n = n
                pool.tensor_scalar(ve, var, EPS, None, ALU.add).then_inc(s("eps_added"), 1)
                pool.wait_ge(s("eps_added"), n)
                pool.tensor_tensor(rs, ve, half[0:parts, 0:rs.shape[1]], ALU.pow).then_inc(s(name), 1)

            rsqrt.n = 0

            def rs_tile(t, j):
                pool.wait_ge(s("mv_ready"), t + 1)
                if not (isinstance(t, int) and t < RING):
                    pool.wait_ge(s("xhat_ready"), t - (RING - 1))
                pool.tensor_tensor(a_ve[j][0:TP], a_mv[j][0:TP, 1:2], eps[0:TP], ALU.add).then_inc(s("a_eps"), 1)
                pool.wait_ge(s("a_eps"), t + 1)
                pool.tensor_tensor(a_rs[j][0:TP], a_ve[j][0:TP], half[0:TP, 0:1], ALU.pow).then_inc(s("rs_ready"), 1)

            def keep_xhat(t, j):
                pool.wait_ge(s("xhat_ready"), t + 1)
                pool.tensor_copy(xhat_all[0:TP, t, :], xhat[j][0:TP]).then_inc(s("xall_done"), 1)

            for t in range(HEAD):
                rs_tile(t, t % RING)
                if t:
                    keep_xhat(t - 1, (t - 1) % RING)
                if t == 3:
                    pool.wait_ge(s("c_norm"), 2)
                    rsqrt(c_ve[0:1], c_mv[0:1, 1:2], c_rs[0:1], "c_rs_ready", parts=1)
            with pool.Fori(HEAD // RING, MID // RING) as r:
                for j in range(RING):
                    rs_tile(RING * r + j, j)
                    keep_xhat(RING * r + (j - 1), (j - 1) % RING)

            def rs_means(w):
                pool.wait_ge(s("win_mv_ready"), w + 1)
                rsqrt(w_ve[:, w:w + 1], w_mv[:, w, 1:2], w_rs[:, w:w + 1], "win_rs_ready")

            for t in range(MID, TILES):
                rs_tile(t, t % RING)
                if t == TILES - 1:
                    rs_means(1)
                keep_xhat(t - 1, (t - 1) % RING)
                if t == MID + 1:
                    rs_means(0)
            keep_xhat(TILES - 1, (TILES - 1) % RING)

            for q in range(STEPS):
                _, n, u = tiles_of(q)[-1]
                rows, wide, j = H8 * n, n * NWIN, q % RING
                pool.wait_ge(s("rec_ready"), q + 1)
                if q >= RING:
                    pool.wait_ge(s("att_turned"), q - RING + 1)
                pool.tensor_tensor(s_att[j][0:rows, 0:u + 1, 0:wide], s_exp[j][0:rows, 0:u + 1, 0:wide],
                                   s_rec[j][0:rows, 0:u + 1].unsqueeze(2).to_broadcast([rows, u + 1, wide]),
                                   ALU.mult).then_inc(s("att_ready"), 1)

            for w in range(2):
                pool.wait_ge(s("win_mv_ready"), 2 + w + 1)
                rsqrt(l_ve[:, w:w + 1], l_mv[:, w, 1:2], l_rs[:, w:w + 1], "win_rs_ready")
                if w == 0:
                    for k in range(KC):
                        pool.tensor_copy(h0T[:, k, :, 0], col("cls_tok", k).to_broadcast([P, IMAGES]))\
                            .then_inc(s("cls_set"), 1)
                    pool.tensor_scalar(b_in_half, col("b_in", 0, KC), 0.5, None, ALU.mult)\
                        .then_inc(s("bhalf_ready"), 1)

            def rs_tokens(n, g):
                sl = slice(TG * g, TG * (g + 1))
                pool.wait_ge(s("t_mv_ready"), TT * n + TG * (g + 1))
                rsqrt(t_ve[0:TR, sl], t_mv[0:TR, sl, 1], t_rs[0:TR, sl], "t_rs_ready", parts=TR)

            bo = w_of(layw, LAYW, "bo_row")[0:TR].unsqueeze(1).to_broadcast([TR, TG, C])
            ob = w_of(layw, LAYW, "ob_row")[0:TR].unsqueeze(1).to_broadcast([TR, TG, C])
            groups = range(G)
            part = lambda v, g: v[0:TR, TG * g:TG * (g + 1), :]
            for g in groups:
                rs_tokens(0, g)
            for g in groups:
                pool.wait_ge(s("xn_ready"), TG * (g + 1))
                pool.wait_ge(s("h0_ready"), g + 1)
                pool.tensor_tensor(part(base, g), part(h, g), part(xn, g), ALU.add).then_inc(s("base_step"), 1)
                pool.wait_ge(s("base_step"), g + 1)
                pool.tensor_tensor(part(base, g), part(base, g), bo, ALU.add).then_inc(s("base_ready"), 1)

            pool.wait_ge(s("layw_in"), 16)
            core = w_of(layw, LAYW, "core", parts=R)
            coreT = w_of(layw, LAYW, "coreT", parts=R)
            nh = 1

            def hstep(i):
                nonlocal nh
                nh += 1
                i.then_inc(s("head_steps"), 1)
                pool.wait_ge(s("head_steps"), nh)

            pool.tensor_tensor(core, core, coreT, ALU.add).then_inc(s("head_steps"), 1)
            hstep(pool.tensor_tensor(tree, heads[:, 0:NH // 2, :], heads[:, NH // 2:NH, :], ALU.add))
            n = NH // 4
            while n:
                hstep(pool.tensor_tensor(tree[:, 0:n, :], tree[:, 0:n, :], tree[:, n:2 * n, :], ALU.add))
                n //= 2
            hstep(pool.tensor_scalar(core, core, 0.5 / NH, None, ALU.mult))
            hstep(pool.tensor_scalar(tree[:, 0, :], tree[:, 0, :], 1.0 / NH, None, ALU.mult))
            hstep(pool.tensor_tensor(heads, heads, tree[:, 0:1, :].to_broadcast([R, NH, R]), ALU.subtract))
            pool.tensor_tensor(heads, heads, core.unsqueeze(1).to_broadcast([R, NH, R]), ALU.add)\
                .then_inc(s("heads_ready"), 1)

            for n in (1, 2):
                for g in groups:
                    rs_tokens(n, g)
                if n == 1:
                    pool.wait_ge(s("h_ready"), G)
                    pool.memset(latD, 0.0).then_inc(s("latD_clear"), 1)
            for g in groups:
                pool.wait_ge(s("h_ready"), G + g + 1)
                pool.tensor_tensor(part(base, g), part(h, g), ob, ALU.add).then_inc(s("base_ready"), 1)
            for n in (3, 4):
                for g in groups:
                    rs_tokens(n, g)
            pool.wait_ge(s("h_ready"), 3 * G)
            pool.memset(ysT, 0.0).then_inc(s("ysT_clear"), 1)
            for g in groups:
                pool.wait_ge(s("h_ready"), 2 * G + g + 1)
                pool.wait_ge(s("xn_ready"), 3 * TT + TG * (g + 1))
                pool.tensor_tensor(part(base, g), part(h, g), part(xn, g), ALU.add).then_inc(s("base_ready"), 1)
            pool.wait_ge(s("slotT_ready"), 2)
            for t in range(TT):
                pool.wait_ge(s("pick_t"), t + 1)
                pool.tensor_tensor(wpick[0:TR, t, :, :], pick[0:TR, t, :, :],
                                   valT[0:TR, t, :].unsqueeze(2).to_broadcast([TR, E8, SW]), ALU.mult)\
                    .then_inc(s("wpick_t"), 1)


def chunked(w):
    w = np.asarray(w)
    return w.reshape(KC, P, -1).transpose(1, 0, 2).reshape(P, -1)


def packed(table, total, parts):
    out = np.zeros((P, total), np.float32)
    for name, a in parts.items():
        at, n = table[name]
        out[:a.shape[0], at:at + n] = a.reshape(a.shape[0], n)
    return out


def constants():
    rows = np.arange(H8 * WT)[:, None] // H8
    mask = np.where(np.arange(TP)[None] // NWIN == rows, 0.0, NEG)
    rows = np.arange(H8 * LASTW)[:, None] // H8
    mask_last = np.where(np.arange(LASTW * NWIN)[None] // NWIN == rows, 0.0, NEG)
    jt = np.arange(NP2 * T)
    causal = np.where(np.arange(T)[None] > (jt // NP2)[:, None], NEG, 0.0)
    chan = np.arange(P)
    spread = (jt[:, None, None] == np.arange(T)[None, :, None] * NP2 + chan[None, None] // HD)
    heads8 = np.arange(H8)[:, None, None] == (np.arange(KC)[:, None] * P + chan[None])[None] // DH
    headcol = (np.arange(KC)[None, :, None] * P + chan[:, None, None]) // DH == np.arange(H8)[None, None]
    f = lambda a: np.asarray(a, np.float32)
    return packed(CONS, CONS_N, {
        "ident": f(np.eye(P)), 
        "mask": f(mask), "mask_last": f(mask_last), "causal": f(causal),
        "slots": f(np.tile(np.arange(1, SW + 1), (P, 1))), "spread": f(spread), "heads8": f(heads8),
        "headcol": f(headcol), "mean": f(np.full((P, P), 1.0 / (C * C)))})


def kernel(**inputs):
    import concourse.bacc as _bacc
    from concourse.bass_utils import run_bass_kernel_spmd as _run

    g = {k: np.asarray(v) for k, v in inputs.items()}
    x = g["x"].reshape(IMAGES, 3, 2, CS, PATCH, 2, CS, PATCH)
    x = x.transpose(1, 4, 7, 0, 2, 5, 3, 6).reshape(PIX, WINDOWS * NWIN)
    full = np.zeros((KX * KP, TILES * TP), np.float32)
    full[:PIX, :WINDOWS * NWIN] = x
    xs = np.ascontiguousarray(full.reshape(KX, KP, TILES, TP).transpose(2, 1, 0, 3))
    cw = np.zeros((KX * KP, C), np.float32)
    cw[:PIX] = g["L0_tok_conv_w"].reshape(C, PIX).T
    cw = np.pad(cw.reshape(KX, KP, C).transpose(1, 0, 2).reshape(KP, KX * C), ((0, P - KP), (0, 0)))

    t = lambda n: g["L0_tok_" + n]
    tokw = packed(TOKW, TOKW_N, {
        "wq": chunked(t("la_wq")), "wkT": chunked(t("la_wkv")[:, :C].T), "wv": chunked(t("la_wkv")[:, C:]),
        "proj": chunked(t("la_proj_w")), "mod": chunked(t("mod_w")), "gwq": chunked(t("ga_wq")),
        "gwkT": chunked(t("ga_wkv")[:, :C].T), "gwv": chunked(t("ga_wkv")[:, C:]),
        "gproj": chunked(t("ga_proj_w"))})
    perm = np.arange(C).reshape(NP2, 2, HD).transpose(1, 0, 2).reshape(-1)
    basis = g["L1_attn_basis_w"].T
    layw = packed(LAYW, LAYW_N, {
        "w_in": chunked(g["L0_attn_W_in"].T), "w_s": chunked(g["L0_attn_W_s"].T),
        "w_o": chunked(g["L0_attn_W_o"].T), "tern": chunked(g["L0_ffn_weight"].T),
        "basis": chunked(np.concatenate([basis, basis], 1)), "v_w": chunked(g["L1_attn_v_w"].T[:, perm]),
        "o_w": chunked(g["L1_attn_o_w"].T[perm]), "gate": chunked(g["L1_ffn_gate_w"].T),
        "heads": g["L1_attn_head_residual"].transpose(1, 0, 2), "core": g["L1_attn_core"],
        "coreT": g["L1_attn_core"].T, "bo_row": np.tile(g["L0_attn_b_o"], (P, 1)),
        "ob_row": np.tile(g["L1_attn_o_b"], (P, 1))})
    cols = packed(COLS, COLS_N, {
        "q_g": chunked(t("la_ln_q_g")), "q_b": chunked(t("la_ln_q_b")), "kv_g": chunked(t("la_ln_kv_g")),
        "kv_b": chunked(t("la_ln_kv_b")), "proj_b": chunked(t("la_proj_b")), "mod_b": chunked(t("mod_b")),
        "gq_g": chunked(t("ga_ln_q_g")), "gq_b": chunked(t("ga_ln_q_b")), "gkv_g": chunked(t("ga_ln_kv_g")),
        "gkv_b": chunked(t("ga_ln_kv_b")), "gproj_b": chunked(t("ga_proj_b")),
        "class_emb": chunked(t("class_emb")), "cls_tok": chunked(g["cls_tok"].reshape(C)),
        "b_s": chunked(g["L0_attn_b_s"]), "v_b": chunked(g["L1_attn_v_b"][perm]),
        "ln_g": chunked(g["L1_ffn_ln_gamma"]), "ln_b": chunked(g["L1_ffn_ln_beta"]),
        "b_in": g["L0_attn_b_in"].reshape(2 * KC, P).T, "class_row": np.tile(t("class_emb"), (P, 1))})
    w1 = g["L1_ffn_fc1s"].reshape(E8, FF, KC, P).transpose(0, 3, 2, 1).reshape(E8, P, KC * FF)
    w2 = g["L1_ffn_fc2s"].reshape(E8, C, FC, P).transpose(0, 3, 2, 1).reshape(E8, P, FC * C)
    experts = np.ascontiguousarray(np.stack([w1, w2], 1).reshape(2 * E8, P, KC * FF))

    nc = _bacc.Bacc("TRN2", target_bir_lowering=False, num_devices=1)
    arrays = {"patches": xs, "conv_w": cw, "columns": cols, "constants": constants(),
              "tokenizer_w": tokw, "layer_w": layw, "experts": experts,
              "bias1": np.ascontiguousarray(g["L1_ffn_b1s"]), "bias2": np.ascontiguousarray(g["L1_ffn_b2s"])}
    args = [nc.dram_tensor(n, a.shape, F32, kind="ExternalInput").ap() for n, a in arrays.items()]
    o = nc.dram_tensor("tokens", (TOK, C), F32, kind="ExternalOutput").ap()
    build(nc, *args, o)
    r = _run(nc, [arrays], core_ids=[0])
    return r.results[0]["tokens"].reshape(IMAGES, T, C)
```
